# Optimizing a Trainium2 kernel written in Bass

```python
import numpy as np
import jax
import jax.numpy as jnp

def _softmax(x, axis=-1):
    return jax.nn.softmax(x, axis=axis)

def _gelu(x):
    return jax.nn.gelu(x, approximate=True)

def _silu(x):
    return jax.nn.silu(x)

def _sigmoid(x):
    return jax.nn.sigmoid(x)

def _layernorm(x, axis=-1, eps=1e-05):
    m = jnp.mean(x, axis=axis, keepdims=True)
    v = jnp.var(x, axis=axis, keepdims=True)
    return (x - m) / jnp.sqrt(v + eps)

def _scatter_add(tgt, idx, src, axis=0):
    return tgt.at[idx].add(src)

def _segment_sum(src, seg, n):
    return jax.ops.segment_sum(src, seg, n)
kernel_name = 'mk_seq_postln_d2_jaxref_r8_0e06a5'

def setup_inputs(seed: int=0):
    np.random.seed(seed)
    _w = jnp.asarray

    def _L0_attn_setup():
        import jax, jax.numpy as jnp
        import numpy as np
        EPS = 1e-06
        N_HEADS = 16

        def _heads(t, B, N, H, Dk):
            return t.reshape(B, N, H, Dk).transpose(0, 2, 1, 3)
        key = jax.random.key(seed)
        ks = jax.random.split(key, 5)
        B, N, D = (64, 64, 128)
        x = jax.random.normal(ks[0], (B, N, D), dtype=jnp.float32)
        s = 0.02
        W_q = jax.random.normal(ks[1], (D, D), dtype=jnp.float32) * s
        W_k = jax.random.normal(ks[2], (D, D), dtype=jnp.float32) * s
        W_v = jax.random.normal(ks[3], (D, D), dtype=jnp.float32) * s
        W_o = jax.random.normal(ks[4], (D, D), dtype=jnp.float32) * s
        z = jnp.zeros((D,), dtype=jnp.float32)
        return {'x': x, 'W_q': W_q, 'b_q': z, 'W_k': W_k, 'b_k': z, 'W_v': W_v, 'b_v': z, 'W_o': W_o, 'b_o': z}
    _L0_attn_in = _L0_attn_setup()

    def _L0_ffn_setup():
        import jax, jax.numpy as jnp
        import numpy as np
        S, B, H = (256, 2, 128)
        NUM_HEADS, NUM_KV_HEADS = (16, 4)
        HEAD_DIM = H // NUM_HEADS
        E, TOP_K, FFN = (16, 2, 256)
        CAP_FACTOR = 1.25
        EPS = 1e-05

        def _layernorm(x, w, b):
            mu = jnp.mean(x, axis=-1, keepdims=True)
            var = jnp.mean((x - mu) ** 2, axis=-1, keepdims=True)
            return (x - mu) * jax.lax.rsqrt(var + EPS) * w + b
        key = jax.random.key(seed)
        ks = jax.random.split(key, 6)
        qkv_out = (NUM_HEADS + 2 * NUM_KV_HEADS) * HEAD_DIM
        sdH = 1.0 / np.sqrt(H)
        sdF = 1.0 / np.sqrt(FFN)
        return {'hidden_states': jax.random.normal(ks[0], (S, B, H), jnp.float32), 'ln1_weight': jnp.ones((H,), jnp.float32), 'ln1_bias': jnp.zeros((H,), jnp.float32), 'ln2_weight': jnp.ones((H,), jnp.float32), 'ln2_bias': jnp.zeros((H,), jnp.float32), 'qkv_weight': jax.random.normal(ks[1], (qkv_out, H), jnp.float32) * sdH, 'proj_weight': jax.random.normal(ks[2], (H, H), jnp.float32) * sdH, 'router_weight': jax.random.normal(ks[3], (E, H), jnp.float32) * sdH, 'moe_w1': jax.random.normal(ks[4], (E, FFN, H), jnp.float32) * sdH, 'moe_w2': jax.random.normal(ks[5], (E, H, FFN), jnp.float32) * sdF}
    _L0_ffn_in = _L0_ffn_setup()

    def _L1_attn_setup():
        import jax, jax.numpy as jnp
        import numpy as np
        D_MODEL = 128
        D_STATE = 16
        D_CONV = 4
        EXPAND = 2
        D_INNER = D_MODEL * EXPAND
        B_SZ, L_SEQ = (4, 128)

        def _selective_scan(x, delta, Bp, Cp, A_log, D_param):
            A = -jnp.exp(A_log)
            deltaA = jnp.exp(delta[..., None] * A)
            deltaB_x = delta[..., None] * Bp[:, :, None, :] * x[..., None]

            def step(h, inp):
                dA, dBx, Ct = inp
                h = dA * h + dBx
                y = jnp.einsum('bn,bdn->bd', Ct, h)
                return (h, y)
            h0 = jnp.zeros((x.shape[0], x.shape[2], A.shape[1]), x.dtype)
            xs = (jnp.swapaxes(deltaA, 0, 1), jnp.swapaxes(deltaB_x, 0, 1), jnp.swapaxes(Cp, 0, 1))
            _, ys = jax.lax.scan(step, h0, xs)
            return jnp.swapaxes(ys, 0, 1) + x * D_param
        key = jax.random.key(seed)
        ks = jax.random.split(key, 8)
        s = lambda fan_in: 1.0 / np.sqrt(fan_in)
        x = jax.random.normal(ks[0], (B_SZ, L_SEQ, D_MODEL), dtype=jnp.float32)
        in_proj_w = jax.random.uniform(ks[1], (2 * D_INNER, D_MODEL), jnp.float32, -s(D_MODEL), s(D_MODEL))
        conv_w = jax.random.uniform(ks[2], (D_INNER, 1, D_CONV), jnp.float32, -s(D_CONV), s(D_CONV))
        conv_b = jax.random.uniform(ks[3], (D_INNER,), jnp.float32, -s(D_CONV), s(D_CONV))
        x_proj_w = jax.random.uniform(ks[4], (2 * D_STATE + D_INNER, D_INNER), jnp.float32, -s(D_INNER), s(D_INNER))
        dt_proj_w = jax.random.uniform(ks[5], (D_INNER, D_INNER), jnp.float32, -s(D_INNER), s(D_INNER))
        dt_proj_b = jax.random.uniform(ks[6], (D_INNER,), jnp.float32, -0.001, 0.001)
        A = jnp.tile(jnp.arange(1, D_STATE + 1, dtype=jnp.float32), (D_INNER, 1))
        A_log = jnp.log(A)
        D_param = jnp.ones((D_INNER,), jnp.float32)
        out_proj_w = jax.random.uniform(ks[7], (D_MODEL, D_INNER), jnp.float32, -s(D_INNER), s(D_INNER))
        return {'x': x, 'in_proj_w': in_proj_w, 'conv_w': conv_w, 'conv_b': conv_b, 'x_proj_w': x_proj_w, 'dt_proj_w': dt_proj_w, 'dt_proj_b': dt_proj_b, 'A_log': A_log, 'D_param': D_param, 'out_proj_w': out_proj_w}
    _L1_attn_in = _L1_attn_setup()

    def _L1_ffn_setup():
        import jax, jax.numpy as jnp
        import numpy as np
        D_IN, D_HID = (128, 512)

        def _ternary(key, shape):
            return jax.random.randint(key, shape, -1, 2).astype(jnp.float32)

        def _tlin(x, w, s):
            return jnp.einsum('bsi,oi->bso', x, w) * s
        key = jax.random.key(seed)
        ks = jax.random.split(key, 12)
        inv = lambda fan: 1.0 / np.sqrt(fan).astype(np.float32)
        return {'x': jax.random.normal(ks[0], (4, 256, D_IN), dtype=jnp.float32), 'w1_w': _ternary(ks[1], (D_HID, D_IN)), 'w1_s': jax.random.uniform(ks[2], (D_HID,), dtype=jnp.float32) * inv(D_IN), 'w2_w': _ternary(ks[3], (D_HID, D_IN)), 'w2_s': jax.random.uniform(ks[4], (D_HID,), dtype=jnp.float32) * inv(D_IN), 'h1_w': _ternary(ks[5], (D_HID, D_HID)), 'h1_s': jax.random.uniform(ks[6], (D_HID,), dtype=jnp.float32) * inv(D_HID), 'h2_w': _ternary(ks[7], (D_HID, D_HID)), 'h2_s': jax.random.uniform(ks[8], (D_HID,), dtype=jnp.float32) * inv(D_HID), 'w3_w': _ternary(ks[9], (D_IN, D_HID)), 'w3_s': jax.random.uniform(ks[10], (D_IN,), dtype=jnp.float32) * inv(D_HID)}
    _L1_ffn_in = _L1_ffn_setup()
    _d = {'L0_attn_x': _L0_attn_in['x'], 'L0_attn_W_q': _L0_attn_in['W_q'], 'L0_attn_b_q': _L0_attn_in['b_q'], 'L0_attn_W_k': _L0_attn_in['W_k'], 'L0_attn_b_k': _L0_attn_in['b_k'], 'L0_attn_W_v': _L0_attn_in['W_v'], 'L0_attn_b_v': _L0_attn_in['b_v'], 'L0_attn_W_o': _L0_attn_in['W_o'], 'L0_attn_b_o': _L0_attn_in['b_o'], 'L0_ffn_ln1_weight': _L0_ffn_in['ln1_weight'], 'L0_ffn_ln1_bias': _L0_ffn_in['ln1_bias'], 'L0_ffn_ln2_weight': _L0_ffn_in['ln2_weight'], 'L0_ffn_ln2_bias': _L0_ffn_in['ln2_bias'], 'L0_ffn_qkv_weight': _L0_ffn_in['qkv_weight'], 'L0_ffn_proj_weight': _L0_ffn_in['proj_weight'], 'L0_ffn_router_weight': _L0_ffn_in['router_weight'], 'L0_ffn_moe_w1': _L0_ffn_in['moe_w1'], 'L0_ffn_moe_w2': _L0_ffn_in['moe_w2'], 'L1_attn_in_proj_w': _L1_attn_in['in_proj_w'], 'L1_attn_conv_w': _L1_attn_in['conv_w'], 'L1_attn_conv_b': _L1_attn_in['conv_b'], 'L1_attn_x_proj_w': _L1_attn_in['x_proj_w'], 'L1_attn_dt_proj_w': _L1_attn_in['dt_proj_w'], 'L1_attn_dt_proj_b': _L1_attn_in['dt_proj_b'], 'L1_attn_A_log': _L1_attn_in['A_log'], 'L1_attn_D_param': _L1_attn_in['D_param'], 'L1_attn_out_proj_w': _L1_attn_in['out_proj_w'], 'L1_ffn_w1_w': _L1_ffn_in['w1_w'], 'L1_ffn_w1_s': _L1_ffn_in['w1_s'], 'L1_ffn_w2_w': _L1_ffn_in['w2_w'], 'L1_ffn_w2_s': _L1_ffn_in['w2_s'], 'L1_ffn_h1_w': _L1_ffn_in['h1_w'], 'L1_ffn_h1_s': _L1_ffn_in['h1_s'], 'L1_ffn_h2_w': _L1_ffn_in['h2_w'], 'L1_ffn_h2_s': _L1_ffn_in['h2_s'], 'L1_ffn_w3_w': _L1_ffn_in['w3_w'], 'L1_ffn_w3_s': _L1_ffn_in['w3_s']}
    _x0 = _d['L0_attn_x']
    _d['L0_attn_x'] = jax.random.normal(jax.random.fold_in(jax.random.key(seed), 1), (8, 1024, 128), dtype=_x0.dtype)
    del _x0
    return _d

def reference(L0_attn_x, L0_attn_W_q, L0_attn_b_q, L0_attn_W_k, L0_attn_b_k, L0_attn_W_v, L0_attn_b_v, L0_attn_W_o, L0_attn_b_o, L0_ffn_ln1_weight, L0_ffn_ln1_bias, L0_ffn_ln2_weight, L0_ffn_ln2_bias, L0_ffn_qkv_weight, L0_ffn_proj_weight, L0_ffn_router_weight, L0_ffn_moe_w1, L0_ffn_moe_w2, L1_attn_in_proj_w, L1_attn_conv_w, L1_attn_conv_b, L1_attn_x_proj_w, L1_attn_dt_proj_w, L1_attn_dt_proj_b, L1_attn_A_log, L1_attn_D_param, L1_attn_out_proj_w, L1_ffn_w1_w, L1_ffn_w1_s, L1_ffn_w2_w, L1_ffn_w2_s, L1_ffn_h1_w, L1_ffn_h1_s, L1_ffn_h2_w, L1_ffn_h2_s, L1_ffn_w3_w, L1_ffn_w3_s):

    def _L0_attn_ref(x, W_q, b_q, W_k, b_k, W_v, b_v, W_o, b_o):
        import jax, jax.numpy as jnp
        import numpy as np
        EPS = 1e-06
        N_HEADS = 16

        def _heads(t, B, N, H, Dk):
            return t.reshape(B, N, H, Dk).transpose(0, 2, 1, 3)
        B, N, Dm = x.shape
        H = N_HEADS
        Dk = Dm // H
        q = _heads(x @ W_q.T + b_q, B, N, H, Dk)
        k = _heads(x @ W_k.T + b_k, B, N, H, Dk)
        v = _heads(x @ W_v.T + b_v, B, N, H, Dk)
        dec = jnp.exp(-jnp.arange(N, dtype=jnp.float32) / N)[None, None, :, None]
        qf = jax.nn.relu(q) * dec
        kf = jax.nn.relu(k) * dec
        KV = jnp.einsum('bhnd,bhne->bhde', kf, v)
        Ksum = kf.sum(axis=2)
        denom = jnp.einsum('bhnd,bhd->bhn', qf, Ksum) + EPS
        out = jnp.einsum('bhnd,bhde->bhne', qf, KV) / denom[..., None]
        out = out.transpose(0, 2, 1, 3).reshape(B, N, Dm)
        return out @ W_o.T + b_o

    def _L0_ffn_ref(hidden_states, ln1_weight, ln1_bias, ln2_weight, ln2_bias, qkv_weight, proj_weight, router_weight, moe_w1, moe_w2):
        import jax, jax.numpy as jnp
        import numpy as np
        S, B, H = (256, 2, 128)
        NUM_HEADS, NUM_KV_HEADS = (16, 4)
        HEAD_DIM = H // NUM_HEADS
        E, TOP_K, FFN = (16, 2, 256)
        CAP_FACTOR = 1.25
        EPS = 1e-05

        def _layernorm(x, w, b):
            mu = jnp.mean(x, axis=-1, keepdims=True)
            var = jnp.mean((x - mu) ** 2, axis=-1, keepdims=True)
            return (x - mu) * jax.lax.rsqrt(var + EPS) * w + b
        S_, B_, H_ = hidden_states.shape
        dtype = hidden_states.dtype
        ln1 = _layernorm(hidden_states, ln1_weight, ln1_bias)
        qkv = jnp.einsum('sbh,oh->sbo', ln1, qkv_weight)
        q_sz = NUM_HEADS * HEAD_DIM
        kv_sz = NUM_KV_HEADS * HEAD_DIM
        q = qkv[..., :q_sz].reshape(S_, B_, NUM_HEADS, HEAD_DIM)
        k = qkv[..., q_sz:q_sz + kv_sz].reshape(S_, B_, NUM_KV_HEADS, HEAD_DIM)
        v = qkv[..., q_sz + kv_sz:].reshape(S_, B_, NUM_KV_HEADS, HEAD_DIM)
        rep = NUM_HEADS // NUM_KV_HEADS
        k = jnp.repeat(k, rep, axis=2)
        v = jnp.repeat(v, rep, axis=2)
        scale = 1.0 / np.sqrt(HEAD_DIM)
        scores = jnp.einsum('qbhd,kbhd->bhqk', q, k) * scale
        causal = jnp.tril(jnp.ones((S_, S_), bool))
        scores = jnp.where(causal, scores, jnp.asarray(-1e+30, dtype))
        attn = jax.nn.softmax(scores, axis=-1)
        attn_out = jnp.einsum('bhqk,kbhd->qbhd', attn, v).reshape(S_, B_, H_)
        proj_out = jnp.einsum('sbh,oh->sbo', attn_out, proj_weight)
        hidden_after_attn = hidden_states + proj_out
        ln2 = _layernorm(hidden_after_attn, ln2_weight, ln2_bias).reshape(-1, H_)
        T = ln2.shape[0]
        logits = ln2 @ router_weight.T
        probs = jax.nn.softmax(logits, axis=-1)
        top_p, top_i = jax.lax.top_k(probs, TOP_K)
        cap = int(np.ceil(T * TOP_K / E * CAP_FACTOR))
        exp_idx = top_i.reshape(-1)
        gate = top_p.reshape(-1).astype(dtype)
        tok = jnp.repeat(jnp.arange(T), TOP_K)
        onehot = jax.nn.one_hot(exp_idx, E, dtype=jnp.int32)
        pos = (jnp.cumsum(onehot, axis=0) * onehot).sum(-1) - 1
        keep = pos < cap
        pos_c = jnp.where(keep, pos, cap)
        buf = jnp.zeros((E, cap + 1, H_), dtype)
        buf = buf.at[exp_idx, pos_c].add(ln2[tok] * keep[:, None].astype(dtype))
        h1 = jax.nn.gelu(jnp.einsum('ech,efh->ecf', buf, moe_w1))
        h2 = jnp.einsum('ecf,ehf->ech', h1, moe_w2)
        out_ent = h2[exp_idx, pos_c] * (gate * keep.astype(dtype))[:, None]
        moe_out = jnp.zeros((T, H_), dtype).at[tok].add(out_ent)
        return hidden_after_attn + moe_out.reshape(S_, B_, H_)

    def _L1_attn_ref(x, in_proj_w, conv_w, conv_b, x_proj_w, dt_proj_w, dt_proj_b, A_log, D_param, out_proj_w):
        import jax, jax.numpy as jnp
        import numpy as np
        D_MODEL = 128
        D_STATE = 16
        D_CONV = 4
        EXPAND = 2
        D_INNER = D_MODEL * EXPAND
        B_SZ, L_SEQ = (4, 128)

        def _selective_scan(x, delta, Bp, Cp, A_log, D_param):
            A = -jnp.exp(A_log)
            deltaA = jnp.exp(delta[..., None] * A)
            deltaB_x = delta[..., None] * Bp[:, :, None, :] * x[..., None]

            def step(h, inp):
                dA, dBx, Ct = inp
                h = dA * h + dBx
                y = jnp.einsum('bn,bdn->bd', Ct, h)
                return (h, y)
            h0 = jnp.zeros((x.shape[0], x.shape[2], A.shape[1]), x.dtype)
            xs = (jnp.swapaxes(deltaA, 0, 1), jnp.swapaxes(deltaB_x, 0, 1), jnp.swapaxes(Cp, 0, 1))
            _, ys = jax.lax.scan(step, h0, xs)
            return jnp.swapaxes(ys, 0, 1) + x * D_param
        B, L, _ = x.shape
        xz = x @ in_proj_w.T
        xi, z = jnp.split(xz, 2, axis=-1)
        xc = jnp.swapaxes(xi, 1, 2)
        xc = jax.lax.conv_general_dilated(xc, conv_w, window_strides=(1,), padding=[(D_CONV - 1, 0)], feature_group_count=D_INNER, dimension_numbers=('NCH', 'OIH', 'NCH'))
        xc = xc + conv_b[None, :, None]
        xi = jax.nn.silu(jnp.swapaxes(xc, 1, 2))
        deltaBC = xi @ x_proj_w.T
        delta, Bp, Cp = jnp.split(deltaBC, [D_INNER, D_INNER + D_STATE], axis=-1)
        delta = jax.nn.softplus(delta @ dt_proj_w.T + dt_proj_b)
        y = _selective_scan(xi, delta, Bp, Cp, A_log, D_param)
        return y * jax.nn.silu(z) @ out_proj_w.T

    def _L1_ffn_ref(x, w1_w, w1_s, w2_w, w2_s, h1_w, h1_s, h2_w, h2_s, w3_w, w3_s):
        import jax, jax.numpy as jnp
        import numpy as np
        D_IN, D_HID = (128, 512)

        def _ternary(key, shape):
            return jax.random.randint(key, shape, -1, 2).astype(jnp.float32)

        def _tlin(x, w, s):
            return jnp.einsum('bsi,oi->bso', x, w) * s
        h = jax.nn.silu(_tlin(x, w1_w, w1_s)) * _tlin(x, w2_w, w2_s)
        h = jax.nn.gelu(_tlin(h, h1_w, h1_s), approximate=False)
        h = jax.nn.gelu(_tlin(h, h2_w, h2_s), approximate=False)
        return _tlin(h, w3_w, w3_s)
    x = L0_attn_x
    x = _layernorm(x + _L0_attn_ref(x, L0_attn_W_q, L0_attn_b_q, L0_attn_W_k, L0_attn_b_k, L0_attn_W_v, L0_attn_b_v, L0_attn_W_o, L0_attn_b_o), axis=-1)
    x = _layernorm(x + _L0_ffn_ref(x, L0_ffn_ln1_weight, L0_ffn_ln1_bias, L0_ffn_ln2_weight, L0_ffn_ln2_bias, L0_ffn_qkv_weight, L0_ffn_proj_weight, L0_ffn_router_weight, L0_ffn_moe_w1, L0_ffn_moe_w2), axis=-1)
    x = _layernorm(x + _L1_attn_ref(x, L1_attn_in_proj_w, L1_attn_conv_w, L1_attn_conv_b, L1_attn_x_proj_w, L1_attn_dt_proj_w, L1_attn_dt_proj_b, L1_attn_A_log, L1_attn_D_param, L1_attn_out_proj_w), axis=-1)
    x = _layernorm(x + _L1_ffn_ref(x, L1_ffn_w1_w, L1_ffn_w1_s, L1_ffn_w2_w, L1_ffn_w2_s, L1_ffn_h1_w, L1_ffn_h1_s, L1_ffn_h2_w, L1_ffn_h2_s, L1_ffn_w3_w, L1_ffn_w3_s), axis=-1)
    return x

_drawn_inputs = setup_inputs


def setup_inputs(seed=0):
    import zlib

    import numpy as np

    out = dict(_drawn_inputs(seed))
    spreads = {'L0_attn_b_q': (0.0, 0.8),
     'L0_attn_b_k': (0.0, 2.0),
     'L0_attn_b_v': (0.0, 0.1),
     'L0_attn_b_o': (0.0, 0.1),
     'L0_ffn_ln1_weight': (1.0, 0.2),
     'L0_ffn_ln1_bias': (0.0, 0.1),
     'L0_ffn_ln2_weight': (1.0, 0.2),
     'L0_ffn_ln2_bias': (0.0, 0.345),
     'L1_attn_D_param': (1.0, 0.6)}
    factors = {'L0_attn_W_q': 8.0,
     'L0_attn_W_k': 8.0,
     'L0_attn_W_v': 8.0,
     'L1_attn_x_proj_w': 8.0,
     'L1_attn_dt_proj_w': 8.0,
     'L1_attn_dt_proj_b': 64.0,
     'L1_attn_A_log': 8.0,
     'L1_ffn_w1_w': 8.0,
     'L1_ffn_w1_s': 8.0,
     'L1_ffn_w2_w': 8.0,
     'L1_ffn_w2_s': 8.0,
     'L1_ffn_h1_w': 8.0,
     'L1_ffn_h1_s': 8.0,
     'L1_ffn_h2_w': 8.0,
     'L1_ffn_h2_s': 8.0,
     'L1_ffn_w3_w': 8.0,
     'L1_ffn_w3_s': 8.0}
    for name, (base, spread) in spreads.items():
        noise = np.random.default_rng([zlib.crc32(name.encode()), seed]).standard_normal(out[name].shape)
        drawn = base * np.exp(spread * noise) if base else spread * noise
        out[name] = jnp.asarray(drawn.astype(out[name].dtype))
    for name, factor in factors.items():
        out[name] = (out[name] * factor).astype(out[name].dtype)
    return out
```

```python
from contextlib import ExitStack

import numpy as np

import concourse.bass as bass
from concourse import mybir

P = 128
SEQ, POS, D = 8, 1024, 128
TOK = SEQ * POS
TILES = TOK // P
GT = 8
GN = GT * P
BANK = 512
HEADS, HD = 16, 8
EXP, FFN, TOPK = 16, 256, 2
CAP = int(np.ceil(TOK * TOPK / EXP * 1.25))
SLOTS = EXP * CAP
CT = CAP // P
DI, NS, TAPS = 256, 16, 4
HID = 512
LN_EPS, ATT_EPS = 1e-5, 1e-6

F32 = mybir.dt.float32
BF16 = mybir.dt.bfloat16
U32 = mybir.dt.uint32
ALU = mybir.AluOpType
ACT = mybir.ActivationFunctionType
AX = mybir.AxisListType.X


def columns(widths):
    at, out = 0, {}
    for name, w in widths:
        out[name] = slice(at, at + w)
        at += w
    return out, at


CONST, CONST_W = columns([("ident", P), ("block", P), ("head", HEADS), ("before", P), ("iota", EXP),
                          ("decay", GT), ("part", 32)])
WA, WA_W = columns([("q", P), ("k", P), ("v", P), ("o", P), ("gq", P), ("gk", P), ("gv", P), ("proj", P),
                    ("router", EXP), ("bq", 1), ("ln1w", 1), ("ln1b", 1), ("ln2w", 1), ("ln2b", 1),
                    ("bk", P), ("bv", P), ("bo", P)])
WM, WM_W = columns([("in", 2 * DI), ("xp", 2 * (DI + 96)), ("dt", 2 * DI), ("out", 2 * D), ("cw", 2 * TAPS),
                    ("cb", 2), ("dtb", 2), ("alog", 2 * NS), ("dpar", 2)])
WF, WF_W = columns([("w1", HID), ("w2", HID), ("h1", 4 * HID), ("h2", 4 * HID), ("w3", 4 * D),
                    ("s1", 4), ("s2", 4), ("t1", 4), ("t2", 4), ("s3", D)])


def program(nc, x_in, const_in, wa_in, moe_in, wm_in, wf_in, out):
    x_tiles = x_in.rearrange("(i p) d -> p i d", p=P)
    out_tiles = out.rearrange("(i p) d -> p i d", p=P)
    slot_rows = nc.dram_tensor("slot_rows", (SLOTS, D), F32, kind="Internal").ap()
    slot_outs = nc.dram_tensor("slot_outs", (SLOTS, D), F32, kind="Internal").ap()

    with ExitStack() as ctx:
        def sb(name, shape, dt=F32, stack=ctx):
            return stack.enter_context(nc.sbuf_tensor(name, shape, dt))

        def sem(name):
            return ctx.enter_context(nc.semaphore(name))

        X = sb("X", [P, TILES, D])
        const = sb("const", [P, CONST_W])
        minus_half = sb("minus_half", [P, GT])
        ident = const[:, CONST["ident"]]
        PS = [ctx.enter_context(nc.psum_tensor(f"ps{u}", [P, 4 * BANK], F32)) for u in range(2)]

        def tiles_of(t, n=GT, w=D):
            return t.rearrange("p (t d) -> p t d", d=w) if n else t

        ln_sems = {n: sem("ln_" + n) for n in ("stats", "moments", "eps", "power")}

        def layernorm(v, y, st, mv, rs, dst, n=GT):
            for t in range(n):
                nc.vector.bn_stats(st[:, t, :], y(t)).then_inc(ln_sems["stats"], 1)
            v.wait_ge(ln_sems["stats"], n).then_inc(ln_sems["stats"], -n)
            for t in range(n):
                last = nc.vector.bn_aggr(mv[:, t, :], st[:, t, :])
            last.then_inc(ln_sems["moments"], 1)
            v.wait_ge(ln_sems["power"], 1).then_inc(ln_sems["power"], -1)
            for t in range(n):
                last = nc.vector.tensor_scalar(dst(t), y(t), mv[:, t, 0:1], rs[:, t:t + 1],
                                               ALU.subtract, ALU.mult)
            return last

        def inverse_root(g, mv, ve, rs, n=GT):
            g.wait_ge(ln_sems["moments"], 1).then_inc(ln_sems["moments"], -1)
            nc.gpsimd.tensor_scalar(ve[:], mv[:, :, 1], LN_EPS, None, ALU.add).then_inc(ln_sems["eps"], 1)
            g.wait_ge(ln_sems["eps"], 1).then_inc(ln_sems["eps"], -1)
            nc.gpsimd.tensor_tensor(rs[:], ve[:], minus_half[:, 0:n], ALU.pow).then_inc(ln_sems["power"], 1)

        wa_stack = ctx.enter_context(ExitStack())
        wa = sb("wa", [P, WA_W], stack=wa_stack)
        w = {n: wa[:, c] for n, c in WA.items()}
        zeros = sb("zeros", [P, 1024], stack=wa_stack)

        with ExitStack() as ph:
            def pb(name, shape, dt=F32):
                return [sb(f"a_{name}{u}", shape, dt, ph) for u in range(2)]

            x_ld, xT, kf, vv = pb("x", [P, GT, D]), pb("xT", [P, GN]), pb("kf", [P, GT, D]), pb("vv", [P, GT, D + 2])
            kv, qf, den, att = pb("kv", [P, D + HEADS]), pb("qf", [P, GN]), pb("den", [P, GT, HEADS]), pb("att", [P, GT, D])
            attT, xb, y = pb("attT", [P, GN]), pb("xb", [P, GT, D]), pb("y", [P, GT, D])
            st, mv, ve, rs = pb("st", [P, GT, 6]), pb("mv", [P, GT, 2]), pb("ve", [P, GT]), pb("rs", [P, GT])
            (s_const, s_wa, s_zero, s_x, s_xfree, s_xp, s_T, s_xT, s_k, s_v, s_kf, s_kvp, s_kv, s_qp, s_qf, s_num,
             s_att, s_aT, s_aTs, s_o, s_xb, s_dve, s_ready, s_psfree, s_xbfree, s_half, s_x1) = [
                sem("a_" + n) for n in "const wa zero x xfree xp T xT k v kf kvp kv qp qf num att aT aTs o xb dve ready psfree xbfree half x1".split()]
            decay = const[:, CONST["decay"]]

            def bc_tiles(row, n=GT, width=D):
                return row[:, None, :].to_broadcast([P, n, width])

            A = [PS[u][:, 0:GN] for u in range(2)]
            B = [PS[u][:, GN:2 * GN] for u in range(2)]

            with nc.Block() as block:
                @block.sync
                def _(sp):
                    sp.dma_start(const[:], const_in).then_inc(s_const, 16)
                    sp.dma_start(wa[:], wa_in).then_inc(s_wa, 16)
                    with sp.Fori(0, SEQ // 2) as pair:
                        for u in range(2):
                            sp.wait_ge(s_xfree, 1).then_inc(s_xfree, -1)
                            sp.dma_start(x_ld[u][:], x_tiles[:, bass.ds(pair * (2 * GT) + u * GT, GT), :]).then_inc((s_x, s_x1)[u], 16)
                    sp.wait_ge(s_zero, 1)
                    for r in range(0, SLOTS, 1024):
                        sp.dma_start(slot_rows[r:r + 1024, :].rearrange("(p a) d -> p (a d)", p=P),
                                     zeros[:, 0:1024]).then_inc(s_half, 16)
                    sp.wait_ge(s_half, 16 * (SLOTS // 1024))

                @block.gpsimd
                def _(g):
                    nc.gpsimd.memset(minus_half[:], -0.5)
                    nc.gpsimd.memset(zeros[:], 0.0).then_inc(s_zero, 1)
                    g.sem_inc(s_xfree, 2)
                    g.wait_ge(s_wa, 16)
                    with g.Fori(0, SEQ // 2) as pair:
                        for u in range(2):
                            g.wait_ge(s_xp, 1).then_inc(s_xp, -1)
                            g.wait_ge(s_xbfree, 1).then_inc(s_xbfree, -1)
                            nc.gpsimd.tensor_tensor(xb[u][:], x_ld[u][:], bc_tiles(w["bo"]), ALU.add).then_inc(s_xb, 1)
                            g.wait_ge(s_xb, 1).then_inc(s_xb, -1)
                            g.sem_inc(s_ready, 1)
                            g.sem_inc(s_xfree, 1)
                        for u in range(2):
                            inverse_root(g, mv[u], ve[u], rs[u])

                @block.scalar
                def _(s):
                    s.wait_ge(s_wa, 16)
                    with s.Fori(0, SEQ // 2) as pair:
                        for u in range(2):
                            s.wait_ge(s_T, 1).then_inc(s_T, -1)
                            s.sem_inc(s_xp, 1)
                            nc.scalar.copy(xT[u][:], A[u]).then_inc(s_xT, 1)
                        for u in range(2):
                            s.wait_ge(s_qp, 1).then_inc(s_qp, -1)
                            nc.scalar.activation(qf[u][:], A[u], ACT.Relu, bias=w["bq"]).then_inc(s_qf, 1)
                        for u in range(2):
                            s.wait_ge(s_aT, 1).then_inc(s_aT, -1)
                            nc.scalar.copy(attT[u][:], A[u]).then_inc(s_aTs, 1)

                @block.vector
                def _(v):
                    def own(ins):
                        ins.then_inc(s_dve, 1)
                        v.wait_ge(s_dve, 1).then_inc(s_dve, -1)

                    for u in range(2):
                        own(nc.vector.memset(vv[u][:], 1.0))
                    v.sem_inc(s_xbfree, 2)
                    v.sem_inc(s_psfree, 2)
                    v.wait_ge(s_const, 16)
                    v.wait_ge(s_wa, 16)
                    with v.Fori(0, SEQ // 2) as pair:
                        for u in range(2):
                            v.wait_ge(s_k, 1).then_inc(s_k, -1)
                            own(nc.vector.tensor_tensor(kf[u][:], tiles_of(B[u]), bc_tiles(w["bk"]), ALU.add))
                            nc.vector.scalar_tensor_tensor(
                                out=kf[u][:], in0=kf[u][:], scalar=0.0,
                                in1=decay[:, :, None].to_broadcast([P, GT, D]), op0=ALU.max, op1=ALU.mult).then_inc(s_kf, 1)
                            v.wait_ge(s_v, 1).then_inc(s_v, -1)
                            nc.vector.tensor_tensor(vv[u][:, :, 0:D], tiles_of(A[u]), bc_tiles(w["bv"]), ALU.add).then_inc(s_kf, 1)
                        for u in range(2):
                            v.wait_ge(s_kvp, 1).then_inc(s_kvp, -1)
                            nc.vector.tensor_tensor(kv[u][:, 0:D], B[u][:, 0:D], const[:, CONST["block"]], ALU.mult)
                            nc.vector.tensor_scalar(kv[u][:, D:], const[:, CONST["head"]], B[u][:, D:D + 1],
                                                    None, ALU.mult).then_inc(s_kv, 1)
                        for u in range(2):
                            v.wait_ge(s_num, 1).then_inc(s_num, -1)
                            own(nc.vector.tensor_tensor(den[u][:], B[u][:, 0:GT * HEADS].rearrange("p (t h) -> p t h", h=HEADS),
                                                        decay[:, :, None].to_broadcast([P, GT, HEADS]), ALU.mult))
                            own(nc.vector.tensor_scalar(den[u][:], den[u][:], ATT_EPS, None, ALU.add))
                            own(nc.vector.reciprocal(den[u][:], den[u][:]))
                            own(nc.vector.tensor_tensor(den[u][:], den[u][:],
                                                        decay[:, :, None].to_broadcast([P, GT, HEADS]), ALU.mult))
                            nc.vector.tensor_tensor(
                                att[u][:].rearrange("p t (h e) -> p (t h) e", e=HD),
                                A[u].rearrange("p (q e) -> p q e", e=HD),
                                den[u][:].rearrange("p t h -> p (t h)")[:, :, None].to_broadcast([P, GT * HEADS, HD]),
                                ALU.mult).then_inc(s_att, 1)
                        for u in range(2):
                            v.wait_ge(s_o, 1).then_inc(s_o, -1)
                            v.wait_ge(s_ready, 1).then_inc(s_ready, -1)
                            own(nc.vector.tensor_tensor(y[u][:], tiles_of(B[u]), xb[u][:], ALU.add))
                            v.sem_inc(s_psfree, 1)
                            v.sem_inc(s_xbfree, 1)
                            last = layernorm(v, lambda t: y[u][:, t, :], st[u], mv[u], rs[u],
                                             lambda t: X[:, bass.ds(pair * (2 * GT) + (u * GT + t), 1), :].rearrange("p o d -> p (o d)"))
                            own(last)

                @block.tensor
                def _(pe):
                    pe.wait_ge(s_const, 16)
                    pe.wait_ge(s_wa, 16)
                    with pe.Fori(0, SEQ // 2) as pair:
                        for u in range(2):
                            pe.wait_ge((s_x, s_x1)[u], 16).then_inc((s_x, s_x1)[u], -16)
                            pe.wait_ge(s_psfree, 1).then_inc(s_psfree, -1)
                            for t in range(GT):
                                mm = nc.tensor.transpose(A[u][:, t * P:(t + 1) * P], x_ld[u][:, t, :], ident)
                            mm.then_inc(s_T, 1)
                        for u in range(2):
                            pe.wait_ge(s_xT, 1).then_inc(s_xT, -1)
                            for t in range(GT):
                                mm = nc.tensor.matmul(B[u][:, t * P:(t + 1) * P], xT[u][:, t * P:(t + 1) * P], w["k"],
                                                      start=True, stop=True)
                            mm.then_inc(s_k, 1)
                            for t in range(GT):
                                mm = nc.tensor.matmul(A[u][:, t * P:(t + 1) * P], xT[u][:, t * P:(t + 1) * P], w["v"],
                                                      start=True, stop=True)
                            mm.then_inc(s_v, 1)
                        for u in range(2):
                            pe.wait_ge(s_kf, 2).then_inc(s_kf, -2)
                            for c in range(2):
                                mm = nc.tensor.matmul(A[u][:, c * BANK:(c + 1) * BANK], w["q"],
                                                      xT[u][:, c * BANK:(c + 1) * BANK], start=True, stop=True)
                            mm.then_inc(s_qp, 1)
                            for t in range(GT):
                                mm = nc.tensor.matmul(B[u][:, 0:D + 1], kf[u][:, t, :], vv[u][:, t, 0:D + 1],
                                                      start=t == 0, stop=t == GT - 1)
                            mm.then_inc(s_kvp, 1)
                        for u in range(2):
                            pe.wait_ge(s_qf, 1).then_inc(s_qf, -1)
                            pe.wait_ge(s_kv, 1).then_inc(s_kv, -1)
                            for t in range(GT):
                                nc.tensor.matmul(A[u][:, t * P:(t + 1) * P], qf[u][:, t * P:(t + 1) * P], kv[u][:, 0:D],
                                                 start=True, stop=True)
                                mm = nc.tensor.matmul(B[u][:, t * HEADS:(t + 1) * HEADS], qf[u][:, t * P:(t + 1) * P],
                                                      kv[u][:, D:], start=True, stop=True)
                            mm.then_inc(s_num, 1)
                        for u in range(2):
                            pe.wait_ge(s_att, 1).then_inc(s_att, -1)
                            for t in range(GT):
                                mm = nc.tensor.transpose(A[u][:, t * P:(t + 1) * P], att[u][:, t, :], ident)
                            mm.then_inc(s_aT, 1)
                        for u in range(2):
                            pe.wait_ge(s_aTs, 1).then_inc(s_aTs, -1)
                            for t in range(GT):
                                mm = nc.tensor.matmul(B[u][:, t * P:(t + 1) * P], attT[u][:, t * P:(t + 1) * P], w["o"],
                                                      start=True, stop=True)
                            mm.then_inc(s_o, 1)

        moe_stack = ctx.enter_context(ExitStack())
        Z2 = sb("Z2", [P, TILES, D], stack=moe_stack)
        prob = sb("prob", [P, TILES, EXP], stack=moe_stack)
        Xg = X[:].rearrange("p (s j) d -> p s j d", j=GT)
        Zg = Z2[:].rearrange("p (s j) d -> p s j d", j=GT)
        prob_g = prob[:].rearrange("p (s j) e -> p s j e", j=GT)
        pair_at = [sum(GT - k for k in range(s)) for s in range(GT + 1)]
        with ExitStack() as ph:
            def pb(name, shape, dt=F32):
                return [sb(f"b_{name}{u}", shape, dt, ph) for u in range(2)]

            z, zT, Q, K, V = pb("z", [P, GT, D]), pb("zT", [P, GN]), pb("Q", [P, GT, D]), pb("K", [P, GT, D]), pb("V", [P, GT, D])
            prod = pb("prod", [P, pair_at[GT], D])
            score, attn = pb("score", [P, GT, GT, HEADS]), pb("attn", [P, GT, GT, HEADS])
            smax, ssum = pb("smax", [P, GT, HEADS]), pb("ssum", [P, GT, HEADS])
            att, H = pb("att", [P, GT, D]), pb("H", [P, GT, D])
            lg, lmax, lsum = pb("lg", [P, GT, EXP]), pb("lmax", [P, GT]), pb("lsum", [P, GT])
            st, mv, ve, rs = pb("st", [P, GT, 6]), pb("mv", [P, GT, 2]), pb("ve", [P, GT]), pb("rs", [P, GT])
            (b_z, b_zT, b_zTs, b_q, b_k, b_v, b_qe, b_ke, b_ve, b_pr, b_sub, b_exp, b_av, b_at, b_aT, b_aTs, b_o,
             b_h, b_z2, b_zT2, b_zTs2, b_lg, b_ls, b_le, b_dve, b_pool, b_zfree, b_bfree, b_xa) = [
                sem("b_" + n) for n in "z zT zTs q k v qe ke ve pr sub exp av at aT aTs o h z2 zT2 zTs2 lg ls le dve pool zfree bfree xa".split()]
            A = [PS[u][:, 0:GN] for u in range(2)]
            B = [PS[u][:, GN:2 * GN] for u in range(2)]
            both = range(2)
            scale = float(HD) ** -0.5
            rows = lambda t, s: t[:, pair_at[s]:pair_at[s + 1], :]
            over_keys = lambda t: t[:].rearrange("p k q h -> p (q h) k")

            with nc.Block() as block:
                @block.gpsimd
                def _(g):
                    with g.Fori(0, GT // 2) as pair:
                        for u in both:
                            inverse_root(g, mv[u], ve[u], rs[u])
                        for u in both:
                            g.wait_ge(b_ke, 1).then_inc(b_ke, -1)
                            for s in range(GT):
                                nc.gpsimd.tensor_tensor(rows(prod[u], s), Q[u][:, s:, :],
                                                        K[u][:, s:s + 1, :].to_broadcast([P, GT - s, D]),
                                                        ALU.mult).then_inc(b_pr, 1)
                        for u in both:
                            g.wait_ge(b_exp, 1).then_inc(b_exp, -1)
                            for s in range(GT):
                                nc.gpsimd.tensor_tensor(
                                    rows(prod[u], s).rearrange("p q (h e) -> p q h e", e=HD),
                                    attn[u][:, s, s:, :, None].to_broadcast([P, GT - s, HEADS, HD]),
                                    V[u][:, s:s + 1, :].rearrange("p o (h e) -> p o h e", e=HD).to_broadcast([P, GT - s, HEADS, HD]),
                                    ALU.mult).then_inc(b_av, 1)
                        for u in both:
                            inverse_root(g, mv[u], ve[u], rs[u])
                        for u in both:
                            g.wait_ge(b_h, 1).then_inc(b_h, -1)
                            own = nc.gpsimd.tensor_tensor(Xg[:, :, bass.ds(pair * 2 + u, 1), :].rearrange("p s o d -> p s (o d)"),
                                                          Xg[:, :, bass.ds(pair * 2 + u, 1), :].rearrange("p s o d -> p s (o d)"),
                                                          H[u][:], ALU.add)
                            g.wait_ge(b_z2, 1).then_inc(b_z2, -1)
                            nc.gpsimd.tensor_copy(Zg[:, :, bass.ds(pair * 2 + u, 1), :].rearrange("p s o d -> p s (o d)"),
                                                  z[u][:]).then_inc(b_pool, 1)
                            g.wait_ge(b_pool, 1).then_inc(b_pool, -1)
                            g.sem_inc(b_zfree, 1)

                @block.scalar
                def _(s):
                    def evac(ready, dst, src, done):
                        s.wait_ge(ready, 1).then_inc(ready, -1)
                        nc.scalar.copy(dst, src).then_inc(done, 1)

                    with s.Fori(0, GT // 2) as pair:
                        for u in both:
                            s.wait_ge(b_zT, 1).then_inc(b_zT, -1)
                            nc.scalar.activation(zT[u][:], A[u], ACT.Identity, bias=w["ln1b"], scale=w["ln1w"]).then_inc(b_zTs, 1)
                        for u in both:
                            evac(b_q, Q[u][:], tiles_of(B[u]), b_qe)
                            s.wait_ge(b_k, 1).then_inc(b_k, -1)
                            nc.scalar.copy(K[u][:], tiles_of(A[u])).then_inc(b_xa, 1)
                            s.wait_ge(b_xa, 1).then_inc(b_xa, -1)
                            s.sem_inc(b_ke, 1)
                            evac(b_v, V[u][:], tiles_of(B[u]), b_ve)
                        for u in both:
                            s.wait_ge(b_sub, 1).then_inc(b_sub, -1)
                            nc.scalar.activation(attn[u][:], score[u][:], ACT.Exp, scale=scale).then_inc(b_exp, 1)
                        for u in both:
                            evac(b_aT, zT[u][:], A[u], b_aTs)
                        for u in both:
                            s.wait_ge(b_zT2, 1).then_inc(b_zT2, -1)
                            nc.scalar.activation(zT[u][:], A[u], ACT.Identity, bias=w["ln2b"], scale=w["ln2w"]).then_inc(b_zTs2, 1)
                        for u in both:
                            s.wait_ge(b_ls, 1).then_inc(b_ls, -1)
                            nc.scalar.activation(lg[u][:], lg[u][:], ACT.Exp).then_inc(b_le, 1)

                @block.vector
                def _(v):
                    def own(ins):
                        ins.then_inc(b_dve, 1)
                        v.wait_ge(b_dve, 1).then_inc(b_dve, -1)

                    v.sem_inc(b_zfree, 2)
                    v.sem_inc(b_bfree, 2)
                    with v.Fori(0, GT // 2) as pair:
                        xrow = lambda t, u: Xg[:, t, bass.ds(pair * 2 + u, 1), :].rearrange("p o d -> p (o d)")
                        for u in both:
                            v.wait_ge(b_zfree, 1).then_inc(b_zfree, -1)
                            layernorm(v, lambda t: xrow(t, u), st[u], mv[u], rs[u], lambda t: z[u][:, t, :]).then_inc(b_z, 1)
                        for u in both:
                            own(nc.vector.memset(score[u][:], -1e30))
                            for s in range(GT):
                                v.wait_ge(b_pr, 1).then_inc(b_pr, -1)
                                last = nc.vector.tensor_reduce(score[u][:, s, s:, :],
                                                               rows(prod[u], s).rearrange("p q (h e) -> p (q h) e", e=HD), AX, ALU.add)
                            own(last)
                            own(nc.vector.tensor_reduce(smax[u][:], over_keys(score[u]), AX, ALU.max))
                            nc.vector.tensor_tensor(score[u][:], score[u][:], smax[u][:, None, :, :].to_broadcast([P, GT, GT, HEADS]),
                                                    ALU.subtract).then_inc(b_sub, 1)
                        for u in both:
                            v.wait_ge(b_av, 1).then_inc(b_av, -1)
                            own(nc.vector.tensor_reduce(ssum[u][:], over_keys(attn[u]), AX, ALU.add))
                            own(nc.vector.reciprocal(ssum[u][:], ssum[u][:]))
                            for s in range(1, GT):
                                v.wait_ge(b_av, 1).then_inc(b_av, -1)
                                own(nc.vector.tensor_tensor(prod[u][:, s:GT, :], prod[u][:, s:GT, :], rows(prod[u], s), ALU.add))
                            nc.vector.tensor_tensor(
                                att[u][:].rearrange("p q (h e) -> p (q h) e", e=HD),
                                prod[u][:, 0:GT, :].rearrange("p q (h e) -> p (q h) e", e=HD),
                                ssum[u][:].rearrange("p q h -> p (q h)")[:, :, None].to_broadcast([P, GT * HEADS, HD]),
                                ALU.mult).then_inc(b_at, 1)
                        for u in both:
                            v.wait_ge(b_o, 1).then_inc(b_o, -1)
                            own(nc.vector.tensor_tensor(H[u][:], tiles_of(B[u]),
                                                        Xg[:, :, bass.ds(pair * 2 + u, 1), :].rearrange("p s o d -> p s (o d)"), ALU.add))
                            v.sem_inc(b_h, 1)
                            own(layernorm(v, lambda t: H[u][:, t, :], st[u], mv[u], rs[u], lambda t: z[u][:, t, :]))
                            v.sem_inc(b_z2, 1)
                            v.sem_inc(b_z, 1)
                        for u in both:
                            v.wait_ge(b_lg, 1).then_inc(b_lg, -1)
                            L = B[u][:, 0:GT * EXP].rearrange("p (t e) -> p t e", e=EXP)
                            own(nc.vector.tensor_reduce(lmax[u][:], L, AX, ALU.max))
                            own(nc.vector.tensor_tensor(lg[u][:], L, lmax[u][:, :, None].to_broadcast([P, GT, EXP]), ALU.subtract))
                            v.sem_inc(b_ls, 1)
                            v.sem_inc(b_bfree, 1)
                        for u in both:
                            v.wait_ge(b_le, 1).then_inc(b_le, -1)
                            own(nc.vector.tensor_reduce(lsum[u][:], lg[u][:], AX, ALU.add))
                            own(nc.vector.reciprocal(lsum[u][:], lsum[u][:]))
                            nc.vector.tensor_tensor(prob_g[:, :, bass.ds(pair * 2 + u, 1), :].rearrange("p s o e -> p s (o e)"),
                                                    lg[u][:], lsum[u][:, :, None].to_broadcast([P, GT, EXP]), ALU.mult)

                @block.tensor
                def _(pe):
                    def turn(dst, src, done):
                        for t in range(GT):
                            mm = nc.tensor.transpose(dst[:, t * P:(t + 1) * P], src[:, t, :], ident)
                        mm.then_inc(done, 1)

                    def project(dst, lhsT, rhs, n, done):
                        for t in range(GT):
                            mm = nc.tensor.matmul(dst[:, t * n:(t + 1) * n], lhsT[:, t * P:(t + 1) * P], rhs, start=True, stop=True)
                        mm.then_inc(done, 1)

                    with pe.Fori(0, GT // 2) as pair:
                        for u in both:
                            pe.wait_ge(b_z, 1).then_inc(b_z, -1)
                            turn(A[u], z[u], b_zT)
                        for u in both:
                            pe.wait_ge(b_zTs, 1).then_inc(b_zTs, -1)
                            pe.wait_ge(b_bfree, 1).then_inc(b_bfree, -1)
                            project(B[u], zT[u], w["gq"], P, b_q)
                            project(A[u], zT[u], w["gk"], P, b_k)
                            pe.wait_ge(b_qe, 1).then_inc(b_qe, -1)
                            project(B[u], zT[u], w["gv"], P, b_v)
                        for u in both:
                            pe.wait_ge(b_at, 1).then_inc(b_at, -1)
                            turn(A[u], att[u], b_aT)
                        for u in both:
                            pe.wait_ge(b_aTs, 1).then_inc(b_aTs, -1)
                            pe.wait_ge(b_ve, 1).then_inc(b_ve, -1)
                            project(B[u], zT[u], w["proj"], P, b_o)
                        for u in both:
                            pe.wait_ge(b_z, 1).then_inc(b_z, -1)
                            turn(A[u], z[u], b_zT2)
                        for u in both:
                            pe.wait_ge(b_zTs2, 1).then_inc(b_zTs2, -1)
                            project(B[u], zT[u], w["router"], EXP, b_lg)

        route_stack = ctx.enter_context(ExitStack())
        gates = sb("gates", [P, TILES, 2], stack=route_stack)
        to_row = sb("to_row", [P, TILES, 2], U32, route_stack)
        from_row = sb("from_row", [P, TILES, 2], U32, route_stack)
        PAST = float(1 << 20)
        with ExitStack() as ph:
            t3 = lambda name: sb("r_" + name, [P, TILES, EXP], F32, ph)
            eq, left, hot, marked, place, tmp = [t3(n) for n in ("eq", "left", "hot0", "marked", "place", "tmp")]
            hot2 = t3("hot1")
            carry = sb("r_carry", [P, EXP, TILES], F32, ph)
            totals = sb("r_totals", [P, EXP, TILES], F32, ph)
            run_on = sb("r_run_on", [P, EXP, TILES], F32, ph)
            ones = sb("r_ones", [P, P], F32, ph)
            pk, ik, fk, keep, rowf, wk = [sb("r_" + n, [P, 2, TILES], F32, ph) for n in ("pk", "ik", "fk", "keep", "rowf", "wk")]
            r_dve, r_marked, r_sums = sem("r_dve"), sem("r_marked"), sem("r_sums")
            iota = const[:, CONST["iota"]][:, None, :].to_broadcast([P, TILES, EXP])
            per_tile = lambda a: a[:, :, None].to_broadcast([P, TILES, EXP])
            flat = lambda a: a[:].rearrange("p a b -> p (a b)")

            with nc.Block() as block:
                @block.vector
                def _(v):
                    def own(ins):
                        ins.then_inc(r_dve, 1)
                        v.wait_ge(r_dve, 1).then_inc(r_dve, -1)

                    own(nc.vector.memset(ones[:], 1.0))
                    own(nc.vector.memset(totals[:], 0.0))
                    own(nc.vector.memset(run_on[:], 1.0))
                    own(nc.vector.memset(run_on[:, :, 0:1], 0.0))
                    for k, (p_in, oh) in enumerate(((prob, hot), (left, hot2))):
                        own(nc.vector.tensor_reduce(pk[:, k, :], p_in[:], AX, ALU.max))
                        own(nc.vector.tensor_tensor(eq[:], p_in[:], per_tile(pk[:, k, :]), ALU.is_equal))
                        own(nc.vector.scalar_tensor_tensor(out=tmp[:], in0=eq[:], scalar=-float(EXP), in1=iota, op0=ALU.mult, op1=ALU.add))
                        own(nc.vector.tensor_reduce(ik[:, k, :], tmp[:], AX, ALU.min))
                        own(nc.vector.tensor_scalar(ik[:, k, :], ik[:, k, :], float(EXP), None, ALU.add))
                        own(nc.vector.tensor_tensor(oh[:], iota, per_tile(ik[:, k, :]), ALU.is_equal))
                        if k == 0:
                            own(nc.vector.scalar_tensor_tensor(out=left[:], in0=hot[:], scalar=-4.0, in1=prob[:], op0=ALU.mult, op1=ALU.add))
                    own(nc.vector.tensor_tensor(marked[:], hot[:], hot2[:], ALU.add))
                    v.sem_inc(r_marked, 1)
                    v.wait_ge(r_sums, 1).then_inc(r_sums, -1)
                    own(nc.vector.tensor_copy(totals[:, :, 1:], PS[1][:, 0:1024].rearrange("p (t e) -> p e t", e=EXP)[:, :, 0:TILES - 1]))
                    own(nc.vector.tensor_tensor_scan(flat(carry), flat(run_on), flat(totals), 0.0, ALU.mult, ALU.add))
                    own(nc.vector.tensor_tensor(place[:], PS[0][:, 0:1024].rearrange("p (t e) -> p t e", e=EXP),
                                                carry[:].rearrange("p e t -> p t e"), ALU.add))
                    for k, oh in enumerate((hot, hot2)):
                        own(nc.vector.tensor_tensor(tmp[:], oh[:], place[:], ALU.mult))
                        own(nc.vector.tensor_reduce(fk[:, k, :], tmp[:], AX, ALU.add))
                    own(nc.vector.tensor_scalar(keep[:], fk[:], float(CAP), None, ALU.is_lt))
                    own(nc.vector.scalar_tensor_tensor(out=rowf[:], in0=ik[:], scalar=float(CAP), in1=fk[:], op0=ALU.mult, op1=ALU.add))
                    own(nc.vector.tensor_tensor(rowf[:], rowf[:], keep[:], ALU.mult))
                    own(nc.vector.tensor_copy(from_row[:].rearrange("p t k -> p k t"), rowf[:]))
                    own(nc.vector.tensor_tensor(gates[:].rearrange("p t k -> p k t"), pk[:], keep[:], ALU.mult))
                    own(nc.vector.tensor_scalar(wk[:], keep[:], -PAST, PAST, ALU.mult, ALU.add))
                    own(nc.vector.tensor_tensor(rowf[:], rowf[:], wk[:], ALU.add))
                    own(nc.vector.tensor_copy(to_row[:].rearrange("p t k -> p k t"), rowf[:]))

                @block.tensor
                def _(pe):
                    pe.wait_ge(r_marked, 1).then_inc(r_marked, -1)
                    for c in range(2):
                        half = flat(marked)[:, c * BANK:(c + 1) * BANK]
                        nc.tensor.matmul(PS[0][:, c * BANK:(c + 1) * BANK], const[:, CONST["before"]], half, start=True, stop=True)
                        mm = nc.tensor.matmul(PS[1][:, c * BANK:(c + 1) * BANK], ones[:], half, start=True, stop=True)
                    mm.then_inc(r_sums, 1)

        with ExitStack() as ph:
            def pb(name, shape, dt=F32):
                return [sb(f"d_{name}{u}", shape, dt, ph) for u in range(2)]
            row_at, rows_out = pb("row_at", [P, GT, 2], U32), pb("rows_out", [P, GT, D])
            d_ready, d_free, d_sent = sem("d_ready"), sem("d_free"), [sem("d_sent0"), sem("d_sent1")]
            with nc.Block() as block:
                @block.vector
                def _(v):
                    v.sem_inc(d_free, 2)
                    with v.Fori(0, SEQ // 2) as pair:
                        for u in range(2):
                            v.wait_ge(d_free, 1).then_inc(d_free, -1)
                            nc.vector.tensor_copy(row_at[u][:], to_row[:, bass.ds(pair * (2 * GT) + u * GT, GT), :]).then_inc(d_ready, 1)
                            nc.vector.tensor_copy(rows_out[u][:], Z2[:, bass.ds(pair * (2 * GT) + u * GT, GT), :]).then_inc(d_ready, 1)
                    v.wait_ge(d_free, 2).then_inc(d_free, -2)

                @block.gpsimd
                def _(g):
                    with g.Fori(0, SEQ // 2) as pair:
                        for u in range(2):
                            g.wait_ge(d_ready, 2).then_inc(d_ready, -2)
                            for t in range(GT):
                                for k in range(2):
                                    nc.gpsimd.indirect_dma_start(
                                        slot_rows, bass.IndirectOffsetOnAxis(ap=row_at[u][:, t, k:k + 1], axis=0),
                                        rows_out[u][:, t, :], None, bounds_check=SLOTS - 1, oob_is_err=False).then_inc(d_sent[u], 16)
                        for u in range(2):
                            g.wait_ge(d_sent[u], pair * (16 * 2 * GT) + 16 * 2 * GT)
                            g.sem_inc(d_free, 1)
        expert_w = {n: wa[:, WA[n]] for n in ("ln2w", "ln2b")}

        with ExitStack() as ph:
            def pb(name, shape, dt=F32):
                return [sb(f"e_{name}{u}", shape, dt, ph) for u in range(2)]
            we, xe, xeT = pb("we", [P, 4 * P]), pb("xe", [P, CT, D]), pb("xeT", [P, CAP])
            he, ye = pb("he", [P, 2, CAP]), pb("ye", [P, CT, D])
            e_w, e_x, e_y = [[sem(f"e_{n}{u}") for u in range(2)] for n in "wxy"]
            e_T, e_Ts, e_up, e_act, e_down, e_out, e_st, e_wfree, e_xfree, e_pf = [
                sem("e_" + n) for n in "T Ts up act down out st wfree xfree pf".split()]
            chunks = [(c, min(c + BANK, CAP)) for c in range(0, CAP, BANK)]
            S = [PS[u][:, 0:CAP] for u in range(2)]
            with nc.Block() as block:
                @block.sync
                def _(sp):
                    for u in range(2):
                        sp.sem_inc(e_y[u], 16)
                    with sp.Fori(0, EXP // 2) as pair:
                        for u in range(2):
                            sp.wait_ge(e_wfree, 1).then_inc(e_wfree, -1)
                            sp.dma_start(we[u][:], moe_in[bass.ds(pair * 2 + u, 1), :, :].rearrange("o p c -> p (o c)")).then_inc(e_w[u], 16)
                            sp.dma_start(xe[u][:].rearrange("p t d -> p (t d)"),
                                         slot_rows.rearrange("(e p t) d -> e p (t d)", p=P, t=CT)[bass.ds(pair * 2 + u, 1), :, :]
                                         .rearrange("o p c -> p (o c)")).then_inc(e_x[u], 16)
                        for u in range(2):
                            sp.wait_ge(e_st, 1).then_inc(e_st, -1)
                            sp.dma_start(slot_outs.rearrange("(e p t) d -> e p (t d)", p=P, t=CT)[bass.ds(pair * 2 + u, 1), :, :]
                                         .rearrange("o p c -> p (o c)"), ye[u][:].rearrange("p t d -> p (t d)")).then_inc(e_y[u], 16)
                    for u in range(2):
                        sp.wait_ge(e_y[u], 16)

                @block.scalar
                def _(s):
                    with s.Fori(0, EXP // 2) as pair:
                        for u in range(2):
                            s.wait_ge(e_T, 1).then_inc(e_T, -1)
                            nc.scalar.activation(xeT[u][:], S[u], ACT.Identity, bias=expert_w["ln2b"], scale=expert_w["ln2w"]).then_inc(e_Ts, 1)
                        for f in range(2):
                            for u in range(2):
                                s.wait_ge(e_up, 1).then_inc(e_up, -1)
                                nc.scalar.activation(he[u][:, f, :], S[u], ACT.Gelu_apprx_tanh).then_inc(e_act, 1)

                @block.vector
                def _(v):
                    v.sem_inc(e_wfree, 2)
                    v.sem_inc(e_pf, 2)
                    with v.Fori(0, EXP // 2) as pair:
                        for u in range(2):
                            v.wait_ge(e_down, 1).then_inc(e_down, -1)
                            v.wait_ge(e_y[u], 16).then_inc(e_y[u], -16)
                            nc.vector.tensor_copy(ye[u][:].rearrange("p t d -> p (t d)"), S[u]).then_inc(e_out, 1)
                            v.wait_ge(e_out, 1).then_inc(e_out, -1)
                            v.sem_inc(e_st, 1)
                            v.sem_inc(e_wfree, 1)
                            v.sem_inc(e_pf, 1)

                @block.tensor
                def _(pe):
                    with pe.Fori(0, EXP // 2) as pair:
                        for u in range(2):
                            pe.wait_ge(e_x[u], 16).then_inc(e_x[u], -16)
                            pe.wait_ge(e_pf, 1).then_inc(e_pf, -1)
                            for t in range(CT):
                                mm = nc.tensor.transpose(S[u][:, t * P:(t + 1) * P], xe[u][:, t, :], ident)
                            mm.then_inc(e_T, 1)
                        for f in range(2):
                            for u in range(2):
                                if f == 0:
                                    pe.wait_ge(e_w[u], 16).then_inc(e_w[u], -16)
                                    pe.wait_ge(e_Ts, 1).then_inc(e_Ts, -1)
                                else:
                                    pe.wait_ge(e_act, 1).then_inc(e_act, -1)
                                for a, b in chunks:
                                    mm = nc.tensor.matmul(S[u][:, a:b], we[u][:, f * P:(f + 1) * P], xeT[u][:, a:b], start=True, stop=True)
                                mm.then_inc(e_up, 1)
                        for u in range(2):
                            pe.wait_ge(e_act, 1).then_inc(e_act, -1)
                            for t in range(CT):
                                for f in range(2):
                                    mm = nc.tensor.matmul(S[u][:, t * P:(t + 1) * P], he[u][:, f, t * P:(t + 1) * P],
                                                          we[u][:, (2 + f) * P:(3 + f) * P], start=f == 0, stop=f == 1)
                            mm.then_inc(e_down, 1)

        with ExitStack() as ph:
            def pb(name, shape, dt=F32):
                return [sb(f"c_{name}{u}", shape, dt, ph) for u in range(2)]
            row_at, gt, got = pb("row_at", [P, GT, 2], U32), pb("gt", [P, GT, 2]), pb("got", [P, GT, 2, D])
            y = pb("y", [P, GT, D])
            st, mv, ve, rs = pb("st", [P, GT, 6]), pb("mv", [P, GT, 2]), pb("ve", [P, GT]), pb("rs", [P, GT])
            c_at, c_got, c_dve = sem("c_at"), [sem("c_got0"), sem("c_got1")], sem("c_dve")
            with nc.Block() as block:
                @block.vector
                def _(v):
                    def own(ins):
                        ins.then_inc(c_dve, 1)
                        v.wait_ge(c_dve, 1).then_inc(c_dve, -1)

                    def ask(group, u):
                        nc.vector.tensor_copy(gt[u][:], gates[:, bass.ds(group * GT, GT), :])
                        nc.vector.tensor_copy(row_at[u][:], from_row[:, bass.ds(group * GT, GT), :]).then_inc(c_at, 1)

                    with v.Fori(0, SEQ // 2) as pair:
                        for u in range(2):
                            ask(pair * 2 + u, u)
                        for u in range(2):
                            v.wait_ge(c_got[u], pair * (16 * 2 * GT) + 16 * 2 * GT)
                            for t in range(GT):
                                last = nc.vector.scalar_tensor_tensor(
                                    out=y[u][:, t, :], in0=got[u][:, t, 0, :], scalar=gt[u][:, t, 0:1],
                                    in1=X[:, bass.ds((pair * 2 + u) * GT + t, 1), :].rearrange("p o d -> p (o d)"), op0=ALU.mult, op1=ALU.add)
                            own(last)
                            for t in range(GT):
                                last = nc.vector.scalar_tensor_tensor(
                                    out=y[u][:, t, :], in0=got[u][:, t, 1, :], scalar=gt[u][:, t, 1:2],
                                    in1=y[u][:, t, :], op0=ALU.mult, op1=ALU.add)
                            own(last)
                            own(layernorm(v, lambda t: y[u][:, t, :], st[u], mv[u], rs[u],
                                          lambda t: X[:, bass.ds((pair * 2 + u) * GT + t, 1), :].rearrange("p o d -> p (o d)")))

                @block.gpsimd
                def _(g):
                    with g.Fori(0, SEQ // 2) as pair:
                        for u in range(2):
                            g.wait_ge(c_at, 1).then_inc(c_at, -1)
                            for t in range(GT):
                                for k in range(2):
                                    nc.gpsimd.indirect_dma_start(
                                        got[u][:, t, k, :], None, slot_outs,
                                        bass.IndirectOffsetOnAxis(ap=row_at[u][:, t, k:k + 1], axis=0)).then_inc(c_got[u], 16)
                        for u in range(2):
                            inverse_root(g, mv[u], ve[u], rs[u])

        route_stack.close()
        moe_stack.close()
        wa_stack.close()
        with ExitStack() as ph:
            def pb(name, shape, dt=F32):
                return sb("m_" + name, shape, dt, ph)
            wm, sel = pb("wm", [P, WM_W]), pb("sel", [96, 32 * P], BF16)
            m = {n: wm[:, c] for n, c in WM.items()}
            w_xp = m["xp"].rearrange("p (k o) -> p k o", k=2)
            w_dt = m["dt"].rearrange("p (k o) -> p k o", k=2)
            w_out = m["out"].rearrange("p (k o) -> p k o", k=2)
            taps = m["cw"].rearrange("p (k o) -> p k o", k=2)
            decay_rate, skip = pb("decay_rate", [P, 2 * NS]), pb("skip", [P, 2, P])
            x_st, xT = pb("x_st", [P, GT, D]), pb("xT", [P, GN])
            xi = pb("xi", [P, 2, GN + TAPS])
            gate, cv, uu = pb("gate", [P, 2, GN]), pb("cv", [P, 2, GN]), pb("uu", [P, 2, GN])
            low, ex, delta, dx = pb("low", [P, 2, GN]), pb("ex", [P, 2, GN]), pb("delta", [P, 2, GN]), pb("dx", [P, 2, GN])
            bc, bc_left = pb("bc", [96, GN], BF16), pb("bc_left", [96, GN])
            dA = [pb(f"dA{q}", [P, 2, GN]) for q in range(2)]
            Cs = [pb(f"Cs{q}", [P, GN]) for q in range(2)]
            dBx = [pb(f"dBx{q}", [P, 2, GN]) for q in range(2)]
            h, ch = pb("h", [P, 2, GN]), pb("ch", [P, 2, GN])
            st, mv, ve, rs = pb("st", [P, GT, 6]), pb("mv", [P, GT, 2]), pb("ve", [P, GT]), pb("rs", [P, GT])
            (m_w, m_sel, m_rate, m_exp, m_skip, m_xst, m_T, m_xT, m_xi, m_z, m_xip, m_zs, m_cv, m_u, m_dr, m_bc, m_drs, m_dt, m_e, m_act,
             m_dve, m_delta, m_rows, m_B, m_C, m_bfree, m_cfree, m_dA, m_dAfree, m_Cs, m_csfree, m_h, m_hfree, m_ch,
             m_chfree, m_pool, m_y, m_gy, m_o, m_next, m_rest) = [sem("m_" + n) for n in (
                "w sel rate exp skip xst T xT xi z xip zs cv u dr bc drs dt e act dve delta rows B C bfree cfree dA dAfree Cs csfree h "
                "hfree ch chfree pool y gy o next rest").split()]
            Bp, Cp, Y = PS[0][:, 0:GN], PS[0][:, GN:2 * GN], PS[1]
            two = lambda t: t.rearrange("p (h t) -> p h t", h=2)

            with nc.Block() as block:
                @block.sync
                def _(sp):
                    sp.dma_start(wm[:], wm_in).then_inc(m_w, 16)

                @block.scalar
                def _(s):
                    def own(ins):
                        ins.then_inc(m_act, 1)
                        s.wait_ge(m_act, 1).then_inc(m_act, -1)

                    s.wait_ge(m_w, 16)
                    own(nc.scalar.activation(decay_rate[:], m["alog"], ACT.Exp))
                    own(nc.scalar.mul(decay_rate[:], decay_rate[:], -1.0))
                    with s.Fori(0, SEQ) as b:
                        s.wait_ge(m_next, 1).then_inc(m_next, -1)
                        nc.scalar.copy(x_st[:], X[:, bass.ds(b * GT, GT), :]).then_inc(m_xst, 1)
                        s.wait_ge(m_T, 1).then_inc(m_T, -1)
                        nc.scalar.copy(xT[:], Bp).then_inc(m_xT, 1)
                        s.wait_ge(m_xi, 1).then_inc(m_xi, -1)
                        nc.scalar.copy(xi[:, :, TAPS - 1:TAPS - 1 + GN], two(Y[:])).then_inc(m_xip, 1)
                        s.wait_ge(m_z, 1).then_inc(m_z, -1)
                        nc.scalar.activation(gate[:], two(PS[0][:]), ACT.Silu).then_inc(m_zs, 1)
                        s.wait_ge(m_cv, 1).then_inc(m_cv, -1)
                        for k in range(2):
                            last = nc.scalar.activation(uu[:, k, :], cv[:, k, :], ACT.Silu, bias=m["cb"][:, k:k + 1])
                        last.then_inc(m_u, 1)
                        s.wait_ge(m_dr, 1).then_inc(m_dr, -1)
                        nc.scalar.copy(low[:], two(Y[:])).then_inc(m_drs, 1)
                        s.wait_ge(m_dt, 1).then_inc(m_dt, -1)
                        for k in range(2):
                            last = nc.scalar.activation(low[:, k, :], two(Y[:])[:, k, :], ACT.Abs, bias=m["dtb"][:, k:k + 1])
                        own(last)
                        own(nc.scalar.activation(ex[:], low[:], ACT.Exp, scale=-1.0))
                        own(nc.scalar.activation(low[:], ex[:], ACT.Ln, bias=1.0))
                        s.sem_inc(m_e, 1)
                        s.wait_ge(m_delta, 1).then_inc(m_delta, -1)
                        with s.Fori(0, NS // 2) as pair:
                            for q in range(2):
                                for k in range(2):
                                    s.wait_ge(m_dAfree, 1).then_inc(m_dAfree, -1)
                                    nc.scalar.activation(dA[q][:, k, :], delta[:, k, :], ACT.Exp,
                                                         scale=decay_rate[:, bass.ds(pair * 2 + (k * NS + q), 1)]).then_inc(m_dA, 1)
                                s.wait_ge(m_C, 1).then_inc(m_C, -1)
                                s.wait_ge(m_csfree, 1).then_inc(m_csfree, -1)
                                own(nc.scalar.copy(Cs[q][:], Cp))
                                s.sem_inc(m_cfree, 1)
                                s.sem_inc(m_Cs, 1)

                @block.vector
                def _(v):
                    def own(ins):
                        ins.then_inc(m_dve, 1)
                        v.wait_ge(m_dve, 1).then_inc(m_dve, -1)

                    v.wait_ge(m_w, 16)
                    for k in range(2):
                        own(nc.vector.tensor_scalar(skip[:, k, :], ident, m["dpar"][:, k:k + 1], None, ALU.mult))
                    own(nc.vector.tensor_copy(sel[:].rearrange("p (r c) -> p r c", c=P),
                                              const[0:96, CONST["part"]][:, :, None].to_broadcast([96, 32, P])))
                    v.sem_inc(m_sel, 1)
                    own(nc.vector.memset(xi[:], 0.0))
                    v.sem_inc(m_next, 1)
                    with v.Fori(0, SEQ) as b:
                        v.wait_ge(m_xip, 1).then_inc(m_xip, -1)
                        for k in range(2):
                            own(nc.vector.tensor_scalar(cv[:, k, :], xi[:, k, 0:GN], taps[:, k, 0:1], None, ALU.mult))
                            for j in range(1, TAPS):
                                own(nc.vector.scalar_tensor_tensor(out=cv[:, k, :], in0=xi[:, k, j:j + GN], scalar=taps[:, k, j:j + 1],
                                                                   in1=cv[:, k, :], op0=ALU.mult, op1=ALU.add))
                        v.sem_inc(m_cv, 1)
                        v.wait_ge(m_bc, 1).then_inc(m_bc, -1)
                        own(nc.vector.tensor_copy(bc[:], Bp[0:96, :]))
                        own(nc.vector.tensor_tensor(bc_left[:], Bp[0:96, :], bc[:], ALU.subtract))
                        own(nc.vector.tensor_copy(bc[32:64, :], bc_left[32:64, :]))
                        own(nc.vector.tensor_copy(bc[64:96, :], bc_left[64:96, :]))
                        own(nc.vector.tensor_tensor(bc_left[64:96, :], bc_left[64:96, :], bc[64:96, :], ALU.subtract))
                        own(nc.vector.tensor_copy(bc[64:96, :], bc_left[64:96, :]))
                        v.sem_inc(m_rows, 1)
                        v.wait_ge(m_e, 1).then_inc(m_e, -1)
                        for k in range(2):
                            own(nc.vector.tensor_scalar(delta[:, k, :], two(Y[:])[:, k, :], m["dtb"][:, k:k + 1], 0.0, ALU.add, ALU.max))
                        own(nc.vector.tensor_tensor(delta[:], delta[:], low[:], ALU.add))
                        own(nc.vector.tensor_scalar(dx[:], ex[:], 1.0, 1.0, ALU.add, ALU.subtract))
                        own(nc.vector.tensor_tensor(dx[:], ex[:], dx[:], ALU.subtract))
                        own(nc.vector.tensor_tensor(delta[:], delta[:], dx[:], ALU.add))
                        v.sem_inc(m_delta, 1)
                        own(nc.vector.tensor_tensor(dx[:], delta[:], uu[:], ALU.mult))
                        v.sem_inc(m_rest, 1)
                        with v.Fori(0, NS // 2) as pair:
                            for q in range(2):
                                v.wait_ge(m_B, 1).then_inc(m_B, -1)
                                for k in range(2):
                                    nc.vector.tensor_tensor(dBx[q][:, k, :], Bp, dx[:, k, :], ALU.mult).then_inc(m_dve, 1)
                                v.wait_ge(m_dve, 2).then_inc(m_dve, -2)
                                v.sem_inc(m_bfree, 1)
                                for k in range(2):
                                    v.wait_ge(m_dA, 1).then_inc(m_dA, -1)
                                    v.wait_ge(m_hfree, 1).then_inc(m_hfree, -1)
                                    nc.vector.tensor_tensor_scan(h[:, k, :], dA[q][:, k, :], dBx[q][:, k, :], 0.0, ALU.mult, ALU.add).then_inc(m_h, 1)
                        v.wait_ge(m_y, 1).then_inc(m_y, -1)
                        v.sem_inc(m_chfree, 1)
                        nc.vector.tensor_tensor(cv[:], two(Y[:]), gate[:], ALU.mult).then_inc(m_gy, 1)
                        v.wait_ge(m_o, 1).then_inc(m_o, -1)
                        own(nc.vector.tensor_tensor(x_st[:], tiles_of(Bp), x_st[:], ALU.add))
                        own(layernorm(v, lambda t: x_st[:, t, :], st, mv, rs,
                                      lambda t: X[:, bass.ds(b * GT + t, 1), :].rearrange("p o d -> p (o d)")))
                        v.sem_inc(m_next, 1)

                @block.gpsimd
                def _(g):
                    g.sem_inc(m_dAfree, 4)
                    g.sem_inc(m_csfree, 2)
                    g.sem_inc(m_hfree, 2)
                    with g.Fori(0, SEQ) as b:
                        with g.Fori(0, NS // 2) as pair:
                            for q in range(2):
                                g.wait_ge(m_Cs, 1).then_inc(m_Cs, -1)
                                for k in range(2):
                                    g.wait_ge(m_h, 1).then_inc(m_h, -1)
                                    g.wait_ge(m_chfree, 1).then_inc(m_chfree, -1)
                                    nc.gpsimd.tensor_tensor(ch[:, k, :], h[:, k, :], Cs[q][:], ALU.mult).then_inc(m_pool, 1)
                                    g.wait_ge(m_pool, 1).then_inc(m_pool, -1)
                                    g.sem_inc(m_ch, 1)
                                    g.sem_inc(m_hfree, 1)
                                    g.sem_inc(m_dAfree, 1)
                                g.sem_inc(m_csfree, 1)
                        inverse_root(g, mv, ve, rs)

                @block.tensor
                def _(pe):
                    def rows_of(r, dst, done):
                        for c in range(2):
                            mm = nc.tensor.matmul(dst[:, c * BANK:(c + 1) * BANK], sel[0:96, bass.ds(r * P, P)] if not isinstance(r, int)
                                                  else sel[0:96, r * P:(r + 1) * P], bc[:, c * BANK:(c + 1) * BANK], start=True, stop=True)
                        mm.then_inc(done, 1)

                    def add_state(last):
                        for k in range(2):
                            pe.wait_ge(m_ch, 1).then_inc(m_ch, -1)
                            for c in range(2):
                                mm = nc.tensor.matmul(Y[:, k * GN + c * BANK:k * GN + (c + 1) * BANK], ident, ch[:, k, c * BANK:(c + 1) * BANK],
                                                      start=False, stop=last)
                            mm.then_inc(m_y if last and k else m_chfree, 1)

                    pe.wait_ge(m_w, 16)
                    pe.wait_ge(m_sel, 1)
                    pe.sem_inc(m_chfree, 2)
                    with pe.Fori(0, SEQ) as b:
                        pe.wait_ge(m_xst, 1).then_inc(m_xst, -1)
                        for t in range(GT):
                            mm = nc.tensor.transpose(Bp[:, t * P:(t + 1) * P], x_st[:, t, :], ident)
                        mm.then_inc(m_T, 1)
                        pe.wait_ge(m_xT, 1).then_inc(m_xT, -1)
                        for part, dst, done in ((0, Y, m_xi), (1, PS[0], m_z)):
                            for k in range(2):
                                for c in range(2):
                                    mm = nc.tensor.matmul(dst[:, k * GN + c * BANK:k * GN + (c + 1) * BANK],
                                                          m["in"][:, (2 * part + k) * P:(2 * part + k + 1) * P],
                                                          xT[:, c * BANK:(c + 1) * BANK], start=True, stop=True)
                            mm.then_inc(done, 1)
                        pe.wait_ge(m_u, 1).then_inc(m_u, -1)
                        pe.wait_ge(m_zs, 1).then_inc(m_zs, -1)
                        for o in range(2):
                            for c in range(2):
                                for k in range(2):
                                    mm = nc.tensor.matmul(Y[:, o * GN + c * BANK:o * GN + (c + 1) * BANK], w_xp[:, k, o * P:(o + 1) * P],
                                                          uu[:, k, c * BANK:(c + 1) * BANK], start=k == 0, stop=k == 1)
                        mm.then_inc(m_dr, 1)
                        for c in range(2):
                            for k in range(2):
                                mm = nc.tensor.matmul(Bp[0:96, c * BANK:(c + 1) * BANK], w_xp[:, k, DI:DI + 96],
                                                      uu[:, k, c * BANK:(c + 1) * BANK], start=k == 0, stop=k == 1)
                        mm.then_inc(m_bc, 1)
                        pe.wait_ge(m_drs, 1).then_inc(m_drs, -1)
                        for o in range(2):
                            for c in range(2):
                                for k in range(2):
                                    mm = nc.tensor.matmul(Y[:, o * GN + c * BANK:o * GN + (c + 1) * BANK], w_dt[:, k, o * P:(o + 1) * P],
                                                          low[:, k, c * BANK:(c + 1) * BANK], start=k == 0, stop=k == 1)
                        mm.then_inc(m_dt, 1)
                        pe.wait_ge(m_rows, 1).then_inc(m_rows, -1)
                        pe.wait_ge(m_rest, 1).then_inc(m_rest, -1)
                        for k in range(2):
                            for c in range(2):
                                nc.tensor.matmul(Y[:, k * GN + c * BANK:k * GN + (c + 1) * BANK], skip[:, k, :],
                                                 uu[:, k, c * BANK:(c + 1) * BANK], start=True, stop=False)
                        rows_of(0, Bp, m_B)
                        rows_of(NS, Cp, m_C)
                        with pe.Fori(1, NS) as n:
                            pe.wait_ge(m_bfree, 1).then_inc(m_bfree, -1)
                            rows_of(n, Bp, m_B)
                            pe.wait_ge(m_cfree, 1).then_inc(m_cfree, -1)
                            rows_of(n + NS, Cp, m_C)
                            add_state(False)
                        add_state(True)
                        pe.wait_ge(m_bfree, 1).then_inc(m_bfree, -1)
                        pe.wait_ge(m_cfree, 1).then_inc(m_cfree, -1)
                        pe.wait_ge(m_gy, 1).then_inc(m_gy, -1)
                        for t in range(GT):
                            for k in range(2):
                                mm = nc.tensor.matmul(Bp[:, t * P:(t + 1) * P], cv[:, k, t * P:(t + 1) * P], w_out[:, k, :],
                                                      start=k == 0, stop=k == 1)
                        mm.then_inc(m_o, 1)


        with ExitStack() as ph:
            def pb(name, shape, dt=F32):
                return [sb(f"f_{name}{u}", shape, dt, ph) for u in range(2)]
            FT = 4
            CN = FT * P
            MB = HID // P
            wf = sb("wf", [P, WF_W], F32, ph)
            f = {n: wf[:, c] for n, c in WF.items()}
            w3 = sb("w3", [P, MB, D], F32, ph)
            x_st, xT, ha, hb = pb("x_st", [P, FT, D]), pb("xT", [P, CN]), pb("ha", [P, MB, CN]), pb("hb", [P, MB, CN])
            y, yo = pb("y", [P, FT, D]), pb("yo", [P, FT, D])
            st, mv, ve, rs = pb("st", [P, FT, 6]), pb("mv", [P, FT, 2]), pb("ve", [P, FT]), pb("rs", [P, FT])
            (f_w, f_xst, f_T, f_xT, f_a, f_s, f_b, f_h, f_c, f_g, f_o, f_dve, f_free, f_out0, f_out1, f_yo, f_w3, f_y) = [
                sem("f_" + n) for n in "w xst T xT a s b h c g o dve free out0 out1 yo w3 y".split()]
            bank = lambda u, k: PS[u][:, k * BANK:(k + 1) * BANK]
            both = range(2)

            with nc.Block() as block:
                @block.sync
                def _(sp):
                    sp.dma_start(wf[:], wf_in).then_inc(f_w, 16)
                    with sp.Fori(0, TILES // FT // 2) as pair:
                        for u in both:
                            sp.wait_ge(f_yo, 1).then_inc(f_yo, -1)
                            sp.dma_start(out_tiles[:, bass.ds(pair * (2 * FT) + u * FT, FT), :], yo[u][:]).then_inc((f_out0, f_out1)[u], 16)
                    sp.wait_ge(f_out0, 16)
                    sp.wait_ge(f_out1, 16)

                @block.scalar
                def _(s):
                    s.wait_ge(f_w, 16)
                    with s.Fori(0, TILES // FT // 2) as pair:
                        for u in both:
                            s.wait_ge(f_free, 1).then_inc(f_free, -1)
                            nc.scalar.copy(x_st[u][:], X[:, bass.ds(pair * (2 * FT) + u * FT, FT), :]).then_inc(f_xst, 1)
                        for u in both:
                            s.wait_ge(f_T, 1).then_inc(f_T, -1)
                            nc.scalar.copy(xT[u][:], bank(u, 0)).then_inc(f_xT, 1)
                        for u in both:
                            for k in range(MB):
                                s.wait_ge(f_a, 1).then_inc(f_a, -1)
                                nc.scalar.activation(ha[u][:, k, :], bank(u, k), ACT.Silu, scale=f["s1"][:, k:k + 1]).then_inc(f_s, 1)
                        for src, dst, sc in ((hb, ha, "t1"), (ha, hb, "t2")):
                            for u in both:
                                for k in range(MB):
                                    s.wait_ge(f_c, 1).then_inc(f_c, -1)
                                    nc.scalar.activation(dst[u][:, k, :], bank(u, k), ACT.Gelu, scale=f[sc][:, k:k + 1]).then_inc(f_g, 1)

                @block.vector
                def _(v):
                    def own(ins):
                        ins.then_inc(f_dve, 1)
                        v.wait_ge(f_dve, 1).then_inc(f_dve, -1)

                    v.wait_ge(f_w, 16)
                    own(nc.vector.tensor_tensor(w3[:], f["w3"].rearrange("p (k d) -> p k d", d=D),
                                                f["s3"][:, None, :].to_broadcast([P, MB, D]), ALU.mult))
                    v.sem_inc(f_w3, 1)
                    v.sem_inc(f_free, 2)
                    v.sem_inc(f_out0, 16)
                    v.sem_inc(f_out1, 16)
                    v.sem_inc(f_y, 2)
                    with v.Fori(0, TILES // FT // 2) as pair:
                        for u in both:
                            for k in range(MB):
                                v.wait_ge(f_b, 1).then_inc(f_b, -1)
                                nc.vector.scalar_tensor_tensor(out=hb[u][:, k, :], in0=bank(u, k), scalar=f["s2"][:, k:k + 1],
                                                               in1=ha[u][:, k, :], op0=ALU.mult, op1=ALU.mult).then_inc(f_h, 1)
                        for u in both:
                            v.wait_ge(f_o, 1).then_inc(f_o, -1)
                            own(nc.vector.tensor_tensor(y[u][:], tiles_of(bank(u, 0)), x_st[u][:], ALU.add))
                            v.sem_inc(f_free, 1)
                            v.sem_inc(f_y, 1)
                            v.wait_ge((f_out0, f_out1)[u], 16).then_inc((f_out0, f_out1)[u], -16)
                            own(layernorm(v, lambda t: y[u][:, t, :], st[u], mv[u], rs[u], lambda t: yo[u][:, t, :], FT))
                            v.sem_inc(f_yo, 1)

                @block.gpsimd
                def _(g):
                    with g.Fori(0, TILES // FT // 2) as pair:
                        for u in both:
                            inverse_root(g, mv[u], ve[u], rs[u], FT)

                @block.tensor
                def _(pe):
                    pe.wait_ge(f_w, 16)
                    pe.wait_ge(f_w3, 1)
                    with pe.Fori(0, TILES // FT // 2) as pair:
                        for u in both:
                            pe.wait_ge(f_xst, 1).then_inc(f_xst, -1)
                            pe.wait_ge(f_y, 1).then_inc(f_y, -1)
                            for t in range(FT):
                                mm = nc.tensor.transpose(PS[u][:, t * P:(t + 1) * P], x_st[u][:, t, :], ident)
                            mm.then_inc(f_T, 1)
                        for u in both:
                            pe.wait_ge(f_xT, 1).then_inc(f_xT, -1)
                            for k in range(MB):
                                nc.tensor.matmul(bank(u, k), f["w1"][:, k * P:(k + 1) * P], xT[u][:], start=True, stop=True).then_inc(f_a, 1)
                        for u in both:
                            for k in range(MB):
                                pe.wait_ge(f_s, 1).then_inc(f_s, -1)
                                nc.tensor.matmul(bank(u, k), f["w2"][:, k * P:(k + 1) * P], xT[u][:], start=True, stop=True).then_inc(f_b, 1)
                        for src, wn, ready in ((hb, "h1", f_h), (ha, "h2", f_g)):
                            for u in both:
                                pe.wait_ge(ready, MB).then_inc(ready, -MB)
                                for o in range(MB):
                                    for k in range(MB):
                                        mm = nc.tensor.matmul(bank(u, o), f[wn][:, k * HID + o * P:k * HID + (o + 1) * P], src[u][:, k, :],
                                                              start=k == 0, stop=k == MB - 1)
                                    mm.then_inc(f_c, 1)
                        for u in both:
                            pe.wait_ge(f_g, MB).then_inc(f_g, -MB)
                            for t in range(FT):
                                for k in range(MB):
                                    mm = nc.tensor.matmul(PS[u][:, t * P:(t + 1) * P], hb[u][:, k, t * P:(t + 1) * P], w3[:, k, :],
                                                          start=k == 0, stop=k == MB - 1)
                            mm.then_inc(f_o, 1)


def _packed(i):
    T = np.transpose
    col = lambda a: np.reshape(a, (-1, P)).T
    rows = lambda a: np.broadcast_to(np.reshape(a, (1, -1)), (P, np.size(a)))
    halves = lambda m: np.concatenate([m[k:k + P] for k in range(0, m.shape[0], P)], 1)
    qkv = i["L0_ffn_qkv_weight"]
    spread = lambda m: np.repeat(m.reshape(4, 1, HD, D), 4, 1).reshape(P, D)
    wa = np.concatenate([T(i["L0_attn_W_q"]), T(i["L0_attn_W_k"]), T(i["L0_attn_W_v"]), T(i["L0_attn_W_o"]),
                         T(qkv[0:128]), T(spread(qkv[128:160])), T(spread(qkv[160:192])), T(i["L0_ffn_proj_weight"]),
                         T(i["L0_ffn_router_weight"]), col(i["L0_attn_b_q"]), col(i["L0_ffn_ln1_weight"]),
                         col(i["L0_ffn_ln1_bias"]), col(i["L0_ffn_ln2_weight"]), col(i["L0_ffn_ln2_bias"]),
                         rows(i["L0_attn_b_k"]), rows(i["L0_attn_b_v"]), rows(i["L0_attn_b_o"])], 1)
    w1, w2 = i["L0_ffn_moe_w1"], i["L0_ffn_moe_w2"]
    moe = np.concatenate([T(w1, (0, 2, 1)), T(w2[:, :, 0:P], (0, 2, 1)), T(w2[:, :, P:], (0, 2, 1))], 2)
    xp = T(i["L1_attn_x_proj_w"])
    xp = np.concatenate([xp[:, 0:DI]] + [xp[:, DI:]] * 3, 1)
    wm = np.concatenate([T(i["L1_attn_in_proj_w"]), halves(xp), halves(T(i["L1_attn_dt_proj_w"])),
                         halves(T(i["L1_attn_out_proj_w"])), halves(np.reshape(i["L1_attn_conv_w"], (DI, TAPS))),
                         col(i["L1_attn_conv_b"]), col(i["L1_attn_dt_proj_b"]), halves(i["L1_attn_A_log"]),
                         col(i["L1_attn_D_param"])], 1)
    wf = np.concatenate([T(i["L1_ffn_w1_w"]), T(i["L1_ffn_w2_w"]), halves(T(i["L1_ffn_h1_w"])),
                         halves(T(i["L1_ffn_h2_w"])), halves(T(i["L1_ffn_w3_w"])), col(i["L1_ffn_w1_s"]),
                         col(i["L1_ffn_w2_s"]), col(i["L1_ffn_h1_s"]), col(i["L1_ffn_h2_s"]), rows(i["L1_ffn_w3_s"])], 1)
    return wa, moe, wm, wf


def _constants():
    p = np.arange(P)
    block = (p[:, None] // HD == p[None, :] // HD)
    head = (p[:, None] // HD == np.arange(HEADS)[None, :])
    before = p[:, None] < p[None, :]
    decay = np.exp(-(np.arange(POS, dtype=np.float32) / np.float32(POS))).reshape(GT, P).T
    part = p[:, None] % 32 == np.arange(32)[None, :]
    const = np.concatenate([np.eye(P), block, head, before, np.broadcast_to(np.arange(EXP), (P, EXP)), decay, part],
                           1).astype(np.float32)
    return const


def kernel(**inputs):
    import concourse.bacc as bacc
    from concourse.bass_utils import run_bass_kernel_spmd

    i = {n: np.asarray(a) for n, a in inputs.items()}
    wa, moe, wm, wf = _packed(i)
    const = _constants()
    arrays = {"x": i["L0_attn_x"].reshape(TOK, D), "const": const, "wa": wa, "moe": moe, "wm": wm, "wf": wf}
    arrays = {n: np.ascontiguousarray(a) for n, a in arrays.items()}
    nc = bacc.Bacc("TRN2", target_bir_lowering=False, num_devices=1)
    aps = [nc.dram_tensor(n + "_dram", a.shape, mybir.dt.from_np(a.dtype), kind="ExternalInput").ap() for n, a in arrays.items()]
    y = nc.dram_tensor("y_dram", (TOK, D), F32, kind="ExternalOutput").ap()
    program(nc, *aps, y)
    r = run_bass_kernel_spmd(nc, [{n + "_dram": a for n, a in arrays.items()}], core_ids=[0])
    return r.results[0]["y_dram"].reshape(SEQ, POS, D)
```

```python
from contextlib import ExitStack

import numpy as np

import concourse.bass as bass
from concourse import mybir

P = 128
SEQ, POS, D = 8, 1024, 128
TOK = SEQ * POS
TILES = TOK // P
GT = 8
GN = GT * P
BANK = 512
HEADS, HD = 16, 8
EXP, FFN, TOPK = 16, 256, 2
CAP = int(np.ceil(TOK * TOPK / EXP * 1.25))
SLOTS = EXP * CAP
CT = CAP // P
DI, NS, TAPS = 256, 16, 4
HID = 512
LN_EPS, ATT_EPS = 1e-5, 1e-6

F32 = mybir.dt.float32
BF16 = mybir.dt.bfloat16
U32 = mybir.dt.uint32
ALU = mybir.AluOpType
ACT = mybir.ActivationFunctionType
AX = mybir.AxisListType.X


def columns(widths):
    at, out = 0, {}
    for name, w in widths:
        out[name] = slice(at, at + w)
        at += w
    return out, at


CONST, CONST_W = columns([("ident", P), ("block", P), ("head", HEADS), ("before", P), ("iota", EXP),
                          ("decay", GT), ("part", 32)])
WA, WA_W = columns([("q", P), ("k", P), ("v", P), ("o", P), ("gq", P), ("gk", P), ("gv", P), ("proj", P),
                    ("router", EXP), ("bq", 1), ("ln1w", 1), ("ln1b", 1), ("ln2w", 1), ("ln2b", 1),
                    ("bk", P), ("bv", P), ("bo", P)])
WM, WM_W = columns([("in", 2 * DI), ("xp", 2 * (DI + 96)), ("dt", 2 * DI), ("out", 2 * D), ("cw", 2 * TAPS),
                    ("cb", 2), ("dtb", 2), ("alog", 2 * NS), ("dpar", 2)])
WF, WF_W = columns([("w1", HID), ("w2", HID), ("h1", 4 * HID), ("h2", 4 * HID), ("w3", 4 * D),
                    ("s1", 4), ("s2", 4), ("t1", 4), ("t2", 4), ("s3", D)])


def program(nc, x_in, const_in, wa_in, moe_in, wm_in, wf_in, out):
    x_tiles = x_in.rearrange("(i p) d -> p i d", p=P)
    out_tiles = out.rearrange("(i p) d -> p i d", p=P)
    slot_rows = nc.dram_tensor("slot_rows", (SLOTS, D), F32, kind="Internal").ap()
    slot_outs = nc.dram_tensor("slot_outs", (SLOTS, D), F32, kind="Internal").ap()
    x_mid = nc.dram_tensor("x_mid", (P, TILES, D), F32, kind="Internal").ap()

    with ExitStack() as ctx:
        def sb(name, shape, dt=F32, stack=ctx):
            return stack.enter_context(nc.sbuf_tensor(name, shape, dt))

        def sem(name):
            return ctx.enter_context(nc.semaphore(name))

        const = sb("const", [P, CONST_W])
        minus_half = sb("minus_half", [P, GT])
        x_stack = ctx.enter_context(ExitStack())
        X = sb("X", [P, TILES, D], stack=x_stack)
        ident = const[:, CONST["ident"]]
        PS = [ctx.enter_context(nc.psum_tensor(f"ps{u}", [P, 4 * BANK], F32)) for u in range(2)]

        def tiles_of(t, n=GT, w=D):
            return t.rearrange("p (t d) -> p t d", d=w) if n else t

        ln_sems = {n: sem("ln_" + n) for n in ("stats", "moments", "eps", "power")}

        def moments(v, y, st, mv, n=GT):
            for t in range(n):
                nc.vector.bn_stats(st[:, t, :], y(t)).then_inc(ln_sems["stats"], 1)
            v.wait_ge(ln_sems["stats"], n).then_inc(ln_sems["stats"], -n)
            for t in range(n):
                last = nc.vector.bn_aggr(mv[:, t, :], st[:, t, :])
            last.then_inc(ln_sems["moments"], 1)

        def normalise(v, y, mv, rs, dst, n=GT):
            v.wait_ge(ln_sems["power"], 1).then_inc(ln_sems["power"], -1)
            for t in range(n):
                last = nc.vector.tensor_scalar(dst(t), y(t), mv[:, t, 0:1], rs[:, t:t + 1],
                                               ALU.subtract, ALU.mult)
            return last

        def layernorm(v, y, st, mv, rs, dst, n=GT):
            moments(v, y, st, mv, n)
            return normalise(v, y, mv, rs, dst, n)

        def inverse_root(g, mv, ve, rs, n=GT):
            g.wait_ge(ln_sems["moments"], 1).then_inc(ln_sems["moments"], -1)
            nc.gpsimd.tensor_scalar(ve[:], mv[:, :, 1], LN_EPS, None, ALU.add).then_inc(ln_sems["eps"], 1)
            g.wait_ge(ln_sems["eps"], 1).then_inc(ln_sems["eps"], -1)
            nc.gpsimd.tensor_tensor(rs[:], ve[:], minus_half[:, 0:n], ALU.pow).then_inc(ln_sems["power"], 1)

        wa_stack = ctx.enter_context(ExitStack())
        wa = sb("wa", [P, WA_W], stack=wa_stack)
        w = {n: wa[:, c] for n, c in WA.items()}
        zeros = sb("zeros", [P, 1024], stack=wa_stack)

        with ExitStack() as ph:
            def pb(name, shape, dt=F32):
                return [sb(f"a_{name}{u}", shape, dt, ph) for u in range(2)]

            x_ld, xT, kf, vv = pb("x", [P, GT, D]), pb("xT", [P, GN]), pb("kf", [P, GT, D]), pb("vv", [P, GT, D + 2])
            kv, qf, den, att = pb("kv", [P, D + HEADS]), pb("qf", [P, GN]), pb("den", [P, GT, HEADS]), pb("att", [P, GT, D])
            attT, xb, y = pb("attT", [P, GN]), pb("xb", [P, GT, D]), pb("y", [P, GT, D])
            st, mv, ve, rs = pb("st", [P, GT, 6]), pb("mv", [P, GT, 2]), pb("ve", [P, GT]), pb("rs", [P, GT])
            (s_const, s_wa, s_zero, s_x, s_xfree, s_xp, s_T, s_xT, s_k, s_v, s_kf, s_kvp, s_kv, s_qp, s_qf, s_num,
             s_att, s_aT, s_aTs, s_o, s_xb, s_dve, s_ready, s_psfree, s_xbfree, s_half, s_x1) = [
                sem("a_" + n) for n in "const wa zero x xfree xp T xT k v kf kvp kv qp qf num att aT aTs o xb dve ready psfree xbfree half x1".split()]
            decay = const[:, CONST["decay"]]

            def bc_tiles(row, n=GT, width=D):
                return row[:, None, :].to_broadcast([P, n, width])

            A = [PS[u][:, 0:GN] for u in range(2)]
            B = [PS[u][:, GN:2 * GN] for u in range(2)]

            with nc.Block() as block:
                @block.sync
                def _(sp):
                    sp.dma_start(const[:], const_in).then_inc(s_const, 16)
                    sp.dma_start(wa[:], wa_in).then_inc(s_wa, 16)
                    with sp.Fori(0, SEQ // 2) as pair:
                        for u in range(2):
                            sp.wait_ge(s_xfree, 1).then_inc(s_xfree, -1)
                            sp.dma_start(x_ld[u][:], x_tiles[:, bass.ds(pair * (2 * GT) + u * GT, GT), :]).then_inc((s_x, s_x1)[u], 16)
                    sp.wait_ge(s_zero, 1)
                    for r in range(0, SLOTS, 1024):
                        sp.dma_start(slot_rows[r:r + 1024, :].rearrange("(p a) d -> p (a d)", p=P),
                                     zeros[:, 0:1024]).then_inc(s_half, 16)
                    sp.wait_ge(s_half, 16 * (SLOTS // 1024))

                @block.gpsimd
                def _(g):
                    nc.gpsimd.memset(minus_half[:], -0.5)
                    nc.gpsimd.memset(zeros[:], 0.0).then_inc(s_zero, 1)
                    g.sem_inc(s_xfree, 2)
                    g.wait_ge(s_wa, 16)
                    with g.Fori(0, SEQ // 2) as pair:
                        for u in range(2):
                            g.wait_ge(s_xp, 1).then_inc(s_xp, -1)
                            g.wait_ge(s_xbfree, 1).then_inc(s_xbfree, -1)
                            nc.gpsimd.tensor_tensor(xb[u][:], x_ld[u][:], bc_tiles(w["bo"]), ALU.add).then_inc(s_xb, 1)
                            g.wait_ge(s_xb, 1).then_inc(s_xb, -1)
                            g.sem_inc(s_ready, 1)
                            g.sem_inc(s_xfree, 1)
                        for u in range(2):
                            inverse_root(g, mv[u], ve[u], rs[u])

                @block.scalar
                def _(s):
                    s.wait_ge(s_wa, 16)
                    with s.Fori(0, SEQ // 2) as pair:
                        for u in range(2):
                            s.wait_ge(s_T, 1).then_inc(s_T, -1)
                            s.sem_inc(s_xp, 1)
                            nc.scalar.copy(xT[u][:], A[u]).then_inc(s_xT, 1)
                        for u in range(2):
                            s.wait_ge(s_qp, 1).then_inc(s_qp, -1)
                            nc.scalar.activation(qf[u][:], A[u], ACT.Relu, bias=w["bq"]).then_inc(s_qf, 1)
                        for u in range(2):
                            s.wait_ge(s_aT, 1).then_inc(s_aT, -1)
                            nc.scalar.copy(attT[u][:], A[u]).then_inc(s_aTs, 1)

                @block.vector
                def _(v):
                    def own(ins):
                        ins.then_inc(s_dve, 1)
                        v.wait_ge(s_dve, 1).then_inc(s_dve, -1)

                    for u in range(2):
                        own(nc.vector.memset(vv[u][:], 1.0))
                    v.sem_inc(s_xbfree, 2)
                    v.sem_inc(s_psfree, 2)
                    v.wait_ge(s_const, 16)
                    v.wait_ge(s_wa, 16)
                    with v.Fori(0, SEQ // 2) as pair:
                        for u in range(2):
                            v.wait_ge(s_k, 1).then_inc(s_k, -1)
                            own(nc.vector.tensor_tensor(kf[u][:], tiles_of(B[u]), bc_tiles(w["bk"]), ALU.add))
                            nc.vector.scalar_tensor_tensor(
                                out=kf[u][:], in0=kf[u][:], scalar=0.0,
                                in1=decay[:, :, None].to_broadcast([P, GT, D]), op0=ALU.max, op1=ALU.mult).then_inc(s_kf, 1)
                            v.wait_ge(s_v, 1).then_inc(s_v, -1)
                            nc.vector.tensor_tensor(vv[u][:, :, 0:D], tiles_of(A[u]), bc_tiles(w["bv"]), ALU.add).then_inc(s_kf, 1)
                        for u in range(2):
                            v.wait_ge(s_kvp, 1).then_inc(s_kvp, -1)
                            nc.vector.tensor_tensor(kv[u][:, 0:D], B[u][:, 0:D], const[:, CONST["block"]], ALU.mult)
                            nc.vector.tensor_scalar(kv[u][:, D:], const[:, CONST["head"]], B[u][:, D:D + 1],
                                                    None, ALU.mult).then_inc(s_kv, 1)
                        for u in range(2):
                            v.wait_ge(s_num, 1).then_inc(s_num, -1)
                            own(nc.vector.tensor_tensor(den[u][:], B[u][:, 0:GT * HEADS].rearrange("p (t h) -> p t h", h=HEADS),
                                                        decay[:, :, None].to_broadcast([P, GT, HEADS]), ALU.mult))
                            own(nc.vector.tensor_scalar(den[u][:], den[u][:], ATT_EPS, None, ALU.add))
                            own(nc.vector.reciprocal(den[u][:], den[u][:]))
                            own(nc.vector.tensor_tensor(den[u][:], den[u][:],
                                                        decay[:, :, None].to_broadcast([P, GT, HEADS]), ALU.mult))
                            nc.vector.tensor_tensor(
                                att[u][:].rearrange("p t (h e) -> p (t h) e", e=HD),
                                A[u].rearrange("p (q e) -> p q e", e=HD),
                                den[u][:].rearrange("p t h -> p (t h)")[:, :, None].to_broadcast([P, GT * HEADS, HD]),
                                ALU.mult).then_inc(s_att, 1)
                        for u in range(2):
                            v.wait_ge(s_o, 1).then_inc(s_o, -1)
                            v.wait_ge(s_ready, 1).then_inc(s_ready, -1)
                            own(nc.vector.tensor_tensor(y[u][:], tiles_of(B[u]), xb[u][:], ALU.add))
                            v.sem_inc(s_psfree, 1)
                            v.sem_inc(s_xbfree, 1)
                            last = layernorm(v, lambda t: y[u][:, t, :], st[u], mv[u], rs[u],
                                             lambda t: X[:, bass.ds(pair * (2 * GT) + (u * GT + t), 1), :].rearrange("p o d -> p (o d)"))
                            own(last)

                @block.tensor
                def _(pe):
                    pe.wait_ge(s_const, 16)
                    pe.wait_ge(s_wa, 16)
                    with pe.Fori(0, SEQ // 2) as pair:
                        for u in range(2):
                            pe.wait_ge((s_x, s_x1)[u], 16).then_inc((s_x, s_x1)[u], -16)
                            pe.wait_ge(s_psfree, 1).then_inc(s_psfree, -1)
                            for t in range(GT):
                                mm = nc.tensor.transpose(A[u][:, t * P:(t + 1) * P], x_ld[u][:, t, :], ident)
                            mm.then_inc(s_T, 1)
                        for u in range(2):
                            pe.wait_ge(s_xT, 1).then_inc(s_xT, -1)
                            for t in range(GT):
                                mm = nc.tensor.matmul(B[u][:, t * P:(t + 1) * P], xT[u][:, t * P:(t + 1) * P], w["k"],
                                                      start=True, stop=True)
                            mm.then_inc(s_k, 1)
                            for t in range(GT):
                                mm = nc.tensor.matmul(A[u][:, t * P:(t + 1) * P], xT[u][:, t * P:(t + 1) * P], w["v"],
                                                      start=True, stop=True)
                            mm.then_inc(s_v, 1)
                        for u in range(2):
                            pe.wait_ge(s_kf, 2).then_inc(s_kf, -2)
                            for c in range(2):
                                mm = nc.tensor.matmul(A[u][:, c * BANK:(c + 1) * BANK], w["q"],
                                                      xT[u][:, c * BANK:(c + 1) * BANK], start=True, stop=True)
                            mm.then_inc(s_qp, 1)
                            for t in range(GT):
                                mm = nc.tensor.matmul(B[u][:, 0:D + 1], kf[u][:, t, :], vv[u][:, t, 0:D + 1],
                                                      start=t == 0, stop=t == GT - 1)
                            mm.then_inc(s_kvp, 1)
                        for u in range(2):
                            pe.wait_ge(s_qf, 1).then_inc(s_qf, -1)
                            pe.wait_ge(s_kv, 1).then_inc(s_kv, -1)
                            for t in range(GT):
                                nc.tensor.matmul(A[u][:, t * P:(t + 1) * P], qf[u][:, t * P:(t + 1) * P], kv[u][:, 0:D],
                                                 start=True, stop=True)
                                mm = nc.tensor.matmul(B[u][:, t * HEADS:(t + 1) * HEADS], qf[u][:, t * P:(t + 1) * P],
                                                      kv[u][:, D:], start=True, stop=True)
                            mm.then_inc(s_num, 1)
                        for u in range(2):
                            pe.wait_ge(s_att, 1).then_inc(s_att, -1)
                            for t in range(GT):
                                mm = nc.tensor.transpose(A[u][:, t * P:(t + 1) * P], att[u][:, t, :], ident)
                            mm.then_inc(s_aT, 1)
                        for u in range(2):
                            pe.wait_ge(s_aTs, 1).then_inc(s_aTs, -1)
                            for t in range(GT):
                                mm = nc.tensor.matmul(B[u][:, t * P:(t + 1) * P], attT[u][:, t * P:(t + 1) * P], w["o"],
                                                      start=True, stop=True)
                            mm.then_inc(s_o, 1)

        moe_stack = ctx.enter_context(ExitStack())
        Z2 = sb("Z2", [P, TILES, D], stack=moe_stack)
        prob = sb("prob", [P, TILES, EXP], stack=moe_stack)
        Xg = X[:].rearrange("p (s j) d -> p s j d", j=GT)
        Zg = Z2[:].rearrange("p (s j) d -> p s j d", j=GT)
        prob_g = prob[:].rearrange("p (s j) e -> p s j e", j=GT)
        pair_at = [sum(GT - k for k in range(s)) for s in range(GT + 1)]
        with ExitStack() as ph:
            def pb(name, shape, dt=F32):
                return [sb(f"b_{name}{u}", shape, dt, ph) for u in range(2)]

            z, zT, Q, K, V = pb("z", [P, GT, D]), pb("zT", [P, GN]), pb("Q", [P, GT, D]), pb("K", [P, GT, D]), pb("V", [P, GT, D])
            prod = pb("prod", [P, pair_at[GT], D])
            score, attn = pb("score", [P, GT, GT, HEADS]), pb("attn", [P, GT, GT, HEADS])
            smax, ssum = pb("smax", [P, GT, HEADS]), pb("ssum", [P, GT, HEADS])
            att, H = pb("att", [P, GT, D]), pb("H", [P, GT, D])
            lg, lmax, lsum = pb("lg", [P, GT, EXP]), pb("lmax", [P, GT]), pb("lsum", [P, GT])
            st, mv, ve, rs = pb("st", [P, GT, 6]), pb("mv", [P, GT, 2]), pb("ve", [P, GT]), pb("rs", [P, GT])
            (b_z, b_zT, b_zTs, b_q, b_k, b_v, b_qe, b_ke, b_ve, b_pr, b_sub, b_exp, b_av, b_at, b_aT, b_aTs, b_o,
             b_h, b_z2, b_zT2, b_zTs2, b_lg, b_ls, b_le, b_dve, b_pool, b_zfree, b_bfree, b_xa) = [
                sem("b_" + n) for n in "z zT zTs q k v qe ke ve pr sub exp av at aT aTs o h z2 zT2 zTs2 lg ls le dve pool zfree bfree xa".split()]
            A = [PS[u][:, 0:GN] for u in range(2)]
            B = [PS[u][:, GN:2 * GN] for u in range(2)]
            both = range(2)
            scale = float(HD) ** -0.5
            rows = lambda t, s: t[:, pair_at[s]:pair_at[s + 1], :]
            over_keys = lambda t: t[:].rearrange("p k q h -> p (q h) k")

            with nc.Block() as block:
                @block.gpsimd
                def _(g):
                    with g.Fori(0, GT // 2) as pair:
                        for u in both:
                            inverse_root(g, mv[u], ve[u], rs[u])
                        for u in both:
                            g.wait_ge(b_ke, 1).then_inc(b_ke, -1)
                            for s in range(GT):
                                nc.gpsimd.tensor_tensor(rows(prod[u], s), Q[u][:, s:, :],
                                                        K[u][:, s:s + 1, :].to_broadcast([P, GT - s, D]),
                                                        ALU.mult).then_inc(b_pr, 1)
                        for u in both:
                            g.wait_ge(b_exp, 1).then_inc(b_exp, -1)
                            for s in range(GT):
                                nc.gpsimd.tensor_tensor(
                                    rows(prod[u], s).rearrange("p q (h e) -> p q h e", e=HD),
                                    attn[u][:, s, s:, :, None].to_broadcast([P, GT - s, HEADS, HD]),
                                    V[u][:, s:s + 1, :].rearrange("p o (h e) -> p o h e", e=HD).to_broadcast([P, GT - s, HEADS, HD]),
                                    ALU.mult).then_inc(b_av, 1)
                        for u in both:
                            inverse_root(g, mv[u], ve[u], rs[u])
                        for u in both:
                            g.wait_ge(b_h, 1).then_inc(b_h, -1)
                            own = nc.gpsimd.tensor_tensor(Xg[:, :, bass.ds(pair * 2 + u, 1), :].rearrange("p s o d -> p s (o d)"),
                                                          Xg[:, :, bass.ds(pair * 2 + u, 1), :].rearrange("p s o d -> p s (o d)"),
                                                          H[u][:], ALU.add)
                            g.wait_ge(b_z2, 1).then_inc(b_z2, -1)
                            nc.gpsimd.tensor_copy(Zg[:, :, bass.ds(pair * 2 + u, 1), :].rearrange("p s o d -> p s (o d)"),
                                                  z[u][:]).then_inc(b_pool, 1)
                            g.wait_ge(b_pool, 1).then_inc(b_pool, -1)
                            g.sem_inc(b_zfree, 1)

                @block.scalar
                def _(s):
                    def evac(ready, dst, src, done):
                        s.wait_ge(ready, 1).then_inc(ready, -1)
                        nc.scalar.copy(dst, src).then_inc(done, 1)

                    with s.Fori(0, GT // 2) as pair:
                        for u in both:
                            s.wait_ge(b_zT, 1).then_inc(b_zT, -1)
                            nc.scalar.activation(zT[u][:], A[u], ACT.Identity, bias=w["ln1b"], scale=w["ln1w"]).then_inc(b_zTs, 1)
                        for u in both:
                            evac(b_q, Q[u][:], tiles_of(B[u]), b_qe)
                            s.wait_ge(b_k, 1).then_inc(b_k, -1)
                            nc.scalar.copy(K[u][:], tiles_of(A[u])).then_inc(b_xa, 1)
                            s.wait_ge(b_xa, 1).then_inc(b_xa, -1)
                            s.sem_inc(b_ke, 1)
                            evac(b_v, V[u][:], tiles_of(B[u]), b_ve)
                        for u in both:
                            s.wait_ge(b_sub, 1).then_inc(b_sub, -1)
                            nc.scalar.activation(attn[u][:], score[u][:], ACT.Exp, scale=scale).then_inc(b_exp, 1)
                        for u in both:
                            evac(b_aT, zT[u][:], A[u], b_aTs)
                        for u in both:
                            s.wait_ge(b_zT2, 1).then_inc(b_zT2, -1)
                            nc.scalar.activation(zT[u][:], A[u], ACT.Identity, bias=w["ln2b"], scale=w["ln2w"]).then_inc(b_zTs2, 1)
                        for u in both:
                            s.wait_ge(b_ls, 1).then_inc(b_ls, -1)
                            nc.scalar.activation(lg[u][:], lg[u][:], ACT.Exp).then_inc(b_le, 1)

                @block.vector
                def _(v):
                    def own(ins):
                        ins.then_inc(b_dve, 1)
                        v.wait_ge(b_dve, 1).then_inc(b_dve, -1)

                    v.sem_inc(b_zfree, 2)
                    v.sem_inc(b_bfree, 2)
                    with v.Fori(0, GT // 2) as pair:
                        xrow = lambda t, u: Xg[:, t, bass.ds(pair * 2 + u, 1), :].rearrange("p o d -> p (o d)")
                        for u in both:
                            v.wait_ge(b_zfree, 1).then_inc(b_zfree, -1)
                            layernorm(v, lambda t: xrow(t, u), st[u], mv[u], rs[u], lambda t: z[u][:, t, :]).then_inc(b_z, 1)
                        for u in both:
                            own(nc.vector.memset(score[u][:], -1e30))
                            for s in range(GT):
                                v.wait_ge(b_pr, 1).then_inc(b_pr, -1)
                                last = nc.vector.tensor_reduce(score[u][:, s, s:, :],
                                                               rows(prod[u], s).rearrange("p q (h e) -> p (q h) e", e=HD), AX, ALU.add)
                            own(last)
                            own(nc.vector.tensor_reduce(smax[u][:], over_keys(score[u]), AX, ALU.max))
                            nc.vector.tensor_tensor(score[u][:], score[u][:], smax[u][:, None, :, :].to_broadcast([P, GT, GT, HEADS]),
                                                    ALU.subtract).then_inc(b_sub, 1)
                        for u in both:
                            v.wait_ge(b_av, 1).then_inc(b_av, -1)
                            own(nc.vector.tensor_reduce(ssum[u][:], over_keys(attn[u]), AX, ALU.add))
                            own(nc.vector.reciprocal(ssum[u][:], ssum[u][:]))
                            for s in range(1, GT):
                                v.wait_ge(b_av, 1).then_inc(b_av, -1)
                                own(nc.vector.tensor_tensor(prod[u][:, s:GT, :], prod[u][:, s:GT, :], rows(prod[u], s), ALU.add))
                            nc.vector.tensor_tensor(
                                att[u][:].rearrange("p q (h e) -> p (q h) e", e=HD),
                                prod[u][:, 0:GT, :].rearrange("p q (h e) -> p (q h) e", e=HD),
                                ssum[u][:].rearrange("p q h -> p (q h)")[:, :, None].to_broadcast([P, GT * HEADS, HD]),
                                ALU.mult).then_inc(b_at, 1)
                        for u in both:
                            v.wait_ge(b_o, 1).then_inc(b_o, -1)
                            own(nc.vector.tensor_tensor(H[u][:], tiles_of(B[u]),
                                                        Xg[:, :, bass.ds(pair * 2 + u, 1), :].rearrange("p s o d -> p s (o d)"), ALU.add))
                            v.sem_inc(b_h, 1)
                            own(layernorm(v, lambda t: H[u][:, t, :], st[u], mv[u], rs[u], lambda t: z[u][:, t, :]))
                            v.sem_inc(b_z2, 1)
                            v.sem_inc(b_z, 1)
                        for u in both:
                            v.wait_ge(b_lg, 1).then_inc(b_lg, -1)
                            L = B[u][:, 0:GT * EXP].rearrange("p (t e) -> p t e", e=EXP)
                            own(nc.vector.tensor_reduce(lmax[u][:], L, AX, ALU.max))
                            own(nc.vector.tensor_tensor(lg[u][:], L, lmax[u][:, :, None].to_broadcast([P, GT, EXP]), ALU.subtract))
                            v.sem_inc(b_ls, 1)
                            v.sem_inc(b_bfree, 1)
                        for u in both:
                            v.wait_ge(b_le, 1).then_inc(b_le, -1)
                            own(nc.vector.tensor_reduce(lsum[u][:], lg[u][:], AX, ALU.add))
                            own(nc.vector.reciprocal(lsum[u][:], lsum[u][:]))
                            nc.vector.tensor_tensor(prob_g[:, :, bass.ds(pair * 2 + u, 1), :].rearrange("p s o e -> p s (o e)"),
                                                    lg[u][:], lsum[u][:, :, None].to_broadcast([P, GT, EXP]), ALU.mult)

                @block.tensor
                def _(pe):
                    def turn(dst, src, done):
                        for t in range(GT):
                            mm = nc.tensor.transpose(dst[:, t * P:(t + 1) * P], src[:, t, :], ident)
                        mm.then_inc(done, 1)

                    def project(dst, lhsT, rhs, n, done):
                        for t in range(GT):
                            mm = nc.tensor.matmul(dst[:, t * n:(t + 1) * n], lhsT[:, t * P:(t + 1) * P], rhs, start=True, stop=True)
                        mm.then_inc(done, 1)

                    with pe.Fori(0, GT // 2) as pair:
                        for u in both:
                            pe.wait_ge(b_z, 1).then_inc(b_z, -1)
                            turn(A[u], z[u], b_zT)
                        for u in both:
                            pe.wait_ge(b_zTs, 1).then_inc(b_zTs, -1)
                            pe.wait_ge(b_bfree, 1).then_inc(b_bfree, -1)
                            project(B[u], zT[u], w["gq"], P, b_q)
                            project(A[u], zT[u], w["gk"], P, b_k)
                            pe.wait_ge(b_qe, 1).then_inc(b_qe, -1)
                            project(B[u], zT[u], w["gv"], P, b_v)
                        for u in both:
                            pe.wait_ge(b_at, 1).then_inc(b_at, -1)
                            turn(A[u], att[u], b_aT)
                        for u in both:
                            pe.wait_ge(b_aTs, 1).then_inc(b_aTs, -1)
                            pe.wait_ge(b_ve, 1).then_inc(b_ve, -1)
                            project(B[u], zT[u], w["proj"], P, b_o)
                        for u in both:
                            pe.wait_ge(b_z, 1).then_inc(b_z, -1)
                            turn(A[u], z[u], b_zT2)
                        for u in both:
                            pe.wait_ge(b_zTs2, 1).then_inc(b_zTs2, -1)
                            project(B[u], zT[u], w["router"], EXP, b_lg)

        route_stack = ctx.enter_context(ExitStack())
        gates = sb("gates", [P, TILES, 2], stack=route_stack)
        to_row = sb("to_row", [P, TILES, 2], U32, route_stack)
        from_row = sb("from_row", [P, TILES, 2], U32, route_stack)
        PAST = float(1 << 20)
        with ExitStack() as ph:
            t3 = lambda name: sb("r_" + name, [P, TILES, EXP], F32, ph)
            eq, left, hot, marked, place, tmp = [t3(n) for n in ("eq", "left", "hot0", "marked", "place", "tmp")]
            hot2 = t3("hot1")
            carry = sb("r_carry", [P, EXP, TILES], F32, ph)
            totals = sb("r_totals", [P, EXP, TILES], F32, ph)
            run_on = sb("r_run_on", [P, EXP, TILES], F32, ph)
            ones = sb("r_ones", [P, P], F32, ph)
            pk, ik, fk, keep, rowf, wk = [sb("r_" + n, [P, 2, TILES], F32, ph) for n in ("pk", "ik", "fk", "keep", "rowf", "wk")]
            r_dve, r_marked, r_sums = sem("r_dve"), sem("r_marked"), sem("r_sums")
            iota = const[:, CONST["iota"]][:, None, :].to_broadcast([P, TILES, EXP])
            per_tile = lambda a: a[:, :, None].to_broadcast([P, TILES, EXP])
            flat = lambda a: a[:].rearrange("p a b -> p (a b)")

            with nc.Block() as block:
                @block.vector
                def _(v):
                    def own(ins):
                        ins.then_inc(r_dve, 1)
                        v.wait_ge(r_dve, 1).then_inc(r_dve, -1)

                    own(nc.vector.memset(ones[:], 1.0))
                    own(nc.vector.memset(totals[:], 0.0))
                    own(nc.vector.memset(run_on[:], 1.0))
                    own(nc.vector.memset(run_on[:, :, 0:1], 0.0))
                    for k, (p_in, oh) in enumerate(((prob, hot), (left, hot2))):
                        own(nc.vector.tensor_reduce(pk[:, k, :], p_in[:], AX, ALU.max))
                        own(nc.vector.tensor_tensor(eq[:], p_in[:], per_tile(pk[:, k, :]), ALU.is_equal))
                        own(nc.vector.scalar_tensor_tensor(out=tmp[:], in0=eq[:], scalar=-float(EXP), in1=iota, op0=ALU.mult, op1=ALU.add))
                        own(nc.vector.tensor_reduce(ik[:, k, :], tmp[:], AX, ALU.min))
                        own(nc.vector.tensor_scalar(ik[:, k, :], ik[:, k, :], float(EXP), None, ALU.add))
                        own(nc.vector.tensor_tensor(oh[:], iota, per_tile(ik[:, k, :]), ALU.is_equal))
                        if k == 0:
                            own(nc.vector.scalar_tensor_tensor(out=left[:], in0=hot[:], scalar=-4.0, in1=prob[:], op0=ALU.mult, op1=ALU.add))
                    own(nc.vector.tensor_tensor(marked[:], hot[:], hot2[:], ALU.add))
                    v.sem_inc(r_marked, 1)
                    v.wait_ge(r_sums, 1).then_inc(r_sums, -1)
                    own(nc.vector.tensor_copy(totals[:, :, 1:], PS[1][:, 0:1024].rearrange("p (t e) -> p e t", e=EXP)[:, :, 0:TILES - 1]))
                    own(nc.vector.tensor_tensor_scan(flat(carry), flat(run_on), flat(totals), 0.0, ALU.mult, ALU.add))
                    own(nc.vector.tensor_tensor(place[:], PS[0][:, 0:1024].rearrange("p (t e) -> p t e", e=EXP),
                                                carry[:].rearrange("p e t -> p t e"), ALU.add))
                    for k, oh in enumerate((hot, hot2)):
                        own(nc.vector.tensor_tensor(tmp[:], oh[:], place[:], ALU.mult))
                        own(nc.vector.tensor_reduce(fk[:, k, :], tmp[:], AX, ALU.add))
                    own(nc.vector.tensor_scalar(keep[:], fk[:], float(CAP), None, ALU.is_lt))
                    own(nc.vector.scalar_tensor_tensor(out=rowf[:], in0=ik[:], scalar=float(CAP), in1=fk[:], op0=ALU.mult, op1=ALU.add))
                    own(nc.vector.tensor_tensor(rowf[:], rowf[:], keep[:], ALU.mult))
                    own(nc.vector.tensor_copy(from_row[:].rearrange("p t k -> p k t"), rowf[:]))
                    own(nc.vector.tensor_tensor(gates[:].rearrange("p t k -> p k t"), pk[:], keep[:], ALU.mult))
                    own(nc.vector.tensor_scalar(wk[:], keep[:], -PAST, PAST, ALU.mult, ALU.add))
                    own(nc.vector.tensor_tensor(rowf[:], rowf[:], wk[:], ALU.add))
                    own(nc.vector.tensor_copy(to_row[:].rearrange("p t k -> p k t"), rowf[:]))

                @block.tensor
                def _(pe):
                    pe.wait_ge(r_marked, 1).then_inc(r_marked, -1)
                    for c in range(2):
                        half = flat(marked)[:, c * BANK:(c + 1) * BANK]
                        nc.tensor.matmul(PS[0][:, c * BANK:(c + 1) * BANK], const[:, CONST["before"]], half, start=True, stop=True)
                        mm = nc.tensor.matmul(PS[1][:, c * BANK:(c + 1) * BANK], ones[:], half, start=True, stop=True)
                    mm.then_inc(r_sums, 1)

        with ExitStack() as ph:
            def pb(name, shape, dt=F32):
                return [sb(f"d_{name}{u}", shape, dt, ph) for u in range(2)]
            row_at, rows_out = pb("row_at", [P, GT, 2], U32), pb("rows_out", [P, GT, D])
            d_ready, d_free, d_sent = sem("d_ready"), sem("d_free"), [sem("d_sent0"), sem("d_sent1")]
            with nc.Block() as block:
                @block.vector
                def _(v):
                    v.sem_inc(d_free, 2)
                    with v.Fori(0, SEQ // 2) as pair:
                        for u in range(2):
                            v.wait_ge(d_free, 1).then_inc(d_free, -1)
                            nc.vector.tensor_copy(row_at[u][:], to_row[:, bass.ds(pair * (2 * GT) + u * GT, GT), :]).then_inc(d_ready, 1)
                            nc.vector.tensor_copy(rows_out[u][:], Z2[:, bass.ds(pair * (2 * GT) + u * GT, GT), :]).then_inc(d_ready, 1)
                    v.wait_ge(d_free, 2).then_inc(d_free, -2)

                @block.gpsimd
                def _(g):
                    with g.Fori(0, SEQ // 2) as pair:
                        for u in range(2):
                            g.wait_ge(d_ready, 2).then_inc(d_ready, -2)
                            for t in range(GT):
                                for k in range(2):
                                    nc.gpsimd.indirect_dma_start(
                                        slot_rows, bass.IndirectOffsetOnAxis(ap=row_at[u][:, t, k:k + 1], axis=0),
                                        rows_out[u][:, t, :], None, bounds_check=SLOTS - 1, oob_is_err=False).then_inc(d_sent[u], 16)
                        for u in range(2):
                            g.wait_ge(d_sent[u], pair * (16 * 2 * GT) + 16 * 2 * GT)
                            g.sem_inc(d_free, 1)
        expert_w = {n: wa[:, WA[n]] for n in ("ln2w", "ln2b")}

        with ExitStack() as ph:
            def pb(name, shape, dt=F32):
                return [sb(f"e_{name}{u}", shape, dt, ph) for u in range(2)]
            we, xe, xeT = pb("we", [P, 4 * P]), pb("xe", [P, CT, D]), pb("xeT", [P, CAP])
            he, ye = pb("he", [P, 2, CAP]), pb("ye", [P, CT, D])
            e_w, e_x, e_y = [[sem(f"e_{n}{u}") for u in range(2)] for n in "wxy"]
            e_T, e_Ts, e_up, e_act, e_down, e_out, e_st, e_wfree, e_xfree, e_pf = [
                sem("e_" + n) for n in "T Ts up act down out st wfree xfree pf".split()]
            chunks = [(c, min(c + BANK, CAP)) for c in range(0, CAP, BANK)]
            S = [PS[u][:, 0:CAP] for u in range(2)]
            with nc.Block() as block:
                @block.sync
                def _(sp):
                    for u in range(2):
                        sp.sem_inc(e_y[u], 16)
                    with sp.Fori(0, EXP // 2) as pair:
                        for u in range(2):
                            sp.wait_ge(e_wfree, 1).then_inc(e_wfree, -1)
                            sp.dma_start(we[u][:], moe_in[bass.ds(pair * 2 + u, 1), :, :].rearrange("o p c -> p (o c)")).then_inc(e_w[u], 16)
                            sp.dma_start(xe[u][:].rearrange("p t d -> p (t d)"),
                                         slot_rows.rearrange("(e p t) d -> e p (t d)", p=P, t=CT)[bass.ds(pair * 2 + u, 1), :, :]
                                         .rearrange("o p c -> p (o c)")).then_inc(e_x[u], 16)
                        for u in range(2):
                            sp.wait_ge(e_st, 1).then_inc(e_st, -1)
                            sp.dma_start(slot_outs.rearrange("(e p t) d -> e p (t d)", p=P, t=CT)[bass.ds(pair * 2 + u, 1), :, :]
                                         .rearrange("o p c -> p (o c)"), ye[u][:].rearrange("p t d -> p (t d)")).then_inc(e_y[u], 16)
                    for u in range(2):
                        sp.wait_ge(e_y[u], 16)

                @block.scalar
                def _(s):
                    with s.Fori(0, EXP // 2) as pair:
                        for u in range(2):
                            s.wait_ge(e_T, 1).then_inc(e_T, -1)
                            nc.scalar.activation(xeT[u][:], S[u], ACT.Identity, bias=expert_w["ln2b"], scale=expert_w["ln2w"]).then_inc(e_Ts, 1)
                        for f in range(2):
                            for u in range(2):
                                s.wait_ge(e_up, 1).then_inc(e_up, -1)
                                nc.scalar.activation(he[u][:, f, :], S[u], ACT.Gelu_apprx_tanh).then_inc(e_act, 1)

                @block.vector
                def _(v):
                    v.sem_inc(e_wfree, 2)
                    v.sem_inc(e_pf, 2)
                    with v.Fori(0, EXP // 2) as pair:
                        for u in range(2):
                            v.wait_ge(e_down, 1).then_inc(e_down, -1)
                            v.wait_ge(e_y[u], 16).then_inc(e_y[u], -16)
                            nc.vector.tensor_copy(ye[u][:].rearrange("p t d -> p (t d)"), S[u]).then_inc(e_out, 1)
                            v.wait_ge(e_out, 1).then_inc(e_out, -1)
                            v.sem_inc(e_st, 1)
                            v.sem_inc(e_wfree, 1)
                            v.sem_inc(e_pf, 1)

                @block.tensor
                def _(pe):
                    with pe.Fori(0, EXP // 2) as pair:
                        for u in range(2):
                            pe.wait_ge(e_x[u], 16).then_inc(e_x[u], -16)
                            pe.wait_ge(e_pf, 1).then_inc(e_pf, -1)
                            for t in range(CT):
                                mm = nc.tensor.transpose(S[u][:, t * P:(t + 1) * P], xe[u][:, t, :], ident)
                            mm.then_inc(e_T, 1)
                        for f in range(2):
                            for u in range(2):
                                if f == 0:
                                    pe.wait_ge(e_w[u], 16).then_inc(e_w[u], -16)
                                    pe.wait_ge(e_Ts, 1).then_inc(e_Ts, -1)
                                else:
                                    pe.wait_ge(e_act, 1).then_inc(e_act, -1)
                                for a, b in chunks:
                                    mm = nc.tensor.matmul(S[u][:, a:b], we[u][:, f * P:(f + 1) * P], xeT[u][:, a:b], start=True, stop=True)
                                mm.then_inc(e_up, 1)
                        for u in range(2):
                            pe.wait_ge(e_act, 1).then_inc(e_act, -1)
                            for t in range(CT):
                                for f in range(2):
                                    mm = nc.tensor.matmul(S[u][:, t * P:(t + 1) * P], he[u][:, f, t * P:(t + 1) * P],
                                                          we[u][:, (2 + f) * P:(3 + f) * P], start=f == 0, stop=f == 1)
                            mm.then_inc(e_down, 1)

        with ExitStack() as ph:
            def pb(name, shape, dt=F32):
                return [sb(f"c_{name}{u}", shape, dt, ph) for u in range(2)]
            row_at, gt, got = pb("row_at", [P, GT, 2], U32), pb("gt", [P, GT, 2]), pb("got", [P, GT, 2, D])
            y = pb("y", [P, GT, D])
            st, mv, ve, rs = pb("st", [P, GT, 6]), pb("mv", [P, GT, 2]), pb("ve", [P, GT]), pb("rs", [P, GT])
            c_at, c_got, c_dve = sem("c_at"), [sem("c_got0"), sem("c_got1")], sem("c_dve")
            c_x, c_stored = sem("c_x"), sem("c_stored")
            with nc.Block() as block:
                @block.sync
                def _(sp):
                    with sp.Fori(0, SEQ) as b:
                        sp.wait_ge(c_x, 1).then_inc(c_x, -1)
                        sp.dma_start(x_mid[:, bass.ds(b * GT, GT), :], X[:, bass.ds(b * GT, GT), :]).then_inc(c_stored, 16)
                    sp.wait_ge(c_stored, 16 * SEQ)

                @block.vector
                def _(v):
                    def own(ins):
                        ins.then_inc(c_dve, 1)
                        v.wait_ge(c_dve, 1).then_inc(c_dve, -1)

                    def ask(group, u):
                        nc.vector.tensor_copy(gt[u][:], gates[:, bass.ds(group * GT, GT), :])
                        nc.vector.tensor_copy(row_at[u][:], from_row[:, bass.ds(group * GT, GT), :]).then_inc(c_at, 1)

                    with v.Fori(0, SEQ // 2) as pair:
                        for u in range(2):
                            ask(pair * 2 + u, u)
                        for u in range(2):
                            v.wait_ge(c_got[u], pair * (16 * 2 * GT) + 16 * 2 * GT)
                            for t in range(GT):
                                last = nc.vector.scalar_tensor_tensor(
                                    out=y[u][:, t, :], in0=got[u][:, t, 0, :], scalar=gt[u][:, t, 0:1],
                                    in1=X[:, bass.ds((pair * 2 + u) * GT + t, 1), :].rearrange("p o d -> p (o d)"), op0=ALU.mult, op1=ALU.add)
                            own(last)
                            for t in range(GT):
                                last = nc.vector.scalar_tensor_tensor(
                                    out=y[u][:, t, :], in0=got[u][:, t, 1, :], scalar=gt[u][:, t, 1:2],
                                    in1=y[u][:, t, :], op0=ALU.mult, op1=ALU.add)
                            own(last)
                            own(layernorm(v, lambda t: y[u][:, t, :], st[u], mv[u], rs[u],
                                          lambda t: X[:, bass.ds((pair * 2 + u) * GT + t, 1), :].rearrange("p o d -> p (o d)")))
                            v.sem_inc(c_x, 1)

                @block.gpsimd
                def _(g):
                    with g.Fori(0, SEQ // 2) as pair:
                        for u in range(2):
                            g.wait_ge(c_at, 1).then_inc(c_at, -1)
                            for t in range(GT):
                                for k in range(2):
                                    nc.gpsimd.indirect_dma_start(
                                        got[u][:, t, k, :], None, slot_outs,
                                        bass.IndirectOffsetOnAxis(ap=row_at[u][:, t, k:k + 1], axis=0)).then_inc(c_got[u], 16)
                        for u in range(2):
                            inverse_root(g, mv[u], ve[u], rs[u])

        route_stack.close()
        moe_stack.close()
        wa_stack.close()
        x_stack.close()
        with ExitStack() as ph:
            def pb(name, shape, dt=F32):
                return sb("m_" + name, shape, dt, ph)

            FT, MB = 4, HID // P
            wm, wf, sel = pb("wm", [P, WM_W]), pb("wf", [P, WF_W]), pb("sel", [96, 32], BF16)
            m = {n: wm[:, c] for n, c in WM.items()}
            f = {n: wf[:, c] for n, c in WF.items()}
            w_xp = m["xp"].rearrange("p (k o) -> p k o", k=2)
            w_dt = m["dt"].rearrange("p (k o) -> p k o", k=2)
            w_out = m["out"].rearrange("p (k o) -> p k o", k=2)
            taps = m["cw"].rearrange("p (k o) -> p k o", k=2)
            w3 = f["w3"].rearrange("p (k d) -> p k d", d=D)
            rate = pb("rate", [P, 2 * NS])
            delta, dx, gate = [[pb(f"{n}{q}", [P, 2, GN]) for q in range(2)] for n in ("delta", "dx", "gate")]
            bc = [pb(f"bc{q}", [96, GN], BF16) for q in range(2)]
            dA, dBx, Cs = [[pb(f"{n}{q}", s) for q in range(2)] for n, s in (("dA", [P, 2, GN]), ("dBx", [P, 2, GN]), ("Cs", [P, GN]))]
            h, ch, acc = pb("h", [P, 2, GN]), pb("ch", [P, 2, GN]), pb("acc", [P, 2, GN])
            x_st, xT, uu = pb("x_st", [P, GT, D]), pb("xT", [P, GN]), pb("uu", [P, 2, GN])
            xi = pb("xi", [P, 2, GN + TAPS])
            low = xi[:, :, TAPS:]
            xf, fT, ha, hb = pb("xf", [P, GT, D]), pb("fT", [P, FT * P]), pb("ha", [P, MB, FT * P]), pb("hb", [P, MB, FT * P])
            yo = [pb(f"yo{c}", [P, FT, D]) for c in range(2)]
            st, mv, ve, rs = pb("st", [P, GT, 6]), pb("mv", [P, GT, 2]), pb("ve", [P, GT]), pb("rs", [P, GT])
            st4, mv4, ve4, rs4 = pb("st4", [P, FT, 6]), pb("mv4", [P, FT, 2]), pb("ve4", [P, FT]), pb("rs4", [P, FT])

            def sems(prefix, names):
                return [sem(prefix + n) for n in names.split()]

            m_wm, m_wf, m_const, m_rate = sems("m_", "wm wf const rate")
            s_B, s_C, s_Bfree, s_Cfree, s_dA, s_dAfree, s_Cs, s_Csfree, s_h, s_hfree, s_ch, s_chfree, s_acc, s_start = sems(
                "s_", "B C Bfree Cfree dA dAfree Cs Csfree h hfree ch chfree acc start")
            (p_x, p_xfree, p_T, p_xT, p_xi, p_xip, p_xiv, p_z, p_zs, p_cv, p_u, p_dr, p_drs, p_dt, p_abs, p_relu, p_bc,
             p_left, p_bcfree, p_split, p_parts, p_ln, p_delta) = sems(
                 "p_", "x xfree T xT xi xip xiv z zs cv u dr drs dt abs relu bc left bcfree split parts ln delta")
            (o_gy, o_y, o_x, o_xf, o_xfree, f_T, f_xT, f_a, f_s, f_b, f_h, f_c, f_g, f_o, f_yfree, f_yo0, f_yo1,
             f_out0, f_out1) = sems("f_", "gy y x xf xfree T xT a s b h c g o yfree yo0 yo1 out0 out1")
            f_yo, f_out = (f_yo0, f_yo1), (f_out0, f_out1)
            v_own, a_own, g_own = sems("own_", "v a g")
            Bp, Cp, W = PS[0][:, 0:GN], PS[0][:, GN:2 * GN], PS[1]
            bank = lambda k: W[:, k * BANK:(k + 1) * BANK]
            two = lambda t: t.rearrange("p (h t) -> p h t", h=2)

            SLICES = [(7, "h1", "t1", (0,)), (8, "h1", "t1", (1, 2)), (9, "h1", "t1", (3,)), (9, "h2", "t2", (0,)),
                      (10, "h2", "t2", (1, 2)), (11, "h2", "t2", (3,)), (13, "h1", "t1", (0, 1)), (14, "h1", "t1", (2, 3)),
                      (15, "h2", "t2", (0, 1)), (16, "h2", "t2", (2, 3))]

            def bodies(eng, prologue, body, tail):
                prologue()
                body(0, 0, True, False)
                with eng.Fori(0, SEQ // 2 - 1) as i:
                    body(i * 2 + 1, 1, True, True)
                    body(i * 2 + 2, 0, True, True)
                body(SEQ - 1, 1, False, True)
                tail()

            with nc.Block() as block:
                @block.sync
                def _(sp):
                    def group(b):
                        return slice(b * GT, (b + 1) * GT) if isinstance(b, int) else bass.ds(b * GT, GT)

                    def load_x(b):
                        sp.wait_ge(p_xfree, 1).then_inc(p_xfree, -1)
                        sp.dma_start(x_st[:], x_mid[:, group(b), :]).then_inc(p_x, 16)

                    def load_residual(b):
                        sp.wait_ge(o_xfree, 1).then_inc(o_xfree, -1)
                        sp.dma_start(xf[:], x_mid[:, group(b), :]).then_inc(o_xf, 16)

                    def store(b, c):
                        sp.wait_ge(f_yo[c], 1).then_inc(f_yo[c], -1)
                        at = slice(b * GT + c * FT, b * GT + (c + 1) * FT) if isinstance(b, int) else bass.ds(b * GT + c * FT, FT)
                        sp.dma_start(out_tiles[:, at, :], yo[c][:]).then_inc(f_out[c], 16)

                    def prologue():
                        sp.dma_start(wm[:], wm_in).then_inc(m_wm, 16)
                        load_x(0)
                        sp.dma_start(wf[:], wf_in).then_inc(m_wf, 16)

                    def body(b, p, prep, mlp):
                        if prep:
                            load_x(b + 1)
                        if mlp:
                            load_residual(b - 1)
                            store(b - 1, 0)
                            store(b - 1, 1)

                    def tail():
                        load_residual(SEQ - 1)
                        store(SEQ - 1, 0)
                        store(SEQ - 1, 1)
                        sp.wait_ge(f_out[0], 16)
                        sp.wait_ge(f_out[1], 16)

                    bodies(sp, prologue, body, tail)

                @block.scalar
                def _(s):
                    def own(ins):
                        ins.then_inc(a_own, 1)
                        s.wait_ge(a_own, 1).then_inc(a_own, -1)

                    def scan_inputs(n, p):
                        s.wait_ge(s_dAfree, 1).then_inc(s_dAfree, -1)
                        for k in range(2):
                            nc.scalar.activation(dA[n % 2][:, k, :], delta[p][:, k, :], ACT.Exp,
                                                 scale=rate[:, k * NS + n:k * NS + n + 1]).then_inc(s_dA, 1)
                        s.wait_ge(s_C, 1).then_inc(s_C, -1)
                        s.wait_ge(s_Csfree, 1).then_inc(s_Csfree, -1)
                        own(nc.scalar.copy(Cs[n % 2][:], Cp))
                        s.sem_inc(s_Cfree, 1)
                        s.sem_inc(s_Cs, 1)

                    def prepare(step, q):
                        if step == 0:
                            s.wait_ge(p_T, 1).then_inc(p_T, -1)
                            s.sem_inc(p_xfree, 1)
                            nc.scalar.copy(xT[:], W[:, 0:GN]).then_inc(p_xT, 1)
                            s.wait_ge(p_xi, 1).then_inc(p_xi, -1)
                            own(nc.scalar.copy(xi[:, :, TAPS - 1:TAPS - 1 + GN], two(W[:])))
                            s.sem_inc(p_xip, 1)
                            s.sem_inc(p_xiv, 1)
                        if step == 2:
                            s.wait_ge(p_z, 1).then_inc(p_z, -1)
                            nc.scalar.activation(gate[q][:], two(W[:]), ACT.Silu).then_inc(p_zs, 1)
                        if step == 3:
                            s.wait_ge(p_cv, 1).then_inc(p_cv, -1)
                            for k in range(2):
                                last = nc.scalar.activation(uu[:, k, :], uu[:, k, :], ACT.Silu, bias=m["cb"][:, k:k + 1])
                            last.then_inc(p_u, 1)
                        if step == 4:
                            s.wait_ge(p_dr, 1).then_inc(p_dr, -1)
                            nc.scalar.copy(low, two(W[:])).then_inc(p_drs, 1)
                        if step == 5:
                            s.wait_ge(p_dt, 1).then_inc(p_dt, -1)
                            for k in range(2):
                                last = nc.scalar.activation(low[:, k, :], two(W[:])[:, k, :], ACT.Abs, bias=m["dtb"][:, k:k + 1])
                            own(last)
                            s.sem_inc(p_abs, 1)
                            own(nc.scalar.activation(low, low, ACT.Exp, scale=-1.0))
                        if step == 6:
                            s.wait_ge(p_bc, 1).then_inc(p_bc, -1)
                            own(nc.scalar.copy(dx[q][0:96, 0, :], W[0:96, GN:2 * GN]))
                            s.sem_inc(p_left, 1)
                            s.sem_inc(p_bcfree, 1)
                        if step == 8:
                            s.wait_ge(p_split, 1).then_inc(p_split, -1)
                            nc.scalar.activation(dx[q][:], low, ACT.Ln, bias=1.0).then_inc(p_ln, 1)

                    def mlp_turn():
                        s.wait_ge(f_T, 1).then_inc(f_T, -1)
                        nc.scalar.copy(fT[:], bank(0)).then_inc(f_xT, 1)

                    def mlp_silu():
                        for k in range(MB):
                            s.wait_ge(f_a, 1).then_inc(f_a, -1)
                            nc.scalar.activation(ha[:, k, :], bank(k), ACT.Silu, scale=f["s1"][:, k:k + 1]).then_inc(f_s, 1)

                    def mlp_gelu(dst, scale, blocks):
                        for k in blocks:
                            s.wait_ge(f_c, 1).then_inc(f_c, -1)
                            nc.scalar.activation(dst[:, k, :], bank(k), ACT.Gelu, scale=f[scale][:, k:k + 1]).then_inc(f_g, 1)

                    def mlp_step(step):
                        if step in (6, 12):
                            mlp_turn()
                            mlp_silu()
                        for at, layer, scale, blocks in SLICES:
                            if at == step:
                                mlp_gelu(ha if layer == "h1" else hb, scale, blocks)

                    def prologue():
                        s.wait_ge(m_wm, 16)
                        own(nc.scalar.activation(rate[:], m["alog"], ACT.Exp))
                        own(nc.scalar.mul(rate[:], rate[:], -1.0))
                        for step in range(NS):
                            prepare(step, 0)
                        s.wait_ge(p_delta, 1).then_inc(p_delta, -1)
                        scan_inputs(0, 0)
                        s.wait_ge(m_wf, 16)

                    def body(b, p, prep, mlp):
                        for n in range(NS):
                            if n < NS - 1:
                                scan_inputs(n + 1, p)
                            if prep:
                                prepare(n, 1 - p)
                            if mlp:
                                mlp_step(n)
                        if prep:
                            s.wait_ge(p_delta, 1).then_inc(p_delta, -1)
                            scan_inputs(0, 1 - p)
                        if mlp:
                            mlp_step(NS)

                    def tail():
                        for n in range(NS + 1):
                            mlp_step(n)

                    bodies(s, prologue, body, tail)

                @block.vector
                def _(v):
                    def own(ins):
                        ins.then_inc(v_own, 1)
                        v.wait_ge(v_own, 1).then_inc(v_own, -1)

                    def scan_products(n, p):
                        v.wait_ge(s_B, 1).then_inc(s_B, -1)
                        for k in range(2):
                            nc.vector.tensor_tensor(dBx[n % 2][:, k, :], Bp, dx[p][:, k, :], ALU.mult).then_inc(v_own, 1)
                        v.wait_ge(v_own, 2).then_inc(v_own, -2)
                        v.sem_inc(s_Bfree, 1)

                    def add_product():
                        v.wait_ge(s_ch, 1).then_inc(s_ch, -1)
                        own(nc.vector.tensor_tensor(acc[:, 0, :], acc[:, 0, :], ch[:, 0, :], ALU.add))
                        v.sem_inc(s_chfree, 1)

                    def scan_states(n):
                        for k in range(2):
                            v.wait_ge(s_dA, 1).then_inc(s_dA, -1)
                            v.wait_ge(s_hfree, 1).then_inc(s_hfree, -1)
                            nc.vector.tensor_tensor_scan(h[:, k, :], dA[n % 2][:, k, :], dBx[n % 2][:, k, :], 0.0, ALU.mult, ALU.add).then_inc(s_h, 1)

                    def gate_output(p):
                        add_product()
                        v.wait_ge(s_acc, 1).then_inc(s_acc, -1)
                        own(nc.vector.tensor_tensor(gate[p][:], acc[:], gate[p][:], ALU.mult))
                        v.sem_inc(o_gy, 1)

                    def start_sum():
                        for k in range(2):
                            last = nc.vector.tensor_scalar(acc[:, k, :], uu[:, k, :], m["dpar"][:, k:k + 1], None, ALU.mult)
                        own(last)
                        v.sem_inc(s_start, 1)

                    def output_moments():
                        v.wait_ge(o_y, 1).then_inc(o_y, -1)
                        v.wait_ge(o_xf, 16).then_inc(o_xf, -16)
                        own(nc.vector.tensor_tensor(xf[:], tiles_of(W[:, 0:GN]), xf[:], ALU.add))
                        v.sem_inc(f_yfree, 1)
                        moments(v, lambda t: xf[:, t, :], st, mv)

                    def output_norm():
                        own(normalise(v, lambda t: xf[:, t, :], mv, rs, lambda t: xf[:, t, :]))
                        v.sem_inc(o_x, 1)

                    def prepare(step, q):
                        if step in (1, 2):
                            k = step - 1
                            if k == 0:
                                v.wait_ge(p_xiv, 1).then_inc(p_xiv, -1)
                            own(nc.vector.tensor_scalar(uu[:, k, :], xi[:, k, 0:GN], taps[:, k, 0:1], None, ALU.mult))
                            for j in range(1, TAPS):
                                own(nc.vector.scalar_tensor_tensor(out=uu[:, k, :], in0=xi[:, k, j:j + GN], scalar=taps[:, k, j:j + 1],
                                                                   in1=uu[:, k, :], op0=ALU.mult, op1=ALU.add))
                            if k == 1:
                                v.sem_inc(p_cv, 1)
                        if step == 6:
                            v.wait_ge(p_abs, 1).then_inc(p_abs, -1)
                            for k in range(2):
                                last = nc.vector.tensor_scalar(delta[q][:, k, :], two(W[:])[:, k, :], m["dtb"][:, k:k + 1], 0.0, ALU.add, ALU.max)
                            own(last)
                            v.sem_inc(p_relu, 1)
                        if step == 7:
                            v.wait_ge(p_left, 1).then_inc(p_left, -1)
                            left = dx[q][0:96, 0, :]
                            own(nc.vector.tensor_copy(bc[q][:], left))
                            own(nc.vector.tensor_tensor(left, left, bc[q][:], ALU.subtract))
                            own(nc.vector.tensor_copy(bc[q][32:64, :], left[32:64, :]))
                            own(nc.vector.tensor_copy(bc[q][64:96, :], left[64:96, :]))
                            own(nc.vector.tensor_tensor(left[64:96, :], left[64:96, :], bc[q][64:96, :], ALU.subtract))
                            own(nc.vector.tensor_copy(bc[q][64:96, :], left[64:96, :]))
                            v.sem_inc(p_split, 1)
                            v.sem_inc(p_parts, 1)
                        if step == 9:
                            v.wait_ge(p_ln, 1).then_inc(p_ln, -1)
                            own(nc.vector.tensor_tensor(delta[q][:], delta[q][:], dx[q][:], ALU.add))
                        if step == 10:
                            own(nc.vector.tensor_scalar(dx[q][:], low, 1.0, 1.0, ALU.add, ALU.subtract))
                            own(nc.vector.tensor_tensor(dx[q][:], low, dx[q][:], ALU.subtract))
                        if step == 12:
                            own(nc.vector.tensor_tensor(delta[q][:], delta[q][:], dx[q][:], ALU.add))
                            v.sem_inc(p_delta, 1)
                        if step == 13:
                            own(nc.vector.tensor_tensor(dx[q][:], delta[q][:], uu[:], ALU.mult))

                    def mlp_gated():
                        for k in range(MB):
                            v.wait_ge(f_b, 1).then_inc(f_b, -1)
                            nc.vector.scalar_tensor_tensor(out=hb[:, k, :], in0=bank(k), scalar=f["s2"][:, k:k + 1],
                                                           in1=ha[:, k, :], op0=ALU.mult, op1=ALU.mult).then_inc(f_h, 1)

                    def mlp_output(c):
                        v.wait_ge(f_o, 1).then_inc(f_o, -1)
                        v.wait_ge(f_out[c], 16).then_inc(f_out[c], -16)
                        own(nc.vector.tensor_tensor(yo[c][:], tiles_of(bank(0)), xf[:, c * FT:(c + 1) * FT, :], ALU.add))
                        v.sem_inc(f_yfree, 1)
                        if c == 1:
                            v.sem_inc(o_xfree, 1)
                        moments(v, lambda t: yo[c][:, t, :], st4, mv4, FT)

                    def mlp_norm(c):
                        own(normalise(v, lambda t: yo[c][:, t, :], mv4, rs4, lambda t: yo[c][:, t, :], FT))
                        v.sem_inc(f_yo[c], 1)

                    def mlp_before(n):
                        if n == 13:
                            mlp_gated()
                        if n == 12:
                            mlp_output(0)

                    def mlp_after(n):
                        if n == 1:
                            output_moments()
                        if n == 2:
                            output_norm()
                        if n == 7:
                            mlp_gated()
                        if n == 13:
                            mlp_norm(0)

                    def mlp_end():
                        mlp_output(1)
                        mlp_norm(1)

                    def prologue():
                        v.wait_ge(m_wm, 16)
                        own(nc.vector.tensor_copy(sel[:], const[0:96, CONST["part"]]))
                        v.sem_inc(m_const, 1)
                        own(nc.vector.memset(xi[:], 0.0))
                        v.sem_inc(p_xfree, 1)
                        v.sem_inc(o_xfree, 1)
                        v.sem_inc(f_yfree, 1)
                        for c in range(2):
                            v.sem_inc(f_out[c], 16)
                        for step in range(NS):
                            prepare(step, 0)
                        v.wait_ge(m_wf, 16)
                        own(nc.vector.tensor_tensor(w3, w3, f["s3"][:, None, :].to_broadcast([P, MB, D]), ALU.mult))
                        v.sem_inc(m_rate, 1)

                    def body(b, p, prep, mlp):
                        for n in range(NS):
                            scan_products(n, p)
                            if n:
                                add_product()
                            if mlp:
                                mlp_before(n)
                            scan_states(n)
                            if n == 0:
                                if mlp:
                                    gate_output(1 - p)
                                start_sum()
                            if prep:
                                prepare(n, 1 - p)
                            if mlp:
                                mlp_after(n)
                        if mlp:
                            mlp_end()

                    def tail():
                        gate_output(1)
                        for n in range(NS):
                            mlp_before(n)
                            mlp_after(n)
                        mlp_end()

                    bodies(v, prologue, body, tail)

                @block.gpsimd
                def _(g):
                    def own(ins):
                        ins.then_inc(g_own, 1)
                        g.wait_ge(g_own, 1).then_inc(g_own, -1)

                    def prologue():
                        g.sem_inc(s_dAfree, 2)
                        g.sem_inc(s_Csfree, 2)
                        g.sem_inc(s_hfree, 2)
                        g.sem_inc(s_chfree, 1)

                    def mlp_step(n):
                        if n == 1:
                            inverse_root(g, mv, ve, rs)
                        if n == 12:
                            inverse_root(g, mv4, ve4, rs4, FT)

                    def mlp_end():
                        inverse_root(g, mv4, ve4, rs4, FT)

                    def body(b, p, prep, mlp):
                        for n in range(NS):
                            g.wait_ge(s_Cs, 1).then_inc(s_Cs, -1)
                            g.wait_ge(s_h, 1).then_inc(s_h, -1)
                            g.wait_ge(s_chfree, 1).then_inc(s_chfree, -1)
                            own(nc.gpsimd.tensor_tensor(ch[:, 0, :], h[:, 0, :], Cs[n % 2][:], ALU.mult))
                            g.sem_inc(s_ch, 1)
                            g.sem_inc(s_hfree, 1)
                            g.wait_ge(s_h, 1).then_inc(s_h, -1)
                            own(nc.gpsimd.tensor_tensor(ch[:, 1, :], h[:, 1, :], Cs[n % 2][:], ALU.mult))
                            g.sem_inc(s_hfree, 1)
                            g.sem_inc(s_dAfree, 1)
                            g.sem_inc(s_Csfree, 1)
                            if n == 0:
                                g.wait_ge(s_start, 1).then_inc(s_start, -1)
                            own(nc.gpsimd.tensor_tensor(acc[:, 1, :], acc[:, 1, :], ch[:, 1, :], ALU.add))
                            if n == NS - 1:
                                g.sem_inc(s_acc, 1)
                            if mlp:
                                mlp_step(n)
                        if mlp:
                            mlp_end()

                    def tail():
                        for n in range(NS):
                            mlp_step(n)
                        mlp_end()

                    bodies(g, prologue, body, tail)

                @block.tensor
                def _(pe):
                    def row_to_all(r, q, dst, done):
                        for c in range(2):
                            mm = nc.tensor.matmul(dst[:, c * BANK:(c + 1) * BANK], sel[0:96, r:r + 1].to_broadcast([96, P]),
                                                  bc[q][:, c * BANK:(c + 1) * BANK], start=True, stop=True)
                        mm.then_inc(done, 1)

                    def into_halves(weights, rhs, done):
                        ks = len(rhs)
                        for o in range(2):
                            for c in range(2):
                                for k in range(ks):
                                    mm = nc.tensor.matmul(bank(2 * o + c), weights(k, o), rhs[k][:, c * BANK:(c + 1) * BANK],
                                                          start=k == 0, stop=k == ks - 1)
                        mm.then_inc(done, 1)

                    def prepare(step, q, mlp):
                        if step == 0:
                            pe.wait_ge(p_x, 16).then_inc(p_x, -16)
                            pe.wait_ge(f_yfree, 1).then_inc(f_yfree, -1)
                            for t in range(GT):
                                mm = nc.tensor.transpose(W[:, t * P:(t + 1) * P], x_st[:, t, :], ident)
                            mm.then_inc(p_T, 1)
                            pe.wait_ge(p_xT, 1).then_inc(p_xT, -1)
                            into_halves(lambda k, o: m["in"][:, o * P:(o + 1) * P], [xT[:]], p_xi)
                        if step == 2:
                            if mlp:
                                pe.wait_ge(f_yfree, 1).then_inc(f_yfree, -1)
                            else:
                                pe.wait_ge(p_xip, 1).then_inc(p_xip, -1)
                            into_halves(lambda k, o: m["in"][:, (2 + o) * P:(3 + o) * P], [xT[:]], p_z)
                        if step == 4:
                            pe.wait_ge(p_u, 1).then_inc(p_u, -1)
                            pe.wait_ge(p_zs, 1).then_inc(p_zs, -1)
                            into_halves(lambda k, o: w_xp[:, k, o * P:(o + 1) * P], [uu[:, 0, :], uu[:, 1, :]], p_dr)
                        if step == 5:
                            pe.wait_ge(p_drs, 1).then_inc(p_drs, -1)
                            into_halves(lambda k, o: w_dt[:, k, o * P:(o + 1) * P], [low[:, 0, :], low[:, 1, :]], p_dt)
                        if step == 6:
                            pe.wait_ge(p_relu, 1).then_inc(p_relu, -1)
                            for c in range(2):
                                for k in range(2):
                                    mm = nc.tensor.matmul(W[0:96, GN + c * BANK:GN + (c + 1) * BANK], w_xp[:, k, DI:DI + 96],
                                                          uu[:, k, c * BANK:(c + 1) * BANK], start=k == 0, stop=k == 1)
                            mm.then_inc(p_bc, 1)
                        if step == 7 and not mlp:
                            pe.wait_ge(p_bcfree, 1).then_inc(p_bcfree, -1)

                    def output(p, prep):
                        pe.wait_ge(o_gy, 1).then_inc(o_gy, -1)
                        if prep:
                            pe.wait_ge(p_xip, 1).then_inc(p_xip, -1)
                        else:
                            pe.wait_ge(f_yfree, 1).then_inc(f_yfree, -1)
                        for t in range(GT):
                            for k in range(2):
                                mm = nc.tensor.matmul(W[:, t * P:(t + 1) * P], gate[p][:, k, t * P:(t + 1) * P], w_out[:, k, :],
                                                      start=k == 0, stop=k == 1)
                        mm.then_inc(o_y, 1)

                    def mlp_in(c, prep):
                        if c == 0:
                            pe.wait_ge(o_x, 1).then_inc(o_x, -1)
                        if c == 1 or not prep:
                            pe.wait_ge(f_yfree, 1).then_inc(f_yfree, -1)
                        for t in range(FT):
                            mm = nc.tensor.transpose(W[:, t * P:(t + 1) * P], xf[:, c * FT + t, :], ident)
                        mm.then_inc(f_T, 1)
                        pe.wait_ge(f_xT, 1).then_inc(f_xT, -1)
                        for k in range(MB):
                            if k == 2 and c == 0 and prep:
                                pe.wait_ge(p_bcfree, 1).then_inc(p_bcfree, -1)
                            nc.tensor.matmul(bank(k), f["w1"][:, k * P:(k + 1) * P], fT[:], start=True, stop=True).then_inc(f_a, 1)

                    def mlp_in2():
                        for k in range(MB):
                            pe.wait_ge(f_s, 1).then_inc(f_s, -1)
                            nc.tensor.matmul(bank(k), f["w2"][:, k * P:(k + 1) * P], fT[:], start=True, stop=True).then_inc(f_b, 1)

                    def mlp_hidden(layer, blocks):
                        src, ready = (hb, f_h) if layer == "h1" else (ha, f_g)
                        for o in blocks:
                            for k in range(MB):
                                if o == 0:
                                    pe.wait_ge(ready, 1).then_inc(ready, -1)
                                mm = nc.tensor.matmul(bank(o), f[layer][:, k * HID + o * P:k * HID + (o + 1) * P], src[:, k, :],
                                                      start=k == 0, stop=k == MB - 1)
                            mm.then_inc(f_c, 1)

                    def mlp_out():
                        pe.wait_ge(f_g, MB).then_inc(f_g, -MB)
                        for t in range(FT):
                            for k in range(MB):
                                mm = nc.tensor.matmul(W[:, t * P:(t + 1) * P], hb[:, k, t * P:(t + 1) * P], w3[:, k, :],
                                                      start=k == 0, stop=k == MB - 1)
                        mm.then_inc(f_o, 1)

                    def mlp_step(n, p, prep):
                        if n == 1:
                            output(p, prep)
                        if n == 6:
                            mlp_in(0, prep)
                        if n == 7:
                            mlp_in2()
                        if n == 12:
                            mlp_in(1, prep)
                            mlp_in2()
                        for at, layer, scale, blocks in SLICES:
                            if at == n:
                                mlp_hidden(layer, blocks)
                        if n in (11, NS):
                            mlp_out()

                    def prologue():
                        pe.wait_ge(m_wm, 16)
                        pe.wait_ge(m_const, 1)
                        for step in range(NS):
                            prepare(step, 0, False)
                        pe.wait_ge(p_parts, 1).then_inc(p_parts, -1)
                        row_to_all(0, 0, Bp, s_B)
                        row_to_all(NS, 0, Cp, s_C)
                        pe.wait_ge(m_wf, 16)
                        pe.wait_ge(m_rate, 1)
                        pe.sem_inc(f_yfree, 1)

                    def body(b, p, prep, mlp):
                        for n in range(NS):
                            pe.wait_ge(s_Bfree, 1).then_inc(s_Bfree, -1)
                            if n < NS - 1:
                                row_to_all(n + 1, p, Bp, s_B)
                            elif prep:
                                pe.wait_ge(p_parts, 1).then_inc(p_parts, -1)
                                row_to_all(0, 1 - p, Bp, s_B)
                            pe.wait_ge(s_Cfree, 1).then_inc(s_Cfree, -1)
                            if n < NS - 1:
                                row_to_all(n + 1 + NS, p, Cp, s_C)
                            elif prep:
                                row_to_all(NS, 1 - p, Cp, s_C)
                            if prep:
                                prepare(n, 1 - p, mlp)
                            if mlp:
                                mlp_step(n, 1 - p, prep)
                        if not mlp:
                            pe.sem_inc(f_yfree, 1)
                        else:
                            mlp_step(NS, 1 - p, prep)

                    def tail():
                        for n in range(NS + 1):
                            mlp_step(n, 1, False)

                    bodies(pe, prologue, body, tail)


def _packed(i):
    T = np.transpose
    col = lambda a: np.reshape(a, (-1, P)).T
    rows = lambda a: np.broadcast_to(np.reshape(a, (1, -1)), (P, np.size(a)))
    halves = lambda m: np.concatenate([m[k:k + P] for k in range(0, m.shape[0], P)], 1)
    qkv = i["L0_ffn_qkv_weight"]
    spread = lambda m: np.repeat(m.reshape(4, 1, HD, D), 4, 1).reshape(P, D)
    wa = np.concatenate([T(i["L0_attn_W_q"]), T(i["L0_attn_W_k"]), T(i["L0_attn_W_v"]), T(i["L0_attn_W_o"]),
                         T(qkv[0:128]), T(spread(qkv[128:160])), T(spread(qkv[160:192])), T(i["L0_ffn_proj_weight"]),
                         T(i["L0_ffn_router_weight"]), col(i["L0_attn_b_q"]), col(i["L0_ffn_ln1_weight"]),
                         col(i["L0_ffn_ln1_bias"]), col(i["L0_ffn_ln2_weight"]), col(i["L0_ffn_ln2_bias"]),
                         rows(i["L0_attn_b_k"]), rows(i["L0_attn_b_v"]), rows(i["L0_attn_b_o"])], 1)
    w1, w2 = i["L0_ffn_moe_w1"], i["L0_ffn_moe_w2"]
    moe = np.concatenate([T(w1, (0, 2, 1)), T(w2[:, :, 0:P], (0, 2, 1)), T(w2[:, :, P:], (0, 2, 1))], 2)
    xp = T(i["L1_attn_x_proj_w"])
    xp = np.concatenate([xp[:, 0:DI]] + [xp[:, DI:]] * 3, 1)
    wm = np.concatenate([T(i["L1_attn_in_proj_w"]), halves(xp), halves(T(i["L1_attn_dt_proj_w"])),
                         halves(T(i["L1_attn_out_proj_w"])), halves(np.reshape(i["L1_attn_conv_w"], (DI, TAPS))),
                         col(i["L1_attn_conv_b"]), col(i["L1_attn_dt_proj_b"]), halves(i["L1_attn_A_log"]),
                         col(i["L1_attn_D_param"])], 1)
    wf = np.concatenate([T(i["L1_ffn_w1_w"]), T(i["L1_ffn_w2_w"]), halves(T(i["L1_ffn_h1_w"])),
                         halves(T(i["L1_ffn_h2_w"])), halves(T(i["L1_ffn_w3_w"])), col(i["L1_ffn_w1_s"]),
                         col(i["L1_ffn_w2_s"]), col(i["L1_ffn_h1_s"]), col(i["L1_ffn_h2_s"]), rows(i["L1_ffn_w3_s"])], 1)
    return wa, moe, wm, wf


def _constants():
    p = np.arange(P)
    block = (p[:, None] // HD == p[None, :] // HD)
    head = (p[:, None] // HD == np.arange(HEADS)[None, :])
    before = p[:, None] < p[None, :]
    decay = np.exp(-(np.arange(POS, dtype=np.float32) / np.float32(POS))).reshape(GT, P).T
    part = p[:, None] % 32 == np.arange(32)[None, :]
    const = np.concatenate([np.eye(P), block, head, before, np.broadcast_to(np.arange(EXP), (P, EXP)), decay, part],
                           1).astype(np.float32)
    return const


def kernel(**inputs):
    import concourse.bacc as bacc
    from concourse.bass_utils import run_bass_kernel_spmd

    i = {n: np.asarray(a) for n, a in inputs.items()}
    wa, moe, wm, wf = _packed(i)
    const = _constants()
    arrays = {"x": i["L0_attn_x"].reshape(TOK, D), "const": const, "wa": wa, "moe": moe, "wm": wm, "wf": wf}
    arrays = {n: np.ascontiguousarray(a) for n, a in arrays.items()}
    nc = bacc.Bacc("TRN2", target_bir_lowering=False, num_devices=1)
    aps = [nc.dram_tensor(n + "_dram", a.shape, mybir.dt.from_np(a.dtype), kind="ExternalInput").ap() for n, a in arrays.items()]
    y = nc.dram_tensor("y_dram", (TOK, D), F32, kind="ExternalOutput").ap()
    program(nc, *aps, y)
    r = run_bass_kernel_spmd(nc, [{n + "_dram": a for n, a in arrays.items()}], core_ids=[0])
    return r.results[0]["y_dram"].reshape(SEQ, POS, D)
```

```python
from contextlib import ExitStack

import numpy as np

import concourse.bass as bass
from concourse import mybir

P = 128
SEQ, POS, D = 8, 1024, 128
TOK = SEQ * POS
TILES = TOK // P
GT = 8
GN = GT * P
BANK = 512
HEADS, HD = 16, 8
EXP, FFN, TOPK = 16, 256, 2
CAP = int(np.ceil(TOK * TOPK / EXP * 1.25))
SLOTS = EXP * CAP
CT = CAP // P
DI, NS, TAPS = 256, 16, 4
HID = 512
LN_EPS, ATT_EPS = 1e-5, 1e-6

F32 = mybir.dt.float32
BF16 = mybir.dt.bfloat16
U32 = mybir.dt.uint32
ALU = mybir.AluOpType
ACT = mybir.ActivationFunctionType
AX = mybir.AxisListType.X


def columns(widths):
    at, out = 0, {}
    for name, w in widths:
        out[name] = slice(at, at + w)
        at += w
    return out, at


CONST, CONST_W = columns([("ident", P), ("block", P), ("head", HEADS), ("before", P), ("iota", EXP),
                          ("decay", GT), ("part", 32)])
WA, WA_W = columns([("q", P), ("k", P), ("v", P), ("o", P), ("gq", P), ("gk", P), ("gv", P), ("proj", P),
                    ("router", EXP), ("bq", 1), ("ln1w", 1), ("ln1b", 1), ("ln2w", 1), ("ln2b", 1),
                    ("bk", P), ("bv", P), ("bo", P)])
WM, WM_W = columns([("in", 2 * DI), ("xp", 2 * (DI + 96)), ("dt", 2 * DI), ("out", 2 * D), ("cw", 2 * TAPS),
                    ("cb", 2), ("dtb", 2), ("alog", 2 * NS), ("dpar", 2)])
WF, WF_W = columns([("w1", HID), ("w2", HID), ("h1", 4 * HID), ("h2", 4 * HID), ("w3", 4 * D),
                    ("s1", 4), ("s2", 4), ("t1", 4), ("t2", 4), ("s3", D)])


def program(nc, x_in, const_in, wa_in, moe_in, wm_in, wf_in, out):
    x_tiles = x_in.rearrange("(i p) d -> p i d", p=P)
    out_tiles = out.rearrange("(i p) d -> p i d", p=P)
    slot_rows = nc.dram_tensor("slot_rows", (SLOTS, D), F32, kind="Internal").ap()
    slot_outs = nc.dram_tensor("slot_outs", (SLOTS, D), F32, kind="Internal").ap()
    x_mid = nc.dram_tensor("x_mid", (P, TILES, D), F32, kind="Internal").ap()

    with ExitStack() as ctx:
        def sb(name, shape, dt=F32, stack=ctx):
            return stack.enter_context(nc.sbuf_tensor(name, shape, dt))

        def sem(name):
            return ctx.enter_context(nc.semaphore(name))

        const = sb("const", [P, CONST_W])
        minus_half = sb("minus_half", [P, GT])
        wm, wf = sb("wm", [P, WM_W]), sb("wf", [P, WF_W])
        m_wm, m_wf = sem("m_wm"), sem("m_wf")
        x_stack = ctx.enter_context(ExitStack())
        X = sb("X", [P, TILES, D], stack=x_stack)
        ident = const[:, CONST["ident"]]
        PS = [ctx.enter_context(nc.psum_tensor(f"ps{u}", [P, 4 * BANK], F32)) for u in range(2)]

        def tiles_of(t, n=GT, w=D):
            return t.rearrange("p (t d) -> p t d", d=w) if n else t

        ln_sems = {n: sem("ln_" + n) for n in ("stats", "moments", "eps", "power")}

        def moments(v, y, st, mv, n=GT):
            for t in range(n):
                nc.vector.bn_stats(st[:, t, :], y(t)).then_inc(ln_sems["stats"], 1)
            v.wait_ge(ln_sems["stats"], n).then_inc(ln_sems["stats"], -n)
            for t in range(n):
                last = nc.vector.bn_aggr(mv[:, t, :], st[:, t, :])
            last.then_inc(ln_sems["moments"], 1)

        def normalise(v, y, mv, rs, dst, n=GT):
            v.wait_ge(ln_sems["power"], 1).then_inc(ln_sems["power"], -1)
            for t in range(n):
                last = nc.vector.tensor_scalar(dst(t), y(t), mv[:, t, 0:1], rs[:, t:t + 1],
                                               ALU.subtract, ALU.mult)
            return last

        def layernorm(v, y, st, mv, rs, dst, n=GT):
            moments(v, y, st, mv, n)
            return normalise(v, y, mv, rs, dst, n)

        def inverse_root(g, mv, ve, rs, n=GT):
            g.wait_ge(ln_sems["moments"], 1).then_inc(ln_sems["moments"], -1)
            nc.gpsimd.tensor_scalar(ve[:], mv[:, :, 1], LN_EPS, None, ALU.add).then_inc(ln_sems["eps"], 1)
            g.wait_ge(ln_sems["eps"], 1).then_inc(ln_sems["eps"], -1)
            nc.gpsimd.tensor_tensor(rs[:], ve[:], minus_half[:, 0:n], ALU.pow).then_inc(ln_sems["power"], 1)

        wa_stack = ctx.enter_context(ExitStack())
        wa = sb("wa", [P, WA_W], stack=wa_stack)
        w = {n: wa[:, c] for n, c in WA.items()}
        zeros = sb("zeros", [P, 1024], stack=wa_stack)

        with ExitStack() as ph:
            def pb(name, shape, dt=F32):
                return [sb(f"a_{name}{u}", shape, dt, ph) for u in range(2)]

            x_ld, xT, kf, vv = pb("x", [P, GT, D]), pb("xT", [P, GN]), pb("kf", [P, GT, D]), pb("vv", [P, GT, D + 2])
            kv, qf, den, att = pb("kv", [P, D + HEADS]), pb("qf", [P, GN]), pb("den", [P, GT, HEADS]), pb("att", [P, GT, D])
            attT, xb, y = pb("attT", [P, GN]), pb("xb", [P, GT, D]), pb("y", [P, GT, D])
            st, mv, ve, rs = pb("st", [P, GT, 6]), pb("mv", [P, GT, 2]), pb("ve", [P, GT]), pb("rs", [P, GT])
            (s_const, s_wa, s_zero, s_x, s_xfree, s_xp, s_T, s_xT, s_k, s_v, s_kf, s_kvp, s_kv, s_qp, s_qf, s_num,
             s_att, s_aT, s_aTs, s_o, s_xb, s_dve, s_ready, s_psfree, s_xbfree, s_half, s_x1) = [
                sem("a_" + n) for n in "const wa zero x xfree xp T xT k v kf kvp kv qp qf num att aT aTs o xb dve ready psfree xbfree half x1".split()]
            decay = const[:, CONST["decay"]]

            def bc_tiles(row, n=GT, width=D):
                return row[:, None, :].to_broadcast([P, n, width])

            A = [PS[u][:, 0:GN] for u in range(2)]
            B = [PS[u][:, GN:2 * GN] for u in range(2)]

            with nc.Block() as block:
                @block.sync
                def _(sp):
                    sp.dma_start(const[:], const_in).then_inc(s_const, 16)
                    sp.dma_start(wa[:], wa_in).then_inc(s_wa, 16)
                    with sp.Fori(0, SEQ // 2) as pair:
                        for u in range(2):
                            sp.wait_ge(s_xfree, 1).then_inc(s_xfree, -1)
                            sp.dma_start(x_ld[u][:], x_tiles[:, bass.ds(pair * (2 * GT) + u * GT, GT), :]).then_inc((s_x, s_x1)[u], 16)
                    sp.dma_start(wm[:], wm_in).then_inc(m_wm, 16)
                    sp.dma_start(wf[:], wf_in).then_inc(m_wf, 16)
                    sp.wait_ge(s_zero, 1)
                    for r in range(0, SLOTS, 1024):
                        sp.dma_start(slot_rows[r:r + 1024, :].rearrange("(p a) d -> p (a d)", p=P),
                                     zeros[:, 0:1024]).then_inc(s_half, 16)
                    sp.wait_ge(s_half, 16 * (SLOTS // 1024))

                @block.gpsimd
                def _(g):
                    nc.gpsimd.memset(minus_half[:], -0.5)
                    nc.gpsimd.memset(zeros[:], 0.0).then_inc(s_zero, 1)
                    g.sem_inc(s_xfree, 2)
                    g.wait_ge(s_wa, 16)
                    with g.Fori(0, SEQ // 2) as pair:
                        for u in range(2):
                            g.wait_ge(s_xp, 1).then_inc(s_xp, -1)
                            g.wait_ge(s_xbfree, 1).then_inc(s_xbfree, -1)
                            nc.gpsimd.tensor_tensor(xb[u][:], x_ld[u][:], bc_tiles(w["bo"]), ALU.add).then_inc(s_xb, 1)
                            g.wait_ge(s_xb, 1).then_inc(s_xb, -1)
                            g.sem_inc(s_ready, 1)
                            g.sem_inc(s_xfree, 1)
                        for u in range(2):
                            inverse_root(g, mv[u], ve[u], rs[u])

                @block.scalar
                def _(s):
                    s.wait_ge(s_wa, 16)
                    with s.Fori(0, SEQ // 2) as pair:
                        for u in range(2):
                            s.wait_ge(s_T, 1).then_inc(s_T, -1)
                            s.sem_inc(s_xp, 1)
                            nc.scalar.copy(xT[u][:], A[u]).then_inc(s_xT, 1)
                        for u in range(2):
                            s.wait_ge(s_qp, 1).then_inc(s_qp, -1)
                            nc.scalar.activation(qf[u][:], A[u], ACT.Relu, bias=w["bq"]).then_inc(s_qf, 1)
                        for u in range(2):
                            s.wait_ge(s_aT, 1).then_inc(s_aT, -1)
                            nc.scalar.copy(attT[u][:], A[u]).then_inc(s_aTs, 1)

                @block.vector
                def _(v):
                    def own(ins):
                        ins.then_inc(s_dve, 1)
                        v.wait_ge(s_dve, 1).then_inc(s_dve, -1)

                    for u in range(2):
                        own(nc.vector.memset(vv[u][:], 1.0))
                    v.sem_inc(s_xbfree, 2)
                    v.sem_inc(s_psfree, 2)
                    v.wait_ge(s_const, 16)
                    v.wait_ge(s_wa, 16)
                    with v.Fori(0, SEQ // 2) as pair:
                        for u in range(2):
                            v.wait_ge(s_k, 1).then_inc(s_k, -1)
                            own(nc.vector.tensor_tensor(kf[u][:], tiles_of(B[u]), bc_tiles(w["bk"]), ALU.add))
                            nc.vector.scalar_tensor_tensor(
                                out=kf[u][:], in0=kf[u][:], scalar=0.0,
                                in1=decay[:, :, None].to_broadcast([P, GT, D]), op0=ALU.max, op1=ALU.mult).then_inc(s_kf, 1)
                            v.wait_ge(s_v, 1).then_inc(s_v, -1)
                            nc.vector.tensor_tensor(vv[u][:, :, 0:D], tiles_of(A[u]), bc_tiles(w["bv"]), ALU.add).then_inc(s_kf, 1)
                        for u in range(2):
                            v.wait_ge(s_kvp, 1).then_inc(s_kvp, -1)
                            nc.vector.tensor_tensor(kv[u][:, 0:D], B[u][:, 0:D], const[:, CONST["block"]], ALU.mult)
                            nc.vector.tensor_scalar(kv[u][:, D:], const[:, CONST["head"]], B[u][:, D:D + 1],
                                                    None, ALU.mult).then_inc(s_kv, 1)
                        for u in range(2):
                            v.wait_ge(s_num, 1).then_inc(s_num, -1)
                            own(nc.vector.tensor_tensor(den[u][:], B[u][:, 0:GT * HEADS].rearrange("p (t h) -> p t h", h=HEADS),
                                                        decay[:, :, None].to_broadcast([P, GT, HEADS]), ALU.mult))
                            own(nc.vector.tensor_scalar(den[u][:], den[u][:], ATT_EPS, None, ALU.add))
                            own(nc.vector.reciprocal(den[u][:], den[u][:]))
                            own(nc.vector.tensor_tensor(den[u][:], den[u][:],
                                                        decay[:, :, None].to_broadcast([P, GT, HEADS]), ALU.mult))
                            nc.vector.tensor_tensor(
                                att[u][:].rearrange("p t (h e) -> p (t h) e", e=HD),
                                A[u].rearrange("p (q e) -> p q e", e=HD),
                                den[u][:].rearrange("p t h -> p (t h)")[:, :, None].to_broadcast([P, GT * HEADS, HD]),
                                ALU.mult).then_inc(s_att, 1)
                        for u in range(2):
                            v.wait_ge(s_o, 1).then_inc(s_o, -1)
                            v.wait_ge(s_ready, 1).then_inc(s_ready, -1)
                            own(nc.vector.tensor_tensor(y[u][:], tiles_of(B[u]), xb[u][:], ALU.add))
                            v.sem_inc(s_psfree, 1)
                            v.sem_inc(s_xbfree, 1)
                            last = layernorm(v, lambda t: y[u][:, t, :], st[u], mv[u], rs[u],
                                             lambda t: X[:, bass.ds(pair * (2 * GT) + (u * GT + t), 1), :].rearrange("p o d -> p (o d)"))
                            own(last)

                @block.tensor
                def _(pe):
                    pe.wait_ge(s_const, 16)
                    pe.wait_ge(s_wa, 16)
                    with pe.Fori(0, SEQ // 2) as pair:
                        for u in range(2):
                            pe.wait_ge((s_x, s_x1)[u], 16).then_inc((s_x, s_x1)[u], -16)
                            pe.wait_ge(s_psfree, 1).then_inc(s_psfree, -1)
                            for t in range(GT):
                                mm = nc.tensor.transpose(A[u][:, t * P:(t + 1) * P], x_ld[u][:, t, :], ident)
                            mm.then_inc(s_T, 1)
                        for u in range(2):
                            pe.wait_ge(s_xT, 1).then_inc(s_xT, -1)
                            for t in range(GT):
                                mm = nc.tensor.matmul(B[u][:, t * P:(t + 1) * P], xT[u][:, t * P:(t + 1) * P], w["k"],
                                                      start=True, stop=True)
                            mm.then_inc(s_k, 1)
                            for t in range(GT):
                                mm = nc.tensor.matmul(A[u][:, t * P:(t + 1) * P], xT[u][:, t * P:(t + 1) * P], w["v"],
                                                      start=True, stop=True)
                            mm.then_inc(s_v, 1)
                        for u in range(2):
                            pe.wait_ge(s_kf, 2).then_inc(s_kf, -2)
                            for c in range(2):
                                mm = nc.tensor.matmul(A[u][:, c * BANK:(c + 1) * BANK], w["q"],
                                                      xT[u][:, c * BANK:(c + 1) * BANK], start=True, stop=True)
                            mm.then_inc(s_qp, 1)
                            for t in range(GT):
                                mm = nc.tensor.matmul(B[u][:, 0:D + 1], kf[u][:, t, :], vv[u][:, t, 0:D + 1],
                                                      start=t == 0, stop=t == GT - 1)
                            mm.then_inc(s_kvp, 1)
                        for u in range(2):
                            pe.wait_ge(s_qf, 1).then_inc(s_qf, -1)
                            pe.wait_ge(s_kv, 1).then_inc(s_kv, -1)
                            for t in range(GT):
                                nc.tensor.matmul(A[u][:, t * P:(t + 1) * P], qf[u][:, t * P:(t + 1) * P], kv[u][:, 0:D],
                                                 start=True, stop=True)
                                mm = nc.tensor.matmul(B[u][:, t * HEADS:(t + 1) * HEADS], qf[u][:, t * P:(t + 1) * P],
                                                      kv[u][:, D:], start=True, stop=True)
                            mm.then_inc(s_num, 1)
                        for u in range(2):
                            pe.wait_ge(s_att, 1).then_inc(s_att, -1)
                            for t in range(GT):
                                mm = nc.tensor.transpose(A[u][:, t * P:(t + 1) * P], att[u][:, t, :], ident)
                            mm.then_inc(s_aT, 1)
                        for u in range(2):
                            pe.wait_ge(s_aTs, 1).then_inc(s_aTs, -1)
                            for t in range(GT):
                                mm = nc.tensor.matmul(B[u][:, t * P:(t + 1) * P], attT[u][:, t * P:(t + 1) * P], w["o"],
                                                      start=True, stop=True)
                            mm.then_inc(s_o, 1)

        moe_stack = ctx.enter_context(ExitStack())
        Z2 = sb("Z2", [P, TILES, D], stack=moe_stack)
        prob = sb("prob", [P, TILES, EXP], stack=moe_stack)
        Xg = X[:].rearrange("p (s j) d -> p s j d", j=GT)
        Zg = Z2[:].rearrange("p (s j) d -> p s j d", j=GT)
        prob_g = prob[:].rearrange("p (s j) e -> p s j e", j=GT)
        pair_at = [sum(GT - k for k in range(s)) for s in range(GT + 1)]
        with ExitStack() as ph:
            def pb(name, shape, n=1):
                tiles = [sb(f"b_{name}{u}", shape, F32, ph) for u in range(n)]
                return tiles if n > 1 else tiles[0]

            z1, z2, zT1, zT2 = pb("z1", [P, GT, D]), pb("z2", [P, GT, D]), pb("zT1", [P, GN]), pb("zT2", [P, GN])
            Q, K, V = pb("Q", [P, GT, D]), pb("K", [P, GT, D]), pb("V", [P, GT, D], 2)
            qk, av = pb("qk", [P, pair_at[GT], D]), pb("av", [P, pair_at[GT], D])
            score, attn = pb("score", [P, GT, GT, HEADS]), pb("attn", [P, GT, GT, HEADS], 2)
            smax, ssum = pb("smax", [P, GT, HEADS]), pb("ssum", [P, GT, HEADS])
            att, H = pb("att", [P, GT, D]), pb("H", [P, GT, D])
            lg, lmax, lsum = pb("lg", [P, GT, EXP]), pb("lmax", [P, GT]), pb("lsum", [P, GT])
            st, mv, ve, rs = pb("st", [P, GT, 6], 2), pb("mv", [P, GT, 2], 2), pb("ve", [P, GT], 2), pb("rs", [P, GT], 2)
            (b_z1, b_T1, b_Ts1, b_q, b_k, b_v, b_qe, b_ke, b_ktaken, b_ve, b_vtaken, b_qkfree, b_pr, b_prfree, b_sub, b_exp, b_av, b_avfree,
             b_vfree, b_at, b_aT, b_aTs, b_o, b_h, b_hfree, b_z2, b_z2free, b_T2, b_Ts2, b_lg, b_ls, b_le, b_lgfree, b_dve,
             b_act) = [
                sem("b_" + n) for n in ("z1 T1 Ts1 q k v qe ke ktaken ve vtaken qkfree pr prfree sub exp av avfree vfree at aT aTs o h hfree "
                                        "z2 z2free T2 Ts2 lg ls le lgfree dve act").split()]
            A = [PS[u][:, 0:GN] for u in range(2)]
            B = [PS[u][:, GN:2 * GN] for u in range(2)]
            scale = float(HD) ** -0.5
            rows = lambda t, s: t[:, pair_at[s]:pair_at[s + 1], :]
            over_keys = lambda t: t[:].rearrange("p k q h -> p (q h) k")
            at_group = lambda t, g: t[:, :, bass.ds(g, 1), :].rearrange("p s o d -> p s (o d)")

            def turns(eng, turn):
                turn(-1, 1, "f")
                turn(0, 0, "fs")
                turn(1, 1, "fsv")
                with eng.Fori(1, GT // 2 - 1) as i:
                    for u in range(2):
                        turn(i * 2 + u, u, "fsvo")
                turn(GT - 2, 0, "fsvo")
                turn(GT - 1, 1, "svo")
                turn(GT, 0, "vo")
                turn(GT + 1, 1, "o")

            with nc.Block() as block:
                @block.gpsimd
                def _(g):
                    def turn(t, u, parts):
                        def scores(keys):
                            for s in keys:
                                nc.gpsimd.tensor_tensor(rows(qk, s), Q[:, s:, :], K[:, s:s + 1, :].to_broadcast([P, GT - s, D]),
                                                        ALU.mult).then_inc(b_pr, 1)
                        def weighted(keys):
                            a, vals = attn[1 - u], V[1 - u]
                            for s in keys:
                                nc.gpsimd.tensor_tensor(
                                    rows(av, s).rearrange("p q (h e) -> p q h e", e=HD),
                                    a[:, s, s:, :, None].to_broadcast([P, GT - s, HEADS, HD]),
                                    vals[:, s:s + 1, :].rearrange("p o (h e) -> p o h e", e=HD).to_broadcast([P, GT - s, HEADS, HD]),
                                    ALU.mult).then_inc(b_av, 1)
                        if "s" in parts:
                            g.wait_ge(b_ke, 1).then_inc(b_ke, -1)
                            g.wait_ge(b_prfree, 1).then_inc(b_prfree, -1)
                            scores(range(0, 5))
                        if "f" in parts:
                            inverse_root(g, mv[0], ve[0], rs[0])
                        if "s" in parts:
                            scores(range(5, GT))
                        if "v" in parts:
                            g.wait_ge(b_exp, 1).then_inc(b_exp, -1)
                            g.wait_ge(b_ve, 1).then_inc(b_ve, -1)
                            g.wait_ge(b_avfree, 1).then_inc(b_avfree, -1)
                            weighted(range(0, 2))
                        if "o" in parts:
                            inverse_root(g, mv[1], ve[1], rs[1])
                            g.wait_ge(b_h, 1).then_inc(b_h, -1)
                            x = at_group(Xg, t - 2)
                            nc.gpsimd.tensor_tensor(x, x, H[:], ALU.add).then_inc(b_hfree, 1)
                        if "v" in parts:
                            weighted(range(2, GT))

                    turns(g, turn)

                @block.scalar
                def _(s):
                    def own(ins):
                        ins.then_inc(b_act, 1)
                        s.wait_ge(b_act, 1).then_inc(b_act, -1)

                    def turn(t, u, parts):
                        if "o" in parts:
                            s.wait_ge(b_aT, 1).then_inc(b_aT, -1)
                            nc.scalar.copy(zT2[:], A[1]).then_inc(b_aTs, 1)
                        if "f" in parts:
                            s.wait_ge(b_T1, 1).then_inc(b_T1, -1)
                            nc.scalar.activation(zT1[:], A[0], ACT.Identity, bias=w["ln1b"], scale=w["ln1w"]).then_inc(b_Ts1, 1)
                            s.wait_ge(b_q, 1).then_inc(b_q, -1)
                            s.wait_ge(b_qkfree, 1).then_inc(b_qkfree, -1)
                            nc.scalar.copy(Q[:], tiles_of(B[0])).then_inc(b_qe, 1)
                            s.wait_ge(b_k, 1).then_inc(b_k, -1)
                            own(nc.scalar.copy(K[:], tiles_of(A[0])))
                            s.sem_inc(b_ke, 1)
                            s.sem_inc(b_ktaken, 1)
                        if "s" in parts:
                            s.wait_ge(b_sub, 1).then_inc(b_sub, -1)
                            nc.scalar.activation(attn[u][:], attn[u][:], ACT.Exp, scale=scale).then_inc(b_exp, 1)
                        if "o" in parts:
                            s.wait_ge(b_T2, 1).then_inc(b_T2, -1)
                            nc.scalar.activation(zT2[:], A[1], ACT.Identity, bias=w["ln2b"], scale=w["ln2w"]).then_inc(b_Ts2, 1)
                            nc.scalar.copy(at_group(Zg, t - 2), z2[:]).then_inc(b_z2free, 1)
                        if "f" in parts:
                            s.wait_ge(b_v, 1).then_inc(b_v, -1)
                            s.wait_ge(b_vfree, 1).then_inc(b_vfree, -1)
                            own(nc.scalar.copy(V[1 - u][:], tiles_of(B[0])))
                            s.sem_inc(b_ve, 1)
                            s.sem_inc(b_vtaken, 1)
                        if "o" in parts:
                            s.wait_ge(b_ls, 1).then_inc(b_ls, -1)
                            nc.scalar.activation(lg[:], lg[:], ACT.Exp).then_inc(b_le, 1)

                    turns(s, turn)

                @block.vector
                def _(v):
                    def own(ins):
                        ins.then_inc(b_dve, 1)
                        v.wait_ge(b_dve, 1).then_inc(b_dve, -1)

                    def turn(t, u, parts):
                        def sums(keys):
                            for s in keys:
                                v.wait_ge(b_pr, 1).then_inc(b_pr, -1)
                                last = nc.vector.tensor_reduce(score[:, s, s:, :], rows(qk, s).rearrange("p q (h e) -> p (q h) e", e=HD),
                                                               AX, ALU.add)
                            return last
                        x1 = lambda r: Xg[:, r, bass.ds(t + 1, 1), :].rearrange("p o d -> p (o d)")
                        def add_keys(keys):
                            for s in keys:
                                v.wait_ge(b_av, 1).then_inc(b_av, -1)
                                own(nc.vector.tensor_tensor(av[:, s:GT, :], av[:, s:GT, :], rows(av, s), ALU.add))
                        if "f" in parts:
                            moments(v, x1, st[0], mv[0])
                        if "s" in parts:
                            sums(range(0, 5))
                        if "f" in parts:
                            normalise(v, x1, mv[0], rs[0], lambda r: z1[:, r, :]).then_inc(b_z1, 1)
                        if "o" in parts:
                            v.wait_ge(b_o, 1).then_inc(b_o, -1)
                            v.wait_ge(b_hfree, 1).then_inc(b_hfree, -1)
                            own(nc.vector.tensor_tensor(H[:], tiles_of(B[1]), at_group(Xg, t - 2), ALU.add))
                            v.sem_inc(b_h, 1)
                            moments(v, lambda r: H[:, r, :], st[1], mv[1])
                        if "s" in parts:
                            own(sums(range(5, GT)))
                            v.sem_inc(b_prfree, 1)
                            v.sem_inc(b_qkfree, 1)
                            own(nc.vector.tensor_reduce(smax[:], over_keys(score), AX, ALU.max))
                            nc.vector.tensor_tensor(attn[u][:], score[:], smax[:, None, :, :].to_broadcast([P, GT, GT, HEADS]),
                                                    ALU.subtract).then_inc(b_sub, 1)
                        if "v" in parts:
                            v.wait_ge(b_av, 1).then_inc(b_av, -1)
                            own(nc.vector.tensor_reduce(ssum[:], over_keys(attn[1 - u]), AX, ALU.add))
                            own(nc.vector.reciprocal(ssum[:], ssum[:]))
                            add_keys(range(1, 2))
                        if "o" in parts:
                            v.wait_ge(b_z2free, 1).then_inc(b_z2free, -1)
                            normalise(v, lambda r: H[:, r, :], mv[1], rs[1], lambda r: z2[:, r, :]).then_inc(b_z2, 1)
                        if "v" in parts:
                            add_keys(range(2, GT))
                            own(nc.vector.tensor_tensor(
                                att[:].rearrange("p q (h e) -> p (q h) e", e=HD),
                                av[:, 0:GT, :].rearrange("p q (h e) -> p (q h) e", e=HD),
                                ssum[:].rearrange("p q h -> p (q h)")[:, :, None].to_broadcast([P, GT * HEADS, HD]), ALU.mult))
                            v.sem_inc(b_at, 1)
                            v.sem_inc(b_avfree, 1)
                            v.sem_inc(b_vfree, 1)
                        if "o" in parts:
                            v.wait_ge(b_lg, 1).then_inc(b_lg, -1)
                            L = B[1][:, 0:GT * EXP].rearrange("p (t e) -> p t e", e=EXP)
                            own(nc.vector.tensor_reduce(lmax[:], L, AX, ALU.max))
                            own(nc.vector.tensor_tensor(lg[:], L, lmax[:, :, None].to_broadcast([P, GT, EXP]), ALU.subtract))
                            v.sem_inc(b_ls, 1)
                            v.sem_inc(b_lgfree, 1)
                            v.wait_ge(b_le, 1).then_inc(b_le, -1)
                            own(nc.vector.tensor_reduce(lsum[:], lg[:], AX, ALU.add))
                            own(nc.vector.reciprocal(lsum[:], lsum[:]))
                            own(nc.vector.tensor_tensor(at_group(prob_g, t - 2), lg[:], lsum[:, :, None].to_broadcast([P, GT, EXP]), ALU.mult))

                    own(nc.vector.memset(score[:], -1e30))
                    for free in (b_hfree, b_z2free, b_prfree, b_qkfree, b_avfree, b_lgfree, b_ktaken, b_vtaken):
                        v.sem_inc(free, 1)
                    v.sem_inc(b_vfree, 2)
                    turns(v, turn)

                @block.tensor
                def _(pe):
                    def turned(dst, src, done):
                        for t in range(GT):
                            mm = nc.tensor.transpose(dst[:, t * P:(t + 1) * P], src[:, t, :], ident)
                        mm.then_inc(done, 1)

                    def project(dst, lhsT, rhs, n, done):
                        for t in range(GT):
                            mm = nc.tensor.matmul(dst[:, t * n:(t + 1) * n], lhsT[:, t * P:(t + 1) * P], rhs, start=True, stop=True)
                        mm.then_inc(done, 1)

                    def turn(t, u, parts):
                        if "o" in parts:
                            pe.wait_ge(b_at, 1).then_inc(b_at, -1)
                            turned(A[1], att, b_aT)
                            pe.wait_ge(b_aTs, 1).then_inc(b_aTs, -1)
                            pe.wait_ge(b_lgfree, 1).then_inc(b_lgfree, -1)
                            project(B[1], zT2, w["proj"], P, b_o)
                        if "f" in parts:
                            pe.wait_ge(b_z1, 1).then_inc(b_z1, -1)
                            pe.wait_ge(b_ktaken, 1).then_inc(b_ktaken, -1)
                            turned(A[0], z1, b_T1)
                            pe.wait_ge(b_Ts1, 1).then_inc(b_Ts1, -1)
                            pe.wait_ge(b_vtaken, 1).then_inc(b_vtaken, -1)
                            project(B[0], zT1, w["gq"], P, b_q)
                            project(A[0], zT1, w["gk"], P, b_k)
                            pe.wait_ge(b_qe, 1).then_inc(b_qe, -1)
                            project(B[0], zT1, w["gv"], P, b_v)
                        if "o" in parts:
                            pe.wait_ge(b_z2, 1).then_inc(b_z2, -1)
                            turned(A[1], z2, b_T2)
                            pe.wait_ge(b_Ts2, 1).then_inc(b_Ts2, -1)
                            project(B[1], zT2, w["router"], EXP, b_lg)

                    turns(pe, turn)

        route_stack = ctx.enter_context(ExitStack())
        gates = sb("gates", [P, TILES, 2], stack=route_stack)
        to_row = sb("to_row", [P, TILES, 2], U32, route_stack)
        from_row = sb("from_row", [P, TILES, 2], U32, route_stack)
        PAST = float(1 << 20)
        with ExitStack() as ph:
            t3 = lambda name: sb("r_" + name, [P, TILES, EXP], F32, ph)
            eq, left, hot, marked, place, tmp = [t3(n) for n in ("eq", "left", "hot0", "marked", "place", "tmp")]
            hot2 = t3("hot1")
            carry = sb("r_carry", [P, EXP, TILES], F32, ph)
            totals = sb("r_totals", [P, EXP, TILES], F32, ph)
            run_on = sb("r_run_on", [P, EXP, TILES], F32, ph)
            ones = sb("r_ones", [P, P], F32, ph)
            pk, ik, fk, keep, rowf, wk = [sb("r_" + n, [P, 2, TILES], F32, ph) for n in ("pk", "ik", "fk", "keep", "rowf", "wk")]
            r_dve, r_marked, r_sums = sem("r_dve"), sem("r_marked"), sem("r_sums")
            iota = const[:, CONST["iota"]][:, None, :].to_broadcast([P, TILES, EXP])
            per_tile = lambda a: a[:, :, None].to_broadcast([P, TILES, EXP])
            flat = lambda a: a[:].rearrange("p a b -> p (a b)")

            with nc.Block() as block:
                @block.vector
                def _(v):
                    def own(ins):
                        ins.then_inc(r_dve, 1)
                        v.wait_ge(r_dve, 1).then_inc(r_dve, -1)

                    own(nc.vector.memset(ones[:], 1.0))
                    own(nc.vector.memset(totals[:], 0.0))
                    own(nc.vector.memset(run_on[:], 1.0))
                    own(nc.vector.memset(run_on[:, :, 0:1], 0.0))
                    for k, (p_in, oh) in enumerate(((prob, hot), (left, hot2))):
                        own(nc.vector.tensor_reduce(pk[:, k, :], p_in[:], AX, ALU.max))
                        own(nc.vector.tensor_tensor(eq[:], p_in[:], per_tile(pk[:, k, :]), ALU.is_equal))
                        own(nc.vector.scalar_tensor_tensor(out=tmp[:], in0=eq[:], scalar=-float(EXP), in1=iota, op0=ALU.mult, op1=ALU.add))
                        own(nc.vector.tensor_reduce(ik[:, k, :], tmp[:], AX, ALU.min))
                        own(nc.vector.tensor_scalar(ik[:, k, :], ik[:, k, :], float(EXP), None, ALU.add))
                        own(nc.vector.tensor_tensor(oh[:], iota, per_tile(ik[:, k, :]), ALU.is_equal))
                        if k == 0:
                            own(nc.vector.scalar_tensor_tensor(out=left[:], in0=hot[:], scalar=-4.0, in1=prob[:], op0=ALU.mult, op1=ALU.add))
                    own(nc.vector.tensor_tensor(marked[:], hot[:], hot2[:], ALU.add))
                    v.sem_inc(r_marked, 1)
                    v.wait_ge(r_sums, 1).then_inc(r_sums, -1)
                    own(nc.vector.tensor_copy(totals[:, :, 1:], PS[1][:, 0:1024].rearrange("p (t e) -> p e t", e=EXP)[:, :, 0:TILES - 1]))
                    own(nc.vector.tensor_tensor_scan(flat(carry), flat(run_on), flat(totals), 0.0, ALU.mult, ALU.add))
                    own(nc.vector.tensor_tensor(place[:], PS[0][:, 0:1024].rearrange("p (t e) -> p t e", e=EXP),
                                                carry[:].rearrange("p e t -> p t e"), ALU.add))
                    for k, oh in enumerate((hot, hot2)):
                        own(nc.vector.tensor_tensor(tmp[:], oh[:], place[:], ALU.mult))
                        own(nc.vector.tensor_reduce(fk[:, k, :], tmp[:], AX, ALU.add))
                    own(nc.vector.tensor_scalar(keep[:], fk[:], float(CAP), None, ALU.is_lt))
                    own(nc.vector.scalar_tensor_tensor(out=rowf[:], in0=ik[:], scalar=float(CAP), in1=fk[:], op0=ALU.mult, op1=ALU.add))
                    own(nc.vector.tensor_tensor(rowf[:], rowf[:], keep[:], ALU.mult))
                    own(nc.vector.tensor_copy(from_row[:].rearrange("p t k -> p k t"), rowf[:]))
                    own(nc.vector.tensor_tensor(gates[:].rearrange("p t k -> p k t"), pk[:], keep[:], ALU.mult))
                    own(nc.vector.tensor_scalar(wk[:], keep[:], -PAST, PAST, ALU.mult, ALU.add))
                    own(nc.vector.tensor_tensor(rowf[:], rowf[:], wk[:], ALU.add))
                    own(nc.vector.tensor_copy(to_row[:].rearrange("p t k -> p k t"), rowf[:]))

                @block.tensor
                def _(pe):
                    pe.wait_ge(r_marked, 1).then_inc(r_marked, -1)
                    for c in range(2):
                        half = flat(marked)[:, c * BANK:(c + 1) * BANK]
                        nc.tensor.matmul(PS[0][:, c * BANK:(c + 1) * BANK], const[:, CONST["before"]], half, start=True, stop=True)
                        mm = nc.tensor.matmul(PS[1][:, c * BANK:(c + 1) * BANK], ones[:], half, start=True, stop=True)
                    mm.then_inc(r_sums, 1)

        with ExitStack() as ph:
            def pb(name, shape, dt=F32):
                return [sb(f"d_{name}{u}", shape, dt, ph) for u in range(2)]
            row_at, rows_out = pb("row_at", [P, GT, 2], U32), pb("rows_out", [P, GT, D])
            d_ready, d_free, d_sent = sem("d_ready"), sem("d_free"), [sem("d_sent0"), sem("d_sent1")]
            with nc.Block() as block:
                @block.vector
                def _(v):
                    v.sem_inc(d_free, 2)
                    with v.Fori(0, SEQ // 2) as pair:
                        for u in range(2):
                            v.wait_ge(d_free, 1).then_inc(d_free, -1)
                            nc.vector.tensor_copy(row_at[u][:], to_row[:, bass.ds(pair * (2 * GT) + u * GT, GT), :]).then_inc(d_ready, 1)
                            nc.vector.tensor_copy(rows_out[u][:], Z2[:, bass.ds(pair * (2 * GT) + u * GT, GT), :]).then_inc(d_ready, 1)
                    v.wait_ge(d_free, 2).then_inc(d_free, -2)

                @block.gpsimd
                def _(g):
                    with g.Fori(0, SEQ // 2) as pair:
                        for u in range(2):
                            g.wait_ge(d_ready, 2).then_inc(d_ready, -2)
                            for t in range(GT):
                                for k in range(2):
                                    nc.gpsimd.indirect_dma_start(
                                        slot_rows, bass.IndirectOffsetOnAxis(ap=row_at[u][:, t, k:k + 1], axis=0),
                                        rows_out[u][:, t, :], None, bounds_check=SLOTS - 1, oob_is_err=False).then_inc(d_sent[u], 16)
                        for u in range(2):
                            g.wait_ge(d_sent[u], pair * (16 * 2 * GT) + 16 * 2 * GT)
                            g.sem_inc(d_free, 1)
        expert_w = {n: wa[:, WA[n]] for n in ("ln2w", "ln2b")}

        with ExitStack() as ph:
            def pb(name, shape, dt=F32):
                return [sb(f"e_{name}{u}", shape, dt, ph) for u in range(2)]
            HT = CT // 2
            HN = HT * P
            we, xe = pb("we", [P, 4 * P]), pb("xe", [P, CT, D])
            xeT, he, ye = pb("xeT", [P, HN]), pb("he", [P, 2, HN]), pb("ye", [P, HT, D])
            e_w, e_x, e_y = [[sem(f"e_{n}{u}") for u in range(2)] for n in "wxy"]
            e_T, e_Ts, e_up, e_act, e_down, e_out, e_st, e_wfree, e_xfree, e_own = [
                sem("e_" + n) for n in "T Ts up act down out st wfree xfree own".split()]
            turned, downs = PS[0][:, 0:HN], PS[0][:, 2 * BANK:2 * BANK + HN]
            ups = [PS[1][:, f * 2 * BANK:f * 2 * BANK + HN] for f in range(2)]
            of_expert = lambda t, e: t[bass.ds(e, 1), :, :].rearrange("o p c -> p (o c)")

            def experts(eng, expert):
                expert(0, 0, True, 2)
                expert(1, 1, False, 2)
                with eng.Fori(1, EXP // 2 - 1) as pair:
                    for u in range(2):
                        expert(pair * 2 + u, u, False, 2)
                expert(EXP - 2, 0, False, 1)
                expert(EXP - 1, 1, False, 0)

            with nc.Block() as block:
                @block.sync
                def _(sp):
                    def load_x(e, u):
                        sp.dma_start(xe[u][:].rearrange("p t d -> p (t d)"),
                                     of_expert(slot_rows.rearrange("(e p t) d -> e p (t d)", p=P, t=CT), e)).then_inc(e_x[u], 16)

                    def load_w(e, u):
                        sp.dma_start(we[u][:], of_expert(moe_in, e)).then_inc(e_w[u], 16)

                    def store(e, h):
                        sp.wait_ge(e_st, 1).then_inc(e_st, -1)
                        sp.dma_start(of_expert(slot_outs.rearrange("(e p h t) d -> e p h (t d)", p=P, h=2, t=HT)[:, :, h, :], e),
                                     ye[h][:].rearrange("p t d -> p (t d)")).then_inc(e_y[h], 16)

                    def expert(e, u, first, after):
                        if after == 2:
                            sp.wait_ge(e_xfree, 1).then_inc(e_xfree, -1)
                            load_x(e + 2, u)
                        if not first:
                            store(e - 1, 1)
                            if after:
                                sp.wait_ge(e_wfree, 1).then_inc(e_wfree, -1)
                        if after:
                            load_w(e + 1, 1 - u)
                        store(e, 0)

                    for h in range(2):
                        sp.sem_inc(e_y[h], 16)
                    load_x(0, 0)
                    load_w(0, 0)
                    load_x(1, 1)
                    experts(sp, expert)
                    store(EXP - 1, 1)
                    for h in range(2):
                        sp.wait_ge(e_y[h], 16)

                @block.scalar
                def _(s):
                    def turn(h):
                        s.wait_ge(e_T, 1).then_inc(e_T, -1)
                        nc.scalar.activation(xeT[h][:], turned, ACT.Identity, bias=expert_w["ln2b"], scale=expert_w["ln2w"]).then_inc(e_Ts, 1)

                    def gelu(h):
                        for f in range(2):
                            s.wait_ge(e_up, 1).then_inc(e_up, -1)
                            nc.scalar.activation(he[h][:, f, :], ups[f], ACT.Gelu_apprx_tanh).then_inc(e_act, 1)

                    def expert(e, u, first, after):
                        turn(1)
                        gelu(0)
                        if after:
                            turn(0)
                        gelu(1)

                    turn(0)
                    experts(s, expert)

                @block.vector
                def _(v):
                    def keep(h):
                        v.wait_ge(e_down, 1).then_inc(e_down, -1)
                        v.wait_ge(e_y[h], 16).then_inc(e_y[h], -16)
                        nc.vector.tensor_copy(ye[h][:].rearrange("p t d -> p (t d)"), downs).then_inc(e_own, 1)
                        v.wait_ge(e_own, 1).then_inc(e_own, -1)
                        v.sem_inc(e_st, 1)
                        v.sem_inc(e_out, 1)

                    def expert(e, u, first, after):
                        if not first:
                            keep(1)
                            if after:
                                v.sem_inc(e_wfree, 1)
                        keep(0)

                    v.sem_inc(e_out, 1)
                    v.sem_inc(e_act, 2)
                    experts(v, expert)
                    keep(1)

                @block.tensor
                def _(pe):
                    def turn(u, h):
                        for t in range(HT):
                            mm = nc.tensor.transpose(turned[:, t * P:(t + 1) * P], xe[u][:, h * HT + t, :], ident)
                        mm.then_inc(e_T, 1)

                    def up(u, h):
                        for f in range(2):
                            pe.wait_ge(e_act, 1).then_inc(e_act, -1)
                            for a in range(0, HN, BANK):
                                b = min(a + BANK, HN)
                                mm = nc.tensor.matmul(ups[f][:, a:b], we[u][:, f * P:(f + 1) * P], xeT[h][:, a:b], start=True, stop=True)
                            mm.then_inc(e_up, 1)

                    def down(u, h):
                        pe.wait_ge(e_out, 1).then_inc(e_out, -1)
                        for t in range(HT):
                            for f in range(2):
                                mm = nc.tensor.matmul(downs[:, t * P:(t + 1) * P], he[h][:, f, t * P:(t + 1) * P],
                                                      we[u][:, (2 + f) * P:(3 + f) * P], start=f == 0, stop=f == 1)
                        mm.then_inc(e_down, 1)

                    def expert(e, u, first, after):
                        pe.wait_ge(e_Ts, 1).then_inc(e_Ts, -1)
                        turn(u, 1)
                        pe.wait_ge(e_w[u], 16).then_inc(e_w[u], -16)
                        up(u, 0)
                        if not first:
                            down(1 - u, 1)
                        pe.wait_ge(e_Ts, 1).then_inc(e_Ts, -1)
                        if after == 2:
                            pe.sem_inc(e_xfree, 1)
                        if after:
                            pe.wait_ge(e_x[1 - u], 16).then_inc(e_x[1 - u], -16)
                            turn(1 - u, 0)
                        up(u, 1)
                        down(u, 0)

                    pe.wait_ge(e_x[0], 16).then_inc(e_x[0], -16)
                    turn(0, 0)
                    experts(pe, expert)
                    pe.wait_ge(e_act, 2).then_inc(e_act, -2)
                    down(1, 1)

        with ExitStack() as ph:
            def pb(name, shape, dt=F32):
                return [sb(f"c_{name}{u}", shape, dt, ph) for u in range(2)]
            row_at, gt, got = pb("row_at", [P, GT, 2], U32), pb("gt", [P, GT, 2]), pb("got", [P, GT, 2, D])
            y = pb("y", [P, GT, D])
            st, mv, ve, rs = pb("st", [P, GT, 6]), pb("mv", [P, GT, 2]), pb("ve", [P, GT]), pb("rs", [P, GT])
            c_at, c_got, c_dve = sem("c_at"), [sem("c_got0"), sem("c_got1")], sem("c_dve")
            c_x, c_stored = sem("c_x"), sem("c_stored")
            with nc.Block() as block:
                @block.sync
                def _(sp):
                    with sp.Fori(0, SEQ) as b:
                        sp.wait_ge(c_x, 1).then_inc(c_x, -1)
                        sp.dma_start(x_mid[:, bass.ds(b * GT, GT), :], X[:, bass.ds(b * GT, GT), :]).then_inc(c_stored, 16)
                    sp.wait_ge(c_stored, 16 * SEQ)

                @block.vector
                def _(v):
                    def own(ins):
                        ins.then_inc(c_dve, 1)
                        v.wait_ge(c_dve, 1).then_inc(c_dve, -1)

                    def ask(group, u):
                        nc.vector.tensor_copy(gt[u][:], gates[:, bass.ds(group * GT, GT), :])
                        nc.vector.tensor_copy(row_at[u][:], from_row[:, bass.ds(group * GT, GT), :]).then_inc(c_at, 1)

                    def combine(group, u, arrived, more):
                        v.wait_ge(c_got[u], arrived)
                        for t in range(GT):
                            last = nc.vector.scalar_tensor_tensor(
                                out=y[u][:, t, :], in0=got[u][:, t, 0, :], scalar=gt[u][:, t, 0:1],
                                in1=X[:, bass.ds(group * GT + t, 1), :].rearrange("p o d -> p (o d)"), op0=ALU.mult, op1=ALU.add)
                        own(last)
                        for t in range(GT):
                            last = nc.vector.scalar_tensor_tensor(
                                out=y[u][:, t, :], in0=got[u][:, t, 1, :], scalar=gt[u][:, t, 1:2],
                                in1=y[u][:, t, :], op0=ALU.mult, op1=ALU.add)
                        own(last)
                        if more:
                            ask(group + 2, u)
                        own(layernorm(v, lambda t: y[u][:, t, :], st[u], mv[u], rs[u],
                                      lambda t: X[:, bass.ds(group * GT + t, 1), :].rearrange("p o d -> p (o d)")))
                        v.sem_inc(c_x, 1)

                    for u in range(2):
                        ask(u, u)
                    with v.Fori(0, SEQ // 2 - 1) as pair:
                        for u in range(2):
                            combine(pair * 2 + u, u, pair * (16 * 2 * GT) + 16 * 2 * GT, True)
                    for u in range(2):
                        combine(SEQ - 2 + u, u, SEQ // 2 * 16 * 2 * GT, False)

                @block.gpsimd
                def _(g):
                    def gather(u):
                        g.wait_ge(c_at, 1).then_inc(c_at, -1)
                        for t in range(GT):
                            for k in range(2):
                                nc.gpsimd.indirect_dma_start(
                                    got[u][:, t, k, :], None, slot_outs,
                                    bass.IndirectOffsetOnAxis(ap=row_at[u][:, t, k:k + 1], axis=0)).then_inc(c_got[u], 16)

                    gather(0)
                    with g.Fori(0, SEQ // 2 - 1) as pair:
                        for u in range(2):
                            gather(1 - u)
                            inverse_root(g, mv[u], ve[u], rs[u])
                    gather(1)
                    for u in range(2):
                        inverse_root(g, mv[u], ve[u], rs[u])

        route_stack.close()
        moe_stack.close()
        wa_stack.close()
        x_stack.close()
        with ExitStack() as ph:
            def pb(name, shape, dt=F32):
                return sb("m_" + name, shape, dt, ph)

            FT, MB = 4, HID // P
            sel = pb("sel", [96, 32], BF16)
            m = {n: wm[:, c] for n, c in WM.items()}
            f = {n: wf[:, c] for n, c in WF.items()}
            w_xp = m["xp"].rearrange("p (k o) -> p k o", k=2)
            w_dt = m["dt"].rearrange("p (k o) -> p k o", k=2)
            w_out = m["out"].rearrange("p (k o) -> p k o", k=2)
            taps = m["cw"].rearrange("p (k o) -> p k o", k=2)
            w3 = f["w3"].rearrange("p (k d) -> p k d", d=D)
            rate = pb("rate", [P, 2 * NS])
            delta, dx, gate = [[pb(f"{n}{q}", [P, 2, GN]) for q in range(2)] for n in ("delta", "dx", "gate")]
            bc = [pb(f"bc{q}", [96, GN], BF16) for q in range(2)]
            dA, dBx, Cs = [[pb(f"{n}{q}", s) for q in range(2)] for n, s in (("dA", [P, 2, GN]), ("dBx", [P, 2, GN]), ("Cs", [P, GN]))]
            h, ch, acc = pb("h", [P, 2, GN]), pb("ch", [P, 2, GN]), pb("acc", [P, 2, GN])
            x_st, xT, uu = pb("x_st", [P, GT, D]), pb("xT", [P, GN]), pb("uu", [P, 2, GN])
            xi = pb("xi", [P, 2, GN + TAPS])
            low = xi[:, :, TAPS:]
            fT, ha, hb = pb("fT", [P, FT * P]), pb("ha", [P, MB, FT * P]), pb("hb", [P, MB, FT * P])
            xf = [pb(f"xf{q}", [P, GT, D]) for q in range(2)]
            yo = [pb(f"yo{c}", [P, FT, D]) for c in range(2)]
            st, mv, ve, rs = pb("st", [P, GT, 6]), pb("mv", [P, GT, 2]), pb("ve", [P, GT]), pb("rs", [P, GT])
            st4, mv4, ve4, rs4 = pb("st4", [P, FT, 6]), pb("mv4", [P, FT, 2]), pb("ve4", [P, FT]), pb("rs4", [P, FT])

            def sems(prefix, names):
                return [sem(prefix + n) for n in names.split()]

            m_const, m_rate = sems("m_", "const rate")
            s_B, s_C, s_Bfree, s_Cfree, s_dA, s_dAfree, s_Cs, s_Csfree, s_h, s_ch, s_chfree, s_acc, s_start = sems(
                "s_", "B C Bfree Cfree dA dAfree Cs Csfree h ch chfree acc start")
            p_x, p_xfree, p_blocks, p_sums, p_xi, p_cv, p_u, p_left, p_parts, p_ln, p_delta = sems(
                "p_", "x xfree blocks sums xi cv u left parts ln delta")
            p_free, f_free = [sem(f"p_free{c}") for c in range(2)], [sem(f"f_free{c}") for c in range(2)]
            (o_gy, o_x, o_xf0, o_xf1, o_xfree, f_blocks, f_sums, f_yo0, f_yo1, f_out0, f_out1) = sems(
                "f_", "gy x xf0 xf1 xfree blocks sums yo0 yo1 out0 out1")
            o_xf, f_yo, f_out = (o_xf0, o_xf1), (f_yo0, f_yo1), (f_out0, f_out1)
            v_own, a_own, g_own, v_added = sems("own_", "v a g v_add")
            Bp, Cp = PS[0][:, 0:GN], PS[0][:, GN:2 * GN]
            p_bank = [PS[1][:, c * BANK:(c + 1) * BANK] for c in range(2)]
            f_bank = [PS[1][:, c * BANK:(c + 1) * BANK] for c in range(2, 4)]
            col = [slice(c * BANK, (c + 1) * BANK) for c in range(2)]

            PREPARE = {1: ["turn"], 2: ["in0", "in1"], 3: ["z0", "conv0a", "conv0b"], 4: ["z1", "conv1a"],
                       5: ["conv1b", "silu"], 6: ["xp0"], 7: ["xp1", "bc"], 8: ["dt0"], 9: ["dt1", "split"],
                       10: ["exp"], 11: ["ln"], 12: ["soft0"], 13: ["soft1"], 14: ["soft2", "soft3"], 15: ["dx"]}
            MLP = {1: ["out"], 2: ["norm"], 3: ["turn0", "w1"], 4: ["w2a", "w2b", "gate_a", "gate_b"],
                   5: ["h1.0", "h1.1"], 6: ["h1.2"], 8: ["h1.3"], 9: ["h2.0"], 10: ["h2.1", "h2.2"],
                   11: ["h2.3", "w3.0"], 12: ["add0", "turn1", "w1"], 13: ["w2a", "w2b", "gate_a", "gate_b"],
                   14: ["h1.0", "h1.1"], 15: ["norm0", "h1.2", "h1.3"]}
            LATE = {0: ["h2.0", "h2.1"], 1: ["h2.2", "h2.3"], 2: ["w3.1"], 3: ["add1"], 5: ["norm1"]}
            BEFORE = ("add1",)
            MLP_FIRST = (1, 2, 3, 4, 5, 11)
            POOL_ADDS = (1, 2, 4, 11, 13)

            DECAYS = {0: (1, 2), 2: (3, 4), 4: (5, 6), 6: (7, 8), 8: (9, 10), 10: (11,), 11: (12, 13), 13: (14, 15), 15: (16,)}
            DECAYS_LAST = (11, 15)

            def beside(step, mlp, late):
                return (MLP.get(step, []) if mlp else []) + (LATE.get(step, []) if late else [])

            def bodies(eng, prologue, body, tail):
                prologue()
                body(0, 0, True, False, False)
                body(1, 1, True, True, False)
                with eng.Fori(1, SEQ // 2 - 1) as i:
                    body(i * 2, 0, True, True, True)
                    body(i * 2 + 1, 1, True, True, True)
                body(SEQ - 2, 0, True, True, True)
                body(SEQ - 1, 1, False, True, True)
                tail()

            with nc.Block() as block:
                @block.sync
                def _(sp):
                    def group(b):
                        return slice(b * GT, (b + 1) * GT) if isinstance(b, int) else bass.ds(b * GT, GT)

                    def load_x(b):
                        sp.wait_ge(p_xfree, 1).then_inc(p_xfree, -1)
                        sp.dma_start(x_st[:], x_mid[:, group(b), :]).then_inc(p_x, 16)

                    def load_residual(b, p):
                        sp.wait_ge(o_xfree, 1).then_inc(o_xfree, -1)
                        sp.dma_start(xf[p][:], x_mid[:, group(b), :]).then_inc(o_xf[p], 16)

                    def store(b, c):
                        sp.wait_ge(f_yo[c], 1).then_inc(f_yo[c], -1)
                        at = slice(b * GT + c * FT, b * GT + (c + 1) * FT) if isinstance(b, int) else bass.ds(b * GT + c * FT, FT)
                        sp.dma_start(out_tiles[:, at, :], yo[c][:]).then_inc(f_out[c], 16)

                    def prologue():
                        load_x(0)

                    def body(b, p, prep, mlp, late):
                        if prep:
                            load_x(b + 1)
                        load_residual(b, p)
                        if late:
                            store(b - 2, 1)
                        if mlp:
                            store(b - 1, 0)

                    def tail():
                        store(SEQ - 2, 1)
                        store(SEQ - 1, 0)
                        store(SEQ - 1, 1)
                        sp.wait_ge(f_out[0], 16)
                        sp.wait_ge(f_out[1], 16)

                    bodies(sp, prologue, body, tail)

                @block.scalar
                def _(s):
                    def own(ins):
                        ins.then_inc(a_own, 1)
                        s.wait_ge(a_own, 1).then_inc(a_own, -1)

                    def copy_c(n):
                        s.wait_ge(s_C, 1).then_inc(s_C, -1)
                        s.wait_ge(s_Csfree, 1).then_inc(s_Csfree, -1)
                        own(nc.scalar.copy(Cs[n % 2][:], Cp))
                        s.sem_inc(s_Cfree, 1)
                        s.sem_inc(s_Cs, 1)

                    def decays(n, p):
                        s.wait_ge(s_dAfree, 1).then_inc(s_dAfree, -1)
                        for k in range(2):
                            nc.scalar.activation(dA[n % 2][:, k, :], delta[p][:, k, :], ACT.Exp,
                                                 scale=rate[:, k * NS + n:k * NS + n + 1]).then_inc(s_dA, 1)

                    def blocks(dst, func, **kw):
                        for c in range(2):
                            s.wait_ge(p_blocks, 1).then_inc(p_blocks, -1)
                            nc.scalar.activation(dst[:, col[c]], p_bank[c], func, **kw).then_inc(p_free[c], 1)

                    def prepare(step, q):
                        for piece in PREPARE.get(step, ()):
                            o = int(piece[-1]) if piece[-1] in "01" else 0
                            if piece == "turn":
                                blocks(xT, ACT.Copy)
                                s.sem_inc(p_xfree, 1)
                            elif piece in ("in0", "in1"):
                                for c in range(2):
                                    s.wait_ge(p_blocks, 1).then_inc(p_blocks, -1)
                                    own(nc.scalar.copy(xi[:, o, TAPS - 1 + c * BANK:TAPS - 1 + (c + 1) * BANK], p_bank[c]))
                                    s.sem_inc(p_free[c], 1)
                                s.sem_inc(p_xi, 1)
                            elif piece in ("z0", "z1"):
                                blocks(gate[q][:, o, :], ACT.Silu)
                            elif piece == "silu":
                                for k in range(2):
                                    s.wait_ge(p_cv, 1).then_inc(p_cv, -1)
                                    nc.scalar.activation(uu[:, k, :], uu[:, k, :], ACT.Silu, bias=m["cb"][:, k:k + 1]).then_inc(p_u, 1)
                            elif piece in ("xp0", "xp1"):
                                blocks(low[:, o, :], ACT.Copy)
                            elif piece in ("dt0", "dt1"):
                                for c in range(2):
                                    s.wait_ge(p_blocks, 1).then_inc(p_blocks, -1)
                                    nc.scalar.activation(delta[q][:, o, col[c]], p_bank[c], ACT.Relu, bias=m["dtb"][:, o:o + 1])
                                    own(nc.scalar.activation(dx[q][:, o, col[c]], p_bank[c], ACT.Abs, bias=m["dtb"][:, o:o + 1]))
                                    s.sem_inc(p_free[c], 1)
                            elif piece == "exp":
                                own(nc.scalar.activation(low, dx[q][:], ACT.Exp, scale=-1.0))
                            elif piece == "ln":
                                nc.scalar.activation(dx[q][:], low, ACT.Ln, bias=1.0).then_inc(p_ln, 1)
                            elif piece == "bc":
                                for c in range(2):
                                    s.wait_ge(p_blocks, 1).then_inc(p_blocks, -1)
                                    nc.scalar.copy(bc[q][:, col[c]], p_bank[c][0:96, :])
                                    own(nc.scalar.copy(xT[0:96, col[c]], p_bank[c][0:96, :]))
                                    s.sem_inc(p_free[c], 1)
                                s.sem_inc(p_left, 1)

                    def mlp_step(pieces):
                        for piece in pieces:
                            if piece in ("turn0", "turn1"):
                                s.wait_ge(f_blocks, 1).then_inc(f_blocks, -1)
                                nc.scalar.copy(fT[:], f_bank[0]).then_inc(f_free[0], 1)
                            elif piece == "w1":
                                for k in range(MB):
                                    s.wait_ge(f_blocks, 1).then_inc(f_blocks, -1)
                                    nc.scalar.activation(ha[:, k, :], f_bank[k % 2], ACT.Silu, scale=f["s1"][:, k:k + 1]).then_inc(f_free[k % 2], 1)
                            elif piece[0] == "h":
                                dst, scale, k = ha if piece[1] == "1" else hb, f["t" + piece[1]], int(piece[3])
                                s.wait_ge(f_blocks, 1).then_inc(f_blocks, -1)
                                nc.scalar.activation(dst[:, k, :], f_bank[k % 2], ACT.Gelu, scale=scale[:, k:k + 1]).then_inc(f_free[k % 2], 1)

                    def prologue():
                        s.wait_ge(m_wm, 16)
                        own(nc.scalar.activation(rate[:], m["alog"], ACT.Exp))
                        own(nc.scalar.mul(rate[:], rate[:], -1.0))
                        for step in range(NS):
                            prepare(step, 0)
                        s.wait_ge(p_delta, 1).then_inc(p_delta, -1)
                        copy_c(0)
                        decays(0, 0)
                        s.wait_ge(m_wf, 16)

                    def some_decays(n, p, prep):
                        for m in DECAYS.get(n, ()):
                            if m < NS:
                                decays(m, p)
                            elif prep:
                                s.wait_ge(p_delta, 1).then_inc(p_delta, -1)
                                decays(0, 1 - p)

                    def body(b, p, prep, mlp, late):
                        for n in range(NS):
                            if n < NS - 1 or prep:
                                copy_c((n + 1) % NS)
                            if n not in DECAYS_LAST:
                                some_decays(n, p, prep)
                            if n in MLP_FIRST:
                                mlp_step(beside(n, mlp, late))
                            if prep:
                                prepare(n, 1 - p)
                            if n not in MLP_FIRST:
                                mlp_step(beside(n, mlp, late))
                            if n in DECAYS_LAST:
                                some_decays(n, p, prep)

                    def tail():
                        for n in range(NS):
                            mlp_step(beside(n, True, True))
                        for n in LATE:
                            mlp_step(LATE[n])

                    bodies(s, prologue, body, tail)

                @block.vector
                def _(v):
                    def own(ins):
                        ins.then_inc(v_own, 1)
                        v.wait_ge(v_own, 1).then_inc(v_own, -1)

                    def scan_products(n, p):
                        v.wait_ge(s_B, 1).then_inc(s_B, -1)
                        for k in range(2):
                            nc.vector.tensor_tensor(dBx[n % 2][:, k, :], Bp, dx[p][:, k, :], ALU.mult).then_inc(v_own, 1)

                    def add_product(n):
                        v.wait_ge(s_ch, 1).then_inc(s_ch, -1)
                        if n not in POOL_ADDS:
                            add = nc.vector.tensor_tensor(acc[:, 0, :], acc[:, 0, :], ch[:, 0, :], ALU.add)
                            if n == NS - 1:
                                add.then_inc(v_added, 1)
                                v.wait_ge(v_added, 1).then_inc(v_added, -1)
                                v.sem_inc(s_chfree, 1)
                            else:
                                add.then_inc(s_chfree, 1)

                    def scan_states(n):
                        for k in range(2):
                            v.wait_ge(s_dA, 1).then_inc(s_dA, -1)
                            if k:
                                v.wait_ge(s_ch, 1).then_inc(s_ch, -1)
                            nc.vector.tensor_tensor_scan(h[:, k, :], dA[n % 2][:, k, :], dBx[n % 2][:, k, :], 0.0, ALU.mult, ALU.add).then_inc(s_h, 1)

                    def gate_output(p):
                        v.wait_ge(s_acc, 1).then_inc(s_acc, -1)
                        own(nc.vector.tensor_tensor(gate[p][:], acc[:], gate[p][:], ALU.mult))
                        v.sem_inc(o_gy, 1)

                    def start_sum():
                        for k in range(2):
                            last = nc.vector.tensor_scalar(acc[:, k, :], uu[:, k, :], m["dpar"][:, k:k + 1], None, ALU.mult)
                        own(last)
                        v.sem_inc(s_start, 1)

                    def prepare(step, q):
                        for piece in PREPARE.get(step, ()):
                            if piece[0:4] == "conv":
                                k, taps_now = int(piece[4]), range(1, 2) if piece[5] == "a" else range(2, TAPS)
                                if piece[5] == "a":
                                    v.wait_ge(p_xi, 1).then_inc(p_xi, -1)
                                    own(nc.vector.tensor_scalar(uu[:, k, :], xi[:, k, 0:GN], taps[:, k, 0:1], None, ALU.mult))
                                for j in taps_now:
                                    own(nc.vector.scalar_tensor_tensor(out=uu[:, k, :], in0=xi[:, k, j:j + GN], scalar=taps[:, k, j:j + 1],
                                                                       in1=uu[:, k, :], op0=ALU.mult, op1=ALU.add))
                                if piece[5] == "b":
                                    v.sem_inc(p_cv, 1)
                            elif piece == "split":
                                v.wait_ge(p_left, 1).then_inc(p_left, -1)
                                left = xT[0:96, :]
                                own(nc.vector.tensor_tensor(left, left, bc[q][:], ALU.subtract))
                                own(nc.vector.tensor_copy(bc[q][32:64, :], left[32:64, :]))
                                own(nc.vector.tensor_copy(bc[q][64:96, :], left[64:96, :]))
                                own(nc.vector.tensor_tensor(left[64:96, :], left[64:96, :], bc[q][64:96, :], ALU.subtract))
                                own(nc.vector.tensor_copy(bc[q][64:96, :], left[64:96, :]))
                                v.sem_inc(p_parts, 1)
                            elif piece == "soft0":
                                v.wait_ge(p_ln, 1).then_inc(p_ln, -1)
                                own(nc.vector.tensor_tensor(delta[q][:], delta[q][:], dx[q][:], ALU.add))
                            elif piece == "soft1":
                                own(nc.vector.tensor_scalar(dx[q][:], low, 1.0, 1.0, ALU.add, ALU.subtract))
                            elif piece == "soft2":
                                own(nc.vector.tensor_tensor(dx[q][:], low, dx[q][:], ALU.subtract))
                            elif piece == "soft3":
                                own(nc.vector.tensor_tensor(delta[q][:], delta[q][:], dx[q][:], ALU.add))
                                v.sem_inc(p_delta, 1)
                            elif piece == "dx":
                                own(nc.vector.tensor_tensor(dx[q][:], delta[q][:], uu[:], ALU.mult))

                    def mlp_step(pieces, p):
                        for piece in pieces:
                            if piece == "out":
                                x = xf[1 - p]
                                v.wait_ge(o_xf[1 - p], 16).then_inc(o_xf[1 - p], -16)
                                for c in range(2):
                                    v.wait_ge(p_sums, 1).then_inc(p_sums, -1)
                                    part = x[:, c * FT:(c + 1) * FT, :]
                                    own(nc.vector.tensor_tensor(part, tiles_of(p_bank[c]), part, ALU.add))
                                    v.sem_inc(p_free[c], 1)
                                moments(v, lambda t: x[:, t, :], st, mv)
                            elif piece == "norm":
                                x = xf[1 - p]
                                own(normalise(v, lambda t: x[:, t, :], mv, rs, lambda t: x[:, t, :]))
                                v.sem_inc(o_x, 1)
                            elif piece in ("gate_a", "gate_b"):
                                for k in range(2) if piece == "gate_a" else range(2, MB):
                                    v.wait_ge(f_sums, 1).then_inc(f_sums, -1)
                                    nc.vector.scalar_tensor_tensor(out=hb[:, k, :], in0=f_bank[k % 2], scalar=f["s2"][:, k:k + 1],
                                                                   in1=ha[:, k, :], op0=ALU.mult, op1=ALU.mult).then_inc(f_free[k % 2], 1)
                            elif piece in ("add0", "add1"):
                                c = int(piece[-1])
                                x = xf[(1 - p) if c == 0 else p]
                                v.wait_ge(f_sums, 1).then_inc(f_sums, -1)
                                v.wait_ge(f_out[c], 16).then_inc(f_out[c], -16)
                                own(nc.vector.tensor_tensor(yo[c][:], tiles_of(f_bank[0]), x[:, c * FT:(c + 1) * FT, :], ALU.add))
                                v.sem_inc(f_free[0], 1)
                                if c == 1:
                                    v.sem_inc(o_xfree, 1)
                                moments(v, lambda t: yo[c][:, t, :], st4, mv4, FT)
                            elif piece in ("norm0", "norm1"):
                                c = int(piece[-1])
                                own(normalise(v, lambda t: yo[c][:, t, :], mv4, rs4, lambda t: yo[c][:, t, :], FT))
                                v.sem_inc(f_yo[c], 1)

                    def prologue():
                        v.wait_ge(m_wm, 16)
                        own(nc.vector.tensor_copy(sel[:], const[0:96, CONST["part"]]))
                        v.sem_inc(m_const, 1)
                        own(nc.vector.memset(xi[:], 0.0))
                        v.sem_inc(p_xfree, 1)
                        v.sem_inc(o_xfree, 2)
                        v.sem_inc(f_free[0], 1)
                        for c in range(2):
                            v.sem_inc(p_free[c], 1)
                            v.sem_inc(f_out[c], 16)
                        for step in range(NS):
                            prepare(step, 0)
                        v.wait_ge(m_wf, 16)
                        own(nc.vector.tensor_tensor(w3, w3, f["s3"][:, None, :].to_broadcast([P, MB, D]), ALU.mult))
                        v.sem_inc(m_rate, 1)

                    def body(b, p, prep, mlp, late):
                        for n in range(NS):
                            pieces = beside(n, mlp, late)
                            scan_products(n, p)
                            if n or mlp:
                                add_product((n - 1) % NS)
                            else:
                                v.wait_ge(s_ch, 1).then_inc(s_ch, -1)
                            v.wait_ge(v_own, 2).then_inc(v_own, -2)
                            v.sem_inc(s_Bfree, 1)
                            mlp_step([x for x in pieces if x in BEFORE], p)
                            scan_states(n)
                            if n == 0:
                                if mlp:
                                    gate_output(1 - p)
                                start_sum()
                            if prep:
                                prepare(n, 1 - p)
                            mlp_step([x for x in pieces if x not in BEFORE], p)

                    def tail():
                        add_product(NS - 1)
                        v.wait_ge(s_ch, 1).then_inc(s_ch, -1)
                        gate_output(1)
                        for n in range(NS):
                            mlp_step(beside(n, True, True), 0)
                        for n in LATE:
                            mlp_step(LATE[n], 1)

                    bodies(v, prologue, body, tail)

                @block.gpsimd
                def _(g):
                    def own(ins):
                        ins.then_inc(g_own, 1)
                        g.wait_ge(g_own, 1).then_inc(g_own, -1)

                    def prologue():
                        g.sem_inc(s_dAfree, 2)
                        g.sem_inc(s_Csfree, 2)
                        g.sem_inc(s_ch, 2)
                        g.sem_inc(s_chfree, 1)

                    def mlp_step(pieces):
                        for piece in pieces:
                            if piece == "norm":
                                inverse_root(g, mv, ve, rs)
                            elif piece in ("norm0", "norm1"):
                                inverse_root(g, mv4, ve4, rs4, FT)

                    def body(b, p, prep, mlp, late):
                        for n in range(NS):
                            mlp_step(beside(n, mlp, late))
                            g.wait_ge(s_Cs, 1).then_inc(s_Cs, -1)
                            g.wait_ge(s_h, 1).then_inc(s_h, -1)
                            if (n - 1) % NS not in POOL_ADDS:
                                g.wait_ge(s_chfree, 1).then_inc(s_chfree, -1)
                            nc.gpsimd.tensor_tensor(ch[:, 0, :], h[:, 0, :], Cs[n % 2][:], ALU.mult).then_inc(s_ch, 1)
                            g.wait_ge(s_h, 1).then_inc(s_h, -1)
                            g.sem_inc(s_dAfree, 1)
                            own(nc.gpsimd.tensor_tensor(ch[:, 1, :], h[:, 1, :], Cs[n % 2][:], ALU.mult))
                            g.sem_inc(s_ch, 1)
                            g.sem_inc(s_Csfree, 1)
                            if n == 0:
                                g.wait_ge(s_start, 1).then_inc(s_start, -1)
                            if n in POOL_ADDS:
                                own(nc.gpsimd.tensor_tensor(acc[:], acc[:], ch[:], ALU.add))
                            else:
                                own(nc.gpsimd.tensor_tensor(acc[:, 1, :], acc[:, 1, :], ch[:, 1, :], ALU.add))
                            if n == NS - 1:
                                g.sem_inc(s_acc, 1)

                    def tail():
                        for n in range(NS):
                            mlp_step(beside(n, True, True))
                        for n in LATE:
                            mlp_step(LATE[n])

                    bodies(g, prologue, body, tail)

                @block.tensor
                def _(pe):
                    def row_to_all(r, q, dst, done):
                        for c in range(2):
                            mm = nc.tensor.matmul(dst[:, c * BANK:(c + 1) * BANK], sel[0:96, r:r + 1].to_broadcast([96, P]),
                                                  bc[q][:, c * BANK:(c + 1) * BANK], start=True, stop=True)
                        mm.then_inc(done, 1)

                    def both(free):
                        pe.wait_ge(free[0], 1).then_inc(free[0], -1)
                        pe.wait_ge(free[1], 1).then_inc(free[1], -1)

                    def half(weights, rhs, o):
                        for c in range(2):
                            if o:
                                pe.wait_ge(p_free[c], 1).then_inc(p_free[c], -1)
                            for k, r in enumerate(rhs):
                                mm = nc.tensor.matmul(p_bank[c], weights(k, o), r[:, col[c]], start=k == 0, stop=k == len(rhs) - 1)
                            mm.then_inc(p_blocks, 1)

                    def prepare(step, q):
                        for piece in PREPARE.get(step, ()):
                            o = int(piece[-1]) if piece[-1] in "01" else 0
                            if piece == "turn":
                                pe.wait_ge(p_x, 16).then_inc(p_x, -16)
                                both(p_free)
                                for c in range(2):
                                    for t in range(FT):
                                        mm = nc.tensor.transpose(p_bank[c][:, t * P:(t + 1) * P], x_st[:, c * FT + t, :], ident)
                                    mm.then_inc(p_blocks, 1)
                            elif piece in ("in0", "in1"):
                                if o == 0:
                                    both(p_free)
                                half(lambda k, o: m["in"][:, o * P:(o + 1) * P], [xT], o)
                            elif piece in ("z0", "z1"):
                                if o == 0:
                                    both(p_free)
                                half(lambda k, o: m["in"][:, (2 + o) * P:(3 + o) * P], [xT], o)
                            elif piece in ("xp0", "xp1"):
                                if o == 0:
                                    pe.wait_ge(p_u, 2).then_inc(p_u, -2)
                                    both(p_free)
                                half(lambda k, o: w_xp[:, k, o * P:(o + 1) * P], [uu[:, 0, :], uu[:, 1, :]], o)
                            elif piece in ("dt0", "dt1"):
                                if o == 0:
                                    both(p_free)
                                half(lambda k, o: w_dt[:, k, o * P:(o + 1) * P], [low[:, 0, :], low[:, 1, :]], o)
                            elif piece == "bc":
                                both(p_free)
                                for c in range(2):
                                    for k in range(2):
                                        mm = nc.tensor.matmul(p_bank[c][0:96, :], w_xp[:, k, DI:DI + 96], uu[:, k, col[c]],
                                                              start=k == 0, stop=k == 1)
                                    mm.then_inc(p_blocks, 1)

                    def mlp_step(pieces, p):
                        for piece in pieces:
                            if piece == "out":
                                pe.wait_ge(o_gy, 1).then_inc(o_gy, -1)
                                both(p_free)
                                for c in range(2):
                                    for t in range(FT):
                                        at = slice((c * FT + t) * P, (c * FT + t + 1) * P)
                                        for k in range(2):
                                            mm = nc.tensor.matmul(p_bank[c][:, t * P:(t + 1) * P], gate[1 - p][:, k, at], w_out[:, k, :],
                                                                  start=k == 0, stop=k == 1)
                                    mm.then_inc(p_sums, 1)
                            elif piece in ("turn0", "turn1"):
                                c = int(piece[-1])
                                if c == 0:
                                    pe.wait_ge(o_x, 1).then_inc(o_x, -1)
                                pe.wait_ge(f_free[0], 1).then_inc(f_free[0], -1)
                                for t in range(FT):
                                    mm = nc.tensor.transpose(f_bank[0][:, t * P:(t + 1) * P], xf[1 - p][:, c * FT + t, :], ident)
                                mm.then_inc(f_blocks, 1)
                            elif piece == "w1":
                                for k in range(MB):
                                    if k != 1:
                                        pe.wait_ge(f_free[k % 2], 1).then_inc(f_free[k % 2], -1)
                                    nc.tensor.matmul(f_bank[k % 2], f["w1"][:, k * P:(k + 1) * P], fT[:], start=True, stop=True).then_inc(f_blocks, 1)
                            elif piece in ("w2a", "w2b"):
                                for k in range(2) if piece == "w2a" else range(2, MB):
                                    pe.wait_ge(f_free[k % 2], 1).then_inc(f_free[k % 2], -1)
                                    nc.tensor.matmul(f_bank[k % 2], f["w2"][:, k * P:(k + 1) * P], fT[:], start=True, stop=True).then_inc(f_sums, 1)
                            elif piece[0] == "h":
                                layer, o = piece[0:2], int(piece[3])
                                src = hb if layer == "h1" else ha
                                if o == 0:
                                    both(f_free)
                                elif o > 1:
                                    pe.wait_ge(f_free[o % 2], 1).then_inc(f_free[o % 2], -1)
                                for k in range(MB):
                                    mm = nc.tensor.matmul(f_bank[o % 2], f[layer][:, k * HID + o * P:k * HID + (o + 1) * P], src[:, k, :],
                                                          start=k == 0, stop=k == MB - 1)
                                mm.then_inc(f_blocks, 1)
                            elif piece in ("w3.0", "w3.1"):
                                both(f_free)
                                for t in range(FT):
                                    for k in range(MB):
                                        mm = nc.tensor.matmul(f_bank[0][:, t * P:(t + 1) * P], hb[:, k, t * P:(t + 1) * P], w3[:, k, :],
                                                              start=k == 0, stop=k == MB - 1)
                                mm.then_inc(f_sums, 1)

                    def prologue():
                        pe.wait_ge(m_wm, 16)
                        pe.wait_ge(m_const, 1)
                        for step in range(NS):
                            prepare(step, 0)
                        pe.wait_ge(p_parts, 1).then_inc(p_parts, -1)
                        row_to_all(0, 0, Bp, s_B)
                        row_to_all(NS, 0, Cp, s_C)
                        pe.wait_ge(m_wf, 16)
                        pe.wait_ge(m_rate, 1)

                    def body(b, p, prep, mlp, late):
                        for n in range(NS):
                            pe.wait_ge(s_Bfree, 1).then_inc(s_Bfree, -1)
                            if n < NS - 1:
                                row_to_all(n + 1, p, Bp, s_B)
                            elif prep:
                                pe.wait_ge(p_parts, 1).then_inc(p_parts, -1)
                                row_to_all(0, 1 - p, Bp, s_B)
                            pe.wait_ge(s_Cfree, 1).then_inc(s_Cfree, -1)
                            if n < NS - 1:
                                row_to_all(n + 1 + NS, p, Cp, s_C)
                            elif prep:
                                row_to_all(NS, 1 - p, Cp, s_C)
                            if n in MLP_FIRST:
                                mlp_step(beside(n, mlp, late), p)
                            if prep:
                                prepare(n, 1 - p)
                            if n not in MLP_FIRST:
                                mlp_step(beside(n, mlp, late), p)

                    def tail():
                        for n in range(NS):
                            mlp_step(beside(n, True, True), 0)
                        for n in LATE:
                            mlp_step(LATE[n], 1)

                    bodies(pe, prologue, body, tail)


def _packed(i):
    T = np.transpose
    col = lambda a: np.reshape(a, (-1, P)).T
    rows = lambda a: np.broadcast_to(np.reshape(a, (1, -1)), (P, np.size(a)))
    halves = lambda m: np.concatenate([m[k:k + P] for k in range(0, m.shape[0], P)], 1)
    qkv = i["L0_ffn_qkv_weight"]
    spread = lambda m: np.repeat(m.reshape(4, 1, HD, D), 4, 1).reshape(P, D)
    wa = np.concatenate([T(i["L0_attn_W_q"]), T(i["L0_attn_W_k"]), T(i["L0_attn_W_v"]), T(i["L0_attn_W_o"]),
                         T(qkv[0:128]), T(spread(qkv[128:160])), T(spread(qkv[160:192])), T(i["L0_ffn_proj_weight"]),
                         T(i["L0_ffn_router_weight"]), col(i["L0_attn_b_q"]), col(i["L0_ffn_ln1_weight"]),
                         col(i["L0_ffn_ln1_bias"]), col(i["L0_ffn_ln2_weight"]), col(i["L0_ffn_ln2_bias"]),
                         rows(i["L0_attn_b_k"]), rows(i["L0_attn_b_v"]), rows(i["L0_attn_b_o"])], 1)
    w1, w2 = i["L0_ffn_moe_w1"], i["L0_ffn_moe_w2"]
    moe = np.concatenate([T(w1, (0, 2, 1)), T(w2[:, :, 0:P], (0, 2, 1)), T(w2[:, :, P:], (0, 2, 1))], 2)
    xp = T(i["L1_attn_x_proj_w"])
    xp = np.concatenate([xp[:, 0:DI]] + [xp[:, DI:]] * 3, 1)
    wm = np.concatenate([T(i["L1_attn_in_proj_w"]), halves(xp), halves(T(i["L1_attn_dt_proj_w"])),
                         halves(T(i["L1_attn_out_proj_w"])), halves(np.reshape(i["L1_attn_conv_w"], (DI, TAPS))),
                         col(i["L1_attn_conv_b"]), col(i["L1_attn_dt_proj_b"]), halves(i["L1_attn_A_log"]),
                         col(i["L1_attn_D_param"])], 1)
    wf = np.concatenate([T(i["L1_ffn_w1_w"]), T(i["L1_ffn_w2_w"]), halves(T(i["L1_ffn_h1_w"])),
                         halves(T(i["L1_ffn_h2_w"])), halves(T(i["L1_ffn_w3_w"])), col(i["L1_ffn_w1_s"]),
                         col(i["L1_ffn_w2_s"]), col(i["L1_ffn_h1_s"]), col(i["L1_ffn_h2_s"]), rows(i["L1_ffn_w3_s"])], 1)
    return wa, moe, wm, wf


def _constants():
    p = np.arange(P)
    block = (p[:, None] // HD == p[None, :] // HD)
    head = (p[:, None] // HD == np.arange(HEADS)[None, :])
    before = p[:, None] < p[None, :]
    decay = np.exp(-(np.arange(POS, dtype=np.float32) / np.float32(POS))).reshape(GT, P).T
    part = p[:, None] % 32 == np.arange(32)[None, :]
    const = np.concatenate([np.eye(P), block, head, before, np.broadcast_to(np.arange(EXP), (P, EXP)), decay, part],
                           1).astype(np.float32)
    return const


def kernel(**inputs):
    import concourse.bacc as bacc
    from concourse.bass_utils import run_bass_kernel_spmd

    i = {n: np.asarray(a) for n, a in inputs.items()}
    wa, moe, wm, wf = _packed(i)
    const = _constants()
    arrays = {"x": i["L0_attn_x"].reshape(TOK, D), "const": const, "wa": wa, "moe": moe, "wm": wm, "wf": wf}
    arrays = {n: np.ascontiguousarray(a) for n, a in arrays.items()}
    nc = bacc.Bacc("TRN2", target_bir_lowering=False, num_devices=1)
    aps = [nc.dram_tensor(n + "_dram", a.shape, mybir.dt.from_np(a.dtype), kind="ExternalInput").ap() for n, a in arrays.items()]
    y = nc.dram_tensor("y_dram", (TOK, D), F32, kind="ExternalOutput").ap()
    program(nc, *aps, y)
    r = run_bass_kernel_spmd(nc, [{n + "_dram": a for n, a in arrays.items()}], core_ids=[0])
    return r.results[0]["y_dram"].reshape(SEQ, POS, D)
```
